# Optimizing a Trainium2 kernel written in Bass

```python
import numpy as np
import jax
import jax.numpy as jnp

def _softmax(x, axis=-1):
    return jax.nn.softmax(x, axis=axis)

def _gelu(x):
    return jax.nn.gelu(x, approximate=True)

def _silu(x):
    return jax.nn.silu(x)

def _sigmoid(x):
    return jax.nn.sigmoid(x)

def _layernorm(x, axis=-1, eps=1e-05):
    m = jnp.mean(x, axis=axis, keepdims=True)
    v = jnp.var(x, axis=axis, keepdims=True)
    return (x - m) / jnp.sqrt(v + eps)

def _scatter_add(tgt, idx, src, axis=0):
    return tgt.at[idx].add(src)

def _segment_sum(src, seg, n):
    return jax.ops.segment_sum(src, seg, n)
kernel_name = 'mk_vit_tower_d1_tok_img1024_r4_a1b711'

def setup_inputs(seed: int=0):
    np.random.seed(seed)
    _w = jnp.asarray

    def _rec_inputs():
        import jax
        import jax.numpy as jnp
        _rk = jax.random.key(seed)
        x = -0.000125008 + 0.999885 * jax.random.normal(jax.random.fold_in(_rk, 1), (16, 512, 256, 4), jnp.float32)
        return x
    x = _rec_inputs()

    def _L0_tok_setup():
        import jax, jax.numpy as jnp
        import numpy as np
        key = jax.random.key(seed)
        k1, k2, k3 = jax.random.split(key, 3)
        B, H, I, O, Dp1 = (4, 512, 256, 256, 4)
        x = jax.random.normal(k1, (B, H, I, Dp1), dtype=jnp.float32)
        weight = 0.1 * jax.random.normal(k2, (O, Dp1), dtype=jnp.float32)
        weighted_sum = 0.1 * jax.random.normal(k3, (O, I), dtype=jnp.float32)
        return {'x': x, 'weight': weight, 'weighted_sum': weighted_sum}
    _L0_tok_all = _L0_tok_setup()
    _L0_tok_in = {k: v for k, v in _L0_tok_all.items() if k in ('weight', 'weighted_sum')}
    del _L0_tok_all

    def _L0_attn_setup():
        import jax, jax.numpy as jnp
        import numpy as np
        B, S, D, H, DH, FF = (2, 1024, 256, 16, 64, 1024)

        def _ln(x, g, b):
            m = x.mean(-1, keepdims=True)
            v = ((x - m) ** 2).mean(-1, keepdims=True)
            return (x - m) * jax.lax.rsqrt(v + 1e-05) * g + b

        def _phi(x, proj):
            return jax.nn.elu(x @ proj) + 1.0
        key = jax.random.key(seed)
        ks = jax.random.split(key, 10)
        s = 0.02
        return {'x': jax.random.normal(ks[0], (B, S, D), jnp.float32), 'wq': jax.random.normal(ks[1], (D, H * DH), jnp.float32) * s, 'wk': jax.random.normal(ks[2], (D, H * DH), jnp.float32) * s, 'wv': jax.random.normal(ks[3], (D, H * DH), jnp.float32) * s, 'wo': jax.random.normal(ks[4], (H * DH, D), jnp.float32) * s, 'proj': jax.random.normal(ks[5], (DH, DH), jnp.float32) / np.sqrt(DH).astype(np.float32), 'w1': jax.random.normal(ks[6], (D, FF), jnp.float32) * s, 'b1': jnp.zeros((FF,), jnp.float32), 'w2': jax.random.normal(ks[7], (FF, D), jnp.float32) * s, 'b2': jnp.zeros((D,), jnp.float32), 'g1': jnp.ones((D,), jnp.float32), 'beta1': jnp.zeros((D,), jnp.float32), 'g2': jnp.ones((D,), jnp.float32), 'beta2': jnp.zeros((D,), jnp.float32)}
    _L0_attn_all = _L0_attn_setup()
    _L0_attn_in = {k: v for k, v in _L0_attn_all.items() if k in ('wq', 'wk', 'wv', 'wo', 'proj', 'w1', 'b1', 'w2', 'b2', 'g1', 'beta1', 'g2', 'beta2')}
    del _L0_attn_all

    def _L0_ffn_setup():
        import jax, jax.numpy as jnp
        import numpy as np
        B, S, H = (2, 512, 256)
        E_DYN, E_FIX = (8, 1)
        I_DYN, I_FIX = (128, 512)
        TOP_K = 4
        TOP_P = 0.75
        JITTER_EPS = 0.1
        CAPACITY_FACTOR = 1.25
        MIN_CAPACITY = 4

        def _sparse_mixer(scores):
            T = scores.shape[0]
            rows = jnp.arange(T)
            masked_scores = scores
            mults, sels = ([], [])
            for _ in range(TOP_K):
                thr = jnp.max(masked_scores, axis=-1, keepdims=True)
                sel = jnp.argmax(masked_scores, axis=-1)
                factor = jnp.maximum(jnp.abs(scores), jnp.abs(thr))
                jmask = (thr - scores) / factor > 2.0 * JITTER_EPS
                gates = jax.nn.softmax(jnp.where(jmask, -jnp.inf, masked_scores), axis=-1)
                mult = jnp.take_along_axis(gates, sel[:, None], axis=-1)[:, 0]
                masked_scores = masked_scores.at[rows, sel].set(-jnp.inf)
                mults.append(mult)
                sels.append(sel)
            return (jnp.stack(mults, axis=-1), jnp.stack(sels, axis=-1))
        key = jax.random.key(seed)
        k = jax.random.split(key, 8)
        sc = 0.02
        return {'hidden_states': jax.random.normal(k[0], (B, S, H), jnp.float32), 'gate_w': jax.random.normal(k[1], (E_DYN + E_FIX, H), jnp.float32) * sc, 'dyn_gate_w': jax.random.normal(k[2], (E_DYN, I_DYN, H), jnp.float32) * sc, 'dyn_up_w': jax.random.normal(k[3], (E_DYN, I_DYN, H), jnp.float32) * sc, 'dyn_down_w': jax.random.normal(k[4], (E_DYN, H, I_DYN), jnp.float32) * sc, 'sh_gate_w': jax.random.normal(k[5], (E_FIX, I_FIX, H), jnp.float32) * sc, 'sh_up_w': jax.random.normal(k[6], (E_FIX, I_FIX, H), jnp.float32) * sc, 'sh_down_w': jax.random.normal(k[7], (E_FIX, H, I_FIX), jnp.float32) * sc}
    _L0_ffn_all = _L0_ffn_setup()
    _L0_ffn_in = {k: v for k, v in _L0_ffn_all.items() if k in ('gate_w', 'dyn_gate_w', 'dyn_up_w', 'dyn_down_w', 'sh_gate_w', 'sh_up_w', 'sh_down_w')}
    del _L0_ffn_all
    return {'x': x, 'L0_tok_weight': _L0_tok_in['weight'], 'L0_tok_weighted_sum': _L0_tok_in['weighted_sum'], 'L0_attn_wq': _L0_attn_in['wq'], 'L0_attn_wk': _L0_attn_in['wk'], 'L0_attn_wv': _L0_attn_in['wv'], 'L0_attn_wo': _L0_attn_in['wo'], 'L0_attn_proj': _L0_attn_in['proj'], 'L0_attn_w1': _L0_attn_in['w1'], 'L0_attn_b1': _L0_attn_in['b1'], 'L0_attn_w2': _L0_attn_in['w2'], 'L0_attn_b2': _L0_attn_in['b2'], 'L0_attn_g1': _L0_attn_in['g1'], 'L0_attn_beta1': _L0_attn_in['beta1'], 'L0_attn_g2': _L0_attn_in['g2'], 'L0_attn_beta2': _L0_attn_in['beta2'], 'L0_ffn_gate_w': _L0_ffn_in['gate_w'], 'L0_ffn_dyn_gate_w': _L0_ffn_in['dyn_gate_w'], 'L0_ffn_dyn_up_w': _L0_ffn_in['dyn_up_w'], 'L0_ffn_dyn_down_w': _L0_ffn_in['dyn_down_w'], 'L0_ffn_sh_gate_w': _L0_ffn_in['sh_gate_w'], 'L0_ffn_sh_up_w': _L0_ffn_in['sh_up_w'], 'L0_ffn_sh_down_w': _L0_ffn_in['sh_down_w']}

def reference(x, L0_tok_weight, L0_tok_weighted_sum, L0_attn_wq, L0_attn_wk, L0_attn_wv, L0_attn_wo, L0_attn_proj, L0_attn_w1, L0_attn_b1, L0_attn_w2, L0_attn_b2, L0_attn_g1, L0_attn_beta1, L0_attn_g2, L0_attn_beta2, L0_ffn_gate_w, L0_ffn_dyn_gate_w, L0_ffn_dyn_up_w, L0_ffn_dyn_down_w, L0_ffn_sh_gate_w, L0_ffn_sh_up_w, L0_ffn_sh_down_w):
    import jax
    import jax.numpy as jnp

    def _L0_tok_ref(x, weight, weighted_sum):
        import jax, jax.numpy as jnp
        import numpy as np
        return jnp.einsum('bhid,oi,od->bho', x, weighted_sum, weight)

    def _L0_attn_ref(x, wq, wk, wv, wo, proj, w1, b1, w2, b2, g1, beta1, g2, beta2):
        import jax, jax.numpy as jnp
        import numpy as np
        B, S, D, H, DH, FF = (2, 1024, 256, 16, 64, 1024)

        def _ln(x, g, b):
            m = x.mean(-1, keepdims=True)
            v = ((x - m) ** 2).mean(-1, keepdims=True)
            return (x - m) * jax.lax.rsqrt(v + 1e-05) * g + b

        def _phi(x, proj):
            return jax.nn.elu(x @ proj) + 1.0
        b, s, d = x.shape
        h = _ln(x, g1, beta1)
        q = _phi((h @ wq).reshape(b, s, H, DH), proj)
        k = _phi((h @ wk).reshape(b, s, H, DH), proj)
        v = (h @ wv).reshape(b, s, H, DH)
        qs = jnp.moveaxis(q, 1, 0)
        ks_ = jnp.moveaxis(k, 1, 0)
        vs = jnp.moveaxis(v, 1, 0)

        def step(carry, qkv_t):
            kv, ksum = carry
            q_t, k_t, v_t = qkv_t
            kv = kv + k_t[..., :, None] * v_t[..., None, :]
            ksum = ksum + k_t
            num = jnp.einsum('bhd,bhde->bhe', q_t, kv)
            den = jnp.einsum('bhd,bhd->bh', q_t, ksum) + 1e-06
            return ((kv, ksum), num / den[..., None])
        kv0 = jnp.zeros((b, H, DH, DH), x.dtype)
        ks0 = jnp.zeros((b, H, DH), x.dtype)
        _, outs = jax.lax.scan(step, (kv0, ks0), (qs, ks_, vs))
        attn = jnp.moveaxis(outs, 0, 1).reshape(b, s, H * DH) @ wo
        x = x + attn
        h2 = _ln(x, g2, beta2)
        x = x + (jax.nn.gelu(h2 @ w1 + b1, approximate=False) @ w2 + b2)
        return x

    def _L0_ffn_ref(hidden_states, gate_w, dyn_gate_w, dyn_up_w, dyn_down_w, sh_gate_w, sh_up_w, sh_down_w):
        import jax, jax.numpy as jnp
        import numpy as np
        B, S, H = (2, 512, 256)
        E_DYN, E_FIX = (8, 1)
        I_DYN, I_FIX = (128, 512)
        TOP_K = 4
        TOP_P = 0.75
        JITTER_EPS = 0.1
        CAPACITY_FACTOR = 1.25
        MIN_CAPACITY = 4

        def _sparse_mixer(scores):
            T = scores.shape[0]
            rows = jnp.arange(T)
            masked_scores = scores
            mults, sels = ([], [])
            for _ in range(TOP_K):
                thr = jnp.max(masked_scores, axis=-1, keepdims=True)
                sel = jnp.argmax(masked_scores, axis=-1)
                factor = jnp.maximum(jnp.abs(scores), jnp.abs(thr))
                jmask = (thr - scores) / factor > 2.0 * JITTER_EPS
                gates = jax.nn.softmax(jnp.where(jmask, -jnp.inf, masked_scores), axis=-1)
                mult = jnp.take_along_axis(gates, sel[:, None], axis=-1)[:, 0]
                masked_scores = masked_scores.at[rows, sel].set(-jnp.inf)
                mults.append(mult)
                sels.append(sel)
            return (jnp.stack(mults, axis=-1), jnp.stack(sels, axis=-1))
        Bv, Sv, Hv = hidden_states.shape
        T = Bv * Sv
        x = hidden_states.reshape(T, Hv)
        full_logits = x @ gate_w.T
        dyn_logits = full_logits[:, :E_DYN]
        probs = jax.nn.softmax(dyn_logits, axis=-1)
        sorted_p = jnp.sort(probs, axis=-1)[:, ::-1]
        csum = jnp.cumsum(sorted_p, axis=-1)
        dyn_k = jnp.minimum(jnp.sum(csum < TOP_P, axis=-1) + 1, TOP_K)
        mult, sel = _sparse_mixer(dyn_logits)
        slot_valid = jnp.arange(TOP_K)[None, :] < dyn_k[:, None]
        mult = jnp.where(slot_valid, mult, 0.0)
        rows = jnp.arange(T)
        rw = jnp.zeros((T, E_DYN), x.dtype).at[rows[:, None], sel].add(mult)
        rw = rw / jnp.sum(rw, axis=-1, keepdims=True)
        mask_dyn = (rw > 0).astype(jnp.int32)
        cap = max(int(np.ceil(T / E_DYN * CAPACITY_FACTOR)), MIN_CAPACITY)
        mask_dyn = mask_dyn * (jnp.cumsum(mask_dyn, axis=0) <= cap)
        expert_mask = jnp.concatenate([mask_dyn, jnp.ones((T, E_FIX), jnp.int32)], axis=-1)
        maskf = expert_mask.astype(x.dtype)
        gw = jax.nn.softmax(jnp.where(expert_mask == 0, -jnp.inf, full_logits), axis=-1)
        gd = rw * jnp.sum(gw[:, :E_DYN], axis=-1, keepdims=True)
        global_w = jnp.concatenate([gd, gw[:, E_DYN:]], axis=-1) * maskf
        g = jnp.einsum('th,eih->tei', x, dyn_gate_w)
        u = jnp.einsum('th,eih->tei', x, dyn_up_w)
        y_dyn = jnp.einsum('tei,ehi->teh', jax.nn.silu(g) * u, dyn_down_w)
        out = jnp.einsum('te,teh->th', global_w[:, :E_DYN], y_dyn)
        gs = jnp.einsum('th,fih->tfi', x, sh_gate_w)
        us = jnp.einsum('th,fih->tfi', x, sh_up_w)
        y_sh = jnp.einsum('tfi,fhi->tfh', jax.nn.silu(gs) * us, sh_down_w)
        out = out + jnp.einsum('tf,tfh->th', global_w[:, E_DYN:], y_sh)
        return out.reshape(Bv, Sv, Hv)
    h = _L0_tok_ref(x, L0_tok_weight, L0_tok_weighted_sum)
    h = h + _L0_attn_ref(_layernorm(h, axis=-1), L0_attn_wq, L0_attn_wk, L0_attn_wv, L0_attn_wo, L0_attn_proj, L0_attn_w1, L0_attn_b1, L0_attn_w2, L0_attn_b2, L0_attn_g1, L0_attn_beta1, L0_attn_g2, L0_attn_beta2)
    h = h + _L0_ffn_ref(_layernorm(h, axis=-1), L0_ffn_gate_w, L0_ffn_dyn_gate_w, L0_ffn_dyn_up_w, L0_ffn_dyn_down_w, L0_ffn_sh_gate_w, L0_ffn_sh_up_w, L0_ffn_sh_down_w)
    return h

_drawn_inputs = setup_inputs


def setup_inputs(seed=0):
    import zlib

    import numpy as np

    out = dict(_drawn_inputs(seed))
    spreads = {'L0_attn_b1': (0.0, 0.301),
     'L0_attn_b2': (0.0, 0.1),
     'L0_attn_g1': (1.0, 0.6),
     'L0_attn_beta1': (0.0, 0.627),
     'L0_attn_g2': (1.0, 0.6),
     'L0_attn_beta2': (0.0, 0.8)}
    factors = {'L0_attn_wq': 8.0,
     'L0_attn_wk': 8.0,
     'L0_attn_proj': 8.0,
     'L0_ffn_gate_w': 8.0,
     'L0_ffn_dyn_gate_w': 8.0,
     'L0_ffn_dyn_up_w': 8.0,
     'L0_ffn_dyn_down_w': 8.0,
     'L0_ffn_sh_gate_w': 3.915,
     'L0_ffn_sh_up_w': 3.854,
     'L0_ffn_sh_down_w': 3.865}
    for name, (base, spread) in spreads.items():
        noise = np.random.default_rng([zlib.crc32(name.encode()), seed]).standard_normal(out[name].shape)
        drawn = base * np.exp(spread * noise) if base else spread * noise
        out[name] = jnp.asarray(drawn.astype(out[name].dtype))
    for name, factor in factors.items():
        out[name] = (out[name] * factor).astype(out[name].dtype)
    return out
```

```python
import math
from contextlib import ExitStack

import concourse.bass as bass
from concourse import mybir

F32 = mybir.dt.float32
F16 = mybir.dt.float16
U32 = mybir.dt.uint32
ALU = mybir.AluOpType
ACT = mybir.ActivationFunctionType
AX = mybir.AxisListType

P = 128
T = 512
SEQS = 16
D = 256
DT = D // P
XK = 8
HEADS = 16
DH = 64
QT = HEADS * DH // P
VW = DH + 1
CH = 4
EPS = 1e-5
DEN_EPS = 1e-6
XS = 4

TOK_SCALE = 256.0
V_SCALE = 64.0
WO_SCALE = 64.0
PHI_DOWN = 16.0
QK_SCALE = 1 / PHI_DOWN


def count(i, per, k):
    return i * per + k


def causal_mask(nc, gp, mask, made, n):
    gp.memset(mask, 1.0).then_inc(made, 1)
    gp.wait_ge(made, n + 1)
    gp.affine_select(out=mask, in_=mask, compare_op=ALU.is_ge, fill=0.0, base=0,
                     pattern=[[1, P]], channel_multiplier=-1).then_inc(made, 1)


def identity(nc, gp, ident, made, n):
    gp.memset(ident, 0.0).then_inc(made, 1)
    gp.wait_ge(made, n + 1)
    gp.affine_select(out=ident, in_=ident, compare_op=ALU.not_equal, fill=1.0, base=0,
                     pattern=[[-1, P]], channel_multiplier=1).then_inc(made, 1)


def attention_phase(nc, io):
    with ExitStack() as ctx:
        def sb(name, shape, dt=F32):
            return ctx.enter_context(nc.sbuf_tensor(name, [P, *shape], dt))

        def sem(name):
            return ctx.enter_context(nc.semaphore(name))

        tok_h, tok_l = sb("tok_h", [XK, D], F16), sb("tok_l", [XK, D], F16)
        qk_h, qk_l = sb("qk_h", [DT, 2 * QT * P], F16), sb("qk_l", [DT, 2 * QT * P], F16)
        wv_h, wv_l = sb("wv_h", [DT, HEADS * DH], F16), sb("wv_l", [DT, HEADS * DH], F16)
        wo_h, wo_l = sb("wo_h", [QT, D], F16), sb("wo_l", [QT, D], F16)
        ones = sb("ones", [P])
        ident = sb("ident", [P], F16)
        mask = sb("mask", [P])
        block_mask = sb("block_mask", [2, 2, VW])
        g1 = sb("g1", [DT])
        b1 = sb("b1", [DT])

        with ExitStack() as pre:
            def tmp(name, shape, dt=F32):
                return pre.enter_context(nc.sbuf_tensor(name, [P, *shape], dt))

            ws = tmp("ws", [DT, D])
            wd = tmp("wd", [4, D])
            tok_w = tmp("tok_w", [2, D])
            wqkT = tmp("wqkT", [2 * QT, D])
            proj2 = tmp("proj2", [P])
            qk_w = tmp("qk_w", [2, P])
            wv_w = tmp("wv_w", [DT, HEADS * DH])
            wo_w = tmp("wo_w", [QT, D])
            ps = [pre.enter_context(nc.psum_tensor(f"pre_ps{i}", [P, 512], F32)) for i in range(2)]
            loaded = pre.enter_context(nc.semaphore("w_loaded"))
            made = pre.enter_context(nc.semaphore("const_made"))
            zeroed = pre.enter_context(nc.semaphore("proj_zeroed"))
            tok_mul = pre.enter_context(nc.semaphore("tok_mul"))
            tok_hi = pre.enter_context(nc.semaphore("tok_hi"))
            tok_lo = pre.enter_context(nc.semaphore("tok_lo"))
            qk_mm = pre.enter_context(nc.semaphore("qk_mm"))
            qk_hi = pre.enter_context(nc.semaphore("qk_hi"))
            qk_lo = pre.enter_context(nc.semaphore("qk_lo"))
            vo_hi = pre.enter_context(nc.semaphore("vo_hi"))
            proj_loaded = pre.enter_context(nc.semaphore("proj_loaded"))
            with nc.Block() as block:
                @block.sync
                def _(sp):
                    sp.dma_start(ws[:, :, :], io["wsT"].rearrange("(t p) o -> p t o", p=P)).then_inc(loaded, 16)
                    sp.dma_start(wd[:, :, :].rearrange("p d o -> p (d o)"), io["wT"].rearrange("d o -> (d o)").partition_broadcast(P)).then_inc(loaded, 16)
                    sp.dma_start(wv_w[:, :, :], io["wv"].rearrange("(t p) n -> p t n", p=P)).then_inc(loaded, 16)
                    sp.dma_start(wo_w[:, :, :], io["wo"].rearrange("(t p) n -> p t n", p=P)).then_inc(loaded, 16)
                    sp.dma_start(g1[:, :], io["g1"]).then_inc(loaded, 16)
                    sp.dma_start(b1[:, :], io["beta1"]).then_inc(loaded, 16)
                    sp.wait_ge(zeroed, 1)
                    sp.dma_start(proj2[0:DH, 0:DH], io["proj"]).then_inc(proj_loaded, 16)
                    sp.dma_start(proj2[DH:P, DH:P], io["proj"]).then_inc(proj_loaded, 16)
                    sp.wait_ge(loaded, 96)
                    sp.wait_ge(proj_loaded, 64)

                @block.gpsimd
                def _(gp):
                    gp.memset(ones[:, :], 1.0 / D).then_inc(made, 1)
                    identity(nc, gp, ident[:, :], made, 1)
                    causal_mask(nc, gp, mask[:, :], made, 3)
                    gp.memset(block_mask[:, :, :, :], 0.0).then_inc(made, 1)
                    gp.wait_ge(made, 6)
                    gp.memset(block_mask[0:DH, :, 0, :], 1.0).then_inc(made, 1)
                    gp.memset(block_mask[DH:P, :, 1, :], 1.0).then_inc(made, 1)

                @block.tensor
                def _(pe):
                    pe.wait_ge(proj_loaded, 64)
                    for n in range(2 * QT * DT):
                        t, m = n // DT, n % DT
                        if n >= 2:
                            pe.wait_ge(qk_lo, n - 1)
                        pe.matmul(ps[n % 2][:, 0:P], wqkT[:, t, m * P:(m + 1) * P], proj2[:, :],
                                  start=True, stop=True).then_inc(qk_mm, 1)

                @block.scalar
                def _(act):
                    act.dma_start(wqkT[:, 0:QT, :], io["wqT"].rearrange("(t p) n -> p t n", p=P)).then_inc(proj_loaded, 16)
                    act.dma_start(wqkT[:, QT:2 * QT, :], io["wkT"].rearrange("(t p) n -> p t n", p=P)).then_inc(proj_loaded, 16)
                    for k in range(XK):
                        act.wait_ge(tok_mul, k + 1)
                        nc.scalar.activation(tok_h[:, k, :], tok_w[:, k % 2, :], ACT.Copy).then_inc(tok_hi, 1)
                    act.wait_ge(loaded, 96)
                    nc.scalar.activation(wv_h[:, :, :], wv_w[:, :, :], ACT.Copy, scale=V_SCALE).then_inc(vo_hi, 1)
                    nc.scalar.activation(wo_h[:, :, :], wo_w[:, :, :], ACT.Copy, scale=WO_SCALE).then_inc(vo_hi, 1)
                    for n in range(2 * QT * DT):
                        t, m = n // DT, n % DT
                        act.wait_ge(qk_mm, n + 1)
                        nc.scalar.activation(qk_h[:, m, t * P:(t + 1) * P], ps[n % 2][:, 0:P], ACT.Copy,
                                             scale=QK_SCALE).then_inc(qk_hi, 1)

                @block.vector
                def _(ve):
                    ve.memset(proj2[:, :], 0.0).then_inc(zeroed, 1)
                    ve.wait_ge(loaded, 96)
                    for k in range(XK):
                        d, t = k // DT, k % DT
                        if k >= 2:
                            ve.wait_ge(tok_hi, k - 1)
                            ve.wait_ge(tok_lo, k - 1)
                        nc.vector.scalar_tensor_tensor(tok_w[:, k % 2, :], ws[:, t, :], TOK_SCALE, wd[:, d, :],
                                                       ALU.mult, ALU.mult).then_inc(tok_mul, 1)
                        ve.wait_ge(tok_mul, k + 1)
                        ve.wait_ge(tok_hi, k + 1)
                        nc.vector.tensor_tensor(tok_l[:, k, :], tok_w[:, k % 2, :], tok_h[:, k, :],
                                                ALU.subtract).then_inc(tok_lo, 1)
                    ve.wait_ge(vo_hi, 1)
                    nc.vector.scalar_tensor_tensor(wv_l[:, :, :], wv_w[:, :, :], V_SCALE, wv_h[:, :, :],
                                                   ALU.mult, ALU.subtract)
                    ve.wait_ge(vo_hi, 2)
                    nc.vector.scalar_tensor_tensor(wo_l[:, :, :], wo_w[:, :, :], WO_SCALE, wo_h[:, :, :],
                                                   ALU.mult, ALU.subtract)
                    for n in range(2 * QT * DT):
                        t, m = n // DT, n % DT
                        ve.wait_ge(qk_hi, n + 1)
                        nc.vector.scalar_tensor_tensor(qk_l[:, m, t * P:(t + 1) * P], ps[n % 2][:, 0:P], QK_SCALE,
                                                       qk_h[:, m, t * P:(t + 1) * P], ALU.mult,
                                                       ALU.subtract).then_inc(qk_lo, 1)

        xs = sb("xs", [XS, T])
        xh, xl = sb("xh", [XS, T], F16), sb("xl", [XS, T], F16)
        hT = sb("hT", [DT, T])
        xc = sb("xc", [DT, T])
        sq = sb("sq", [DT, T])
        lnt = sb("lnt", [T])
        r0 = sb("r0", [T])
        r1 = sb("r1", [T])
        x0 = sb("x0", [DT, T])
        tn = sb("tn", [DT, T])
        nh, nl = sb("nh", [DT, T], F16), sb("nl", [DT, T], F16)
        ez, rz, fz = sb("ez", [2, T]), sb("rz", [2, T]), sb("fz", [2, T])
        qkh, qkl = sb("qkh", [2 * QT, T], F16), sb("qkl", [2 * QT, T], F16)
        vh, vl = sb("vh", [CH, HEADS, VW], F16), sb("vl", [CH, HEADS, VW], F16)
        kth, ktl = sb("kth", [QT, P], F16), sb("ktl", [QT, P], F16)
        kvt = sb("kvt", [2, 2, VW])
        kvacc = sb("kvacc", [QT, 2, VW])
        kvh, kvl = sb("kvh", [QT, 2, VW], F16), sb("kvl", [QT, 2, VW], F16)
        sm = sb("sm", [2, 4, P])
        sh, sl = sb("sh", [4, 4, P], F16), sb("sl", [4, 4, P], F16)
        dn, rd = sb("dn", [2, 4]), sb("rd", [2, 4])
        on = sb("on", [2, 4, DH])
        oh, ol = sb("oh", [2, 4 * DH], F16), sb("ol", [2, 4 * DH], F16)
        ot = sb("ot", [2, QT, T], F16)
        at = sb("at", [DT, T])

        def bank(name, dt=F32):
            return ctx.enter_context(nc.psum_tensor(name, [P, 2048 // (4 if dt == F32 else 2)], dt))

        pd = [bank("pd0"), bank("pd1")]
        pS = [bank("pS0"), bank("pS1")]
        pO = [bank("pO0"), bank("pO1")]
        pT = bank("pT", F16)
        pKV = bank("pKV")

        x_loaded = [sem(f"x_loaded{i}") for i in range(XS)]
        xh_ready, xl_ready, tok_done = sem("xh_ready"), sem("xl_ready"), sem("tok_done")
        h_ready, mean_done, xc_ready, sq_ready, var_done = (
            sem("h_ready"), sem("mean_done"), sem("xc_ready"), sem("sq_ready"), sem("var_done"))
        rs_step = sem("rs_step")
        r01_ready, x0_ready, tn_ready, nh_ready, nl_ready = (
            sem("r01_ready"), sem("x0_ready"), sem("tn_ready"), sem("nh_ready"), sem("nl_ready"))
        h_stored, x0_stored = sem("h_stored"), sem("x0_stored")
        qk_done, e_ready, z_read, f_ready, fh_ready, fl_ready = (
            sem("qk_done"), sem("e_ready"), sem("z_read"), sem("f_ready"), sem("fh_ready"), sem("fl_ready"))
        v_done, vh_ready, vl_ready, v_ones = sem("v_done"), sem("vh_ready"), sem("vl_ready"), sem("v_ones")
        kt_done, kth_ready, ktl_ready = sem("kt_done"), sem("kth_ready"), sem("ktl_ready")
        s_done, sm_ready, sh_ready, sl_ready = sem("s_done"), sem("sm_ready"), sem("sh_ready"), sem("sl_ready")
        o_done, dn_ready, rd_ready, on_ready, oh_ready, ol_ready = (
            sem("o_done"), sem("dn_ready"), sem("rd_ready"), sem("on_ready"), sem("oh_ready"), sem("ol_ready"))
        ot_done, ot_ready = sem("ot_done"), sem("ot_ready")
        kv_done, kvt_ready, kva_ready, kvh_ready, kvl_ready = (
            sem("kv_done"), sem("kvt_ready"), sem("kva_ready"), sem("kvh_ready"), sem("kvl_ready"))
        at_done, at_ready, at_stored = sem("at_done"), sem("at_ready"), sem("at_stored")

        NKV = 4 * (CH - 1)

        def quad_heads(q):
            return [8 * (q // 2) + q % 2 + 2 * k for k in range(4)]

        def score_place(h):
            return 2 * (h // 8) + h % 2, (h % 8) // 2

        def run(engine, steps):
            def mix(i):
                steps["mix"](i)
                steps["mean"](i)
                steps["var"](i)

            def both(i, last, first=False):
                steps["scores"](i, 0, (0, 1, 2, 3))
                for c in range(CH):
                    if not last and c == 0:
                        steps["mix"](i + 1)
                    if not last and c == 1:
                        steps["mean"](i + 1)
                    if not last and c == 2:
                        steps["var"](i + 1)
                    if c < CH - 1:
                        steps["keys"](i, c)
                    for g in range(4):
                        steps["outputs"](i, c, g)
                        if c < CH - 1:
                            steps["sums"](i, c, g)
                        if g % 2 == 1 and c < CH - 1:
                            steps["scores"](i, c + 1, (g - 1, g))
                        if g > 0:
                            steps["turn"](i, c, g - 1)
                    steps["turn"](i, c, 3)
                steps["project"](i, last)
                if not last:
                    steps["features"](i + 1, False)
                    steps["values"](i + 1)

            mix(0)
            steps["features"](0, True)
            steps["values"](0)
            both(0, False)
            with engine.Fori(1, SEQS - 1) as i:
                both(i, False)
            both(SEQS - 1, True)

        block = ctx.enter_context(nc.Block())

        @block.sync
        def _(sp):
            def load(i, k):
                s = k % XS
                if k >= XS or not (type(i) is int and i == 0):
                    sp.wait_ge(xh_ready, count(i, XK, k - XS + 1))
                    sp.wait_ge(xl_ready, count(i, XK, k - XS + 1))
                sp.dma_start(xs[:, s, :], io["x"][i, k]).then_inc(x_loaded[s], 16)

            def stores(i):
                sp.wait_ge(h_ready, count(i, DT, DT))
                sp.dma_start(io["h_dram"][i].rearrange("t p n -> p t n"), hT[:, :, :]).then_inc(h_stored, 16)
                sp.wait_ge(x0_ready, count(i, DT, DT))
                sp.dma_start(io["x0_dram"][i].rearrange("t p n -> p t n"), x0[:, :, :]).then_inc(x0_stored, 16)

            def store_attention(i):
                sp.wait_ge(at_ready, count(i, DT, DT))
                sp.dma_start(io["at_dram"][i].rearrange("t p n -> p t n"), at[:, :, :]).then_inc(at_stored, 16)

            for k in range(XK):
                load(0, k)
            for k in range(XS):
                load(1, k)
            stores(0)
            with sp.Fori(1, SEQS - 1) as i:
                for k in range(XS, XK):
                    load(i, k)
                for k in range(XS):
                    load(i + 1, k)
                stores(i)
                store_attention(i - 1)
            for k in range(XS, XK):
                load(SEQS - 1, k)
            stores(SEQS - 1)
            store_attention(SEQS - 2)
            store_attention(SEQS - 1)
            sp.wait_ge(h_stored, 16 * SEQS)
            sp.wait_ge(x0_stored, 16 * SEQS)
            sp.wait_ge(at_stored, 16 * SEQS)

        @block.tensor
        def _(pe):
            def three(out, wh, wl, mh, ml, first, last):
                pe.matmul(out, wh, mh, start=first, stop=False, skip_group_check=True)
                pe.matmul(out, wl, mh, start=False, stop=False, skip_group_check=True)
                return pe.matmul(out, wh, ml, start=False, stop=last, skip_group_check=True)

            def mix(i):
                if not (type(i) is int and i == 0):
                    pe.wait_ge(vl_ready, count(i, 2 * CH, 0))
                for k in range(XK):
                    pe.wait_ge(xh_ready, count(i, XK, k + 1))
                    pe.wait_ge(xl_ready, count(i, XK, k + 1))
                    s = k % XS
                    for m in range(DT):
                        cols = slice(m * P, (m + 1) * P)
                        mm = three(pd[m][:, :], tok_h[:, k, cols], tok_l[:, k, cols], xh[:, s, :], xl[:, s, :],
                                   k == 0, k == XK - 1)
                    mm.then_inc(tok_done, 1)

            def mean(i):
                pe.wait_ge(h_ready, count(i, DT, DT))
                for t in range(DT):
                    mm = pe.matmul(pd[0][:, :], ones[:, :], hT[:, t, :], start=(t == 0), stop=(t == DT - 1))
                mm.then_inc(mean_done, 1)

            def var(i):
                pe.wait_ge(sq_ready, count(i, DT, DT))
                for t in range(DT):
                    mm = pe.matmul(pd[1][:, :], ones[:, :], sq[:, t, :], start=(t == 0), stop=(t == DT - 1))
                mm.then_inc(var_done, 1)

            def features(i, first):
                pe.wait_ge(nh_ready, count(i, DT, DT))
                pe.wait_ge(nl_ready, count(i, DT, DT))
                for j in range(2 * QT):
                    if j >= 2:
                        pe.wait_ge(f_ready, count(i, 2 * QT, j - 1))
                    elif not first:
                        pe.wait_ge(at_ready, count(i, DT, j + 1 - DT))
                    for t in range(DT):
                        cols = slice(j * P, (j + 1) * P)
                        mm = three(pd[j % 2][:, :], qk_h[:, t, cols], qk_l[:, t, cols], nh[:, t, :], nl[:, t, :],
                                   t == 0, t == DT - 1)
                    mm.then_inc(qk_done, 1)

            def values(i):
                for n in range(2 * CH):
                    c, half = n // 2, n % 2
                    if n < 2:
                        pe.wait_ge(f_ready, count(i, 2 * QT, 2 * QT - 1 + n))
                    else:
                        pe.wait_ge(vl_ready, count(i, 2 * CH, n - 1))
                    toks, cols = slice(c * P, (c + 1) * P), slice(half * T, (half + 1) * T)
                    for t in range(DT):
                        mm = three(pd[n % 2][:, :], nh[:, t, toks], nl[:, t, toks], wv_h[:, t, cols], wv_l[:, t, cols],
                                   t == 0, t == DT - 1)
                    mm.then_inc(v_done, 1)

            def scores(i, c, quads):
                toks = slice(c * P, (c + 1) * P)
                if c == 0 and 0 in quads:
                    pe.wait_ge(fh_ready, count(i, 2 * QT, 2 * QT))
                    pe.wait_ge(fl_ready, count(i, 2 * QT, 2 * QT))
                for q in quads:
                    n = 4 * c + q
                    if n >= 2:
                        pe.wait_ge(sm_ready, count(i, 16, n - 1))
                    elif not (type(i) is int and i == 0):
                        pe.wait_ge(sm_ready, count(i, 16, n - 1))
                    for k, h in enumerate(quad_heads(q)):
                        rows = slice(DH * (h % 2), DH * (h % 2) + DH)
                        key, qry = QT + h // 2, h // 2
                        mm = three(pS[n % 2][:, k * P:(k + 1) * P], qkh[rows, key, toks], qkl[rows, key, toks],
                                   qkh[rows, qry, toks], qkl[rows, qry, toks], k == 0, True)
                    mm.then_inc(s_done, 1)

            def keys(i, c):
                toks = slice(c * P, (c + 1) * P)
                for part, src in enumerate((qkh, qkl)):
                    if part == 1:
                        pe.wait_ge(kth_ready, count(i, CH - 1, c + 1))
                    elif c > 0 or not (type(i) is int and i == 0):
                        pe.wait_ge(ot_ready, count(i, 16, 4 * c))
                    for p in range(QT):
                        mm = pe.transpose(pT[:, p * P:(p + 1) * P], src[:, QT + p, toks], ident[:, :])
                    mm.then_inc(kt_done, 1)

            def outputs(i, c, g):
                n = 4 * c + g
                toks = slice(c * P, (c + 1) * P)
                out = pO[g % 2]
                if n >= 2 or not (type(i) is int and i == 0):
                    pe.wait_ge(on_ready, count(i, 16, n - 1))
                first = True
                if c > 0:
                    pe.wait_ge(kvh_ready, count(i, NKV, 4 * (c - 1) + g + 1))
                    pe.wait_ge(kvl_ready, count(i, NKV, 4 * (c - 1) + g + 1))
                    for k in range(2):
                        p = 2 * g + k
                        mm = three(out[:, 2 * VW * k:2 * VW * (k + 1)], qkh[:, p, toks], qkl[:, p, toks],
                                   kvh[:, p, :, :], kvl[:, p, :, :], first, True)
                        first = False
                if g % 2 == 0:
                    pe.wait_ge(sh_ready, count(i, 16, 4 * c + g + 2))
                    pe.wait_ge(sl_ready, count(i, 16, 4 * c + g + 2))
                if n == 0:
                    pe.wait_ge(v_ones, 2)
                    pe.wait_ge(vh_ready, count(i, 2 * CH, 2 * CH))
                    pe.wait_ge(vl_ready, count(i, 2 * CH, 2 * CH))
                for k in range(4):
                    h = 4 * g + k
                    q, w = score_place(h)
                    mm = three(out[:, VW * k:VW * (k + 1)], sh[:, q, w, :], sl[:, q, w, :],
                               vh[:, c, h, :], vl[:, c, h, :], first, True)
                    first = False
                mm.then_inc(o_done, 1)

            def sums(i, c, g):
                u = 4 * c + g
                if g == 0:
                    pe.wait_ge(kth_ready, count(i, CH - 1, c + 1))
                    pe.wait_ge(ktl_ready, count(i, CH - 1, c + 1))
                if u >= 1 or not (type(i) is int and i == 0):
                    pe.wait_ge(kvt_ready, count(i, NKV, u))
                for k in range(2):
                    p = 2 * g + k
                    mm = three(pKV[:, 2 * VW * k:2 * VW * (k + 1)], kth[:, p, :], ktl[:, p, :],
                               vh[:, c, 2 * p:2 * p + 2, :], vl[:, c, 2 * p:2 * p + 2, :], k == 0, True)
                mm.then_inc(kv_done, 1)

            def turn(i, c, g):
                n = 4 * c + g
                if g == 0 and c < CH - 1:
                    pe.wait_ge(ktl_ready, count(i, CH - 1, c + 1))
                elif n >= 1:
                    pe.wait_ge(ot_ready, count(i, 16, n))
                pe.wait_ge(oh_ready, count(i, 16, n + 1))
                pe.wait_ge(ol_ready, count(i, 16, n + 1))
                for part, src in enumerate((oh, ol)):
                    for f in range(2):
                        w = 2 * part + f
                        mm = pe.transpose(pT[:, w * P:(w + 1) * P], src[:, n % 2, f * P:(f + 1) * P], ident[:, :])
                mm.then_inc(ot_done, 1)

            def project(i, last):
                pe.wait_ge(ot_ready, count(i, 16, 16))
                for m in range(DT):
                    if last:
                        pe.wait_ge(vl_ready, count(i, 2 * CH, 2 * CH))
                    elif m == 0:
                        pe.wait_ge(xc_ready, count(i + 1, DT, DT))
                    else:
                        pe.wait_ge(rs_step, count(i + 1, 5, 1))
                    cols = slice(m * P, (m + 1) * P)
                    for t in range(QT):
                        mm = three(pd[m][:, :], wo_h[:, t, cols], wo_l[:, t, cols], ot[:, 0, t, :], ot[:, 1, t, :],
                                   t == 0, t == QT - 1)
                    mm.then_inc(at_done, 1)

            run(pe, dict(mix=mix, mean=mean, var=var, features=features, values=values, scores=scores, keys=keys,
                         outputs=outputs, sums=sums, turn=turn, project=project))

        @block.scalar
        def _(act):
            def mix(i):
                for k in range(XK):
                    s = k % XS
                    act.wait_ge(x_loaded[s], count(i, 32, 16 * (k // XS + 1)))
                    if k >= XS or not (type(i) is int and i == 0):
                        act.wait_ge(tok_done, count(i, XK, k - XS + 1))
                    nc.scalar.activation(xh[:, s, :], xs[:, s, :], ACT.Copy).then_inc(xh_ready, 1)
                act.wait_ge(tok_done, count(i, XK, XK))
                if not (type(i) is int and i == 0):
                    act.wait_ge(h_stored, count(i, 16, 0))
                    act.wait_ge(xc_ready, count(i, DT, 0))
                for m in range(DT):
                    nc.scalar.activation(hT[:, m, :], pd[m][:, :], ACT.Copy, scale=1 / TOK_SCALE).then_inc(h_ready, 1)

            def mean(i):
                for m in range(DT):
                    act.wait_ge(xc_ready, count(i, DT, m + 1))
                    nc.scalar.activation(sq[:, m, :], xc[:, m, :], ACT.Square).then_inc(sq_ready, 1)

            def var(i):
                act.wait_ge(var_done, count(i, 1, 1))
                if not (type(i) is int and i == 0):
                    act.wait_ge(tn_ready, count(i, DT, 0))
                nc.scalar.activation(lnt[:, :], pd[1][:, :], ACT.Ln, bias=EPS).then_inc(rs_step, 1)
                act.wait_ge(rs_step, count(i, 5, 1))
                nc.scalar.activation(r0[:, :], lnt[:, :], ACT.Exp, scale=-0.5).then_inc(rs_step, 1)
                act.wait_ge(rs_step, count(i, 5, 2))
                nc.scalar.activation(r1[:, :], r0[:, :], ACT.Square).then_inc(rs_step, 1)
                act.wait_ge(rs_step, count(i, 5, 3))
                nc.scalar.activation(lnt[:, :], r1[:, :], ACT.Ln, scale=-EPS, bias=1.0 + EPS).then_inc(rs_step, 1)
                act.wait_ge(rs_step, count(i, 5, 4))
                nc.scalar.activation(r1[:, :], lnt[:, :], ACT.Exp, scale=-0.5).then_inc(rs_step, 1)
                for m in range(DT):
                    act.wait_ge(tn_ready, count(i, DT, m + 1))
                    if not (type(i) is int and i == 0):
                        act.wait_ge(v_done, count(i, 2 * CH, 0))
                    nc.scalar.activation(nh[:, m, :], tn[:, m, :], ACT.Identity,
                                         bias=b1[:, m:m + 1]).then_inc(nh_ready, 1)

            def features(i, first):
                for j in range(2 * QT):
                    s = j % 2
                    act.wait_ge(qk_done, count(i, 2 * QT, j + 1))
                    if j >= 2 or not (type(i) is int and i == 0):
                        act.wait_ge(e_ready, count(i, 2 * QT, j - 1))
                    nc.scalar.activation(rz[:, s, :], pd[s][:, :], ACT.Relu, scale=-PHI_DOWN).then_inc(z_read, 1)
                    if j >= 1:
                        exponential(i, j - 1)
                exponential(i, 2 * QT - 1)

            def exponential(i, j):
                s = j % 2
                act.wait_ge(z_read, count(i, 2 * QT, j + 1))
                if j >= 2 or not (type(i) is int and i == 0):
                    act.wait_ge(f_ready, count(i, 2 * QT, j - 1))
                nc.scalar.activation(ez[:, s, :], rz[:, s, :], ACT.Exp, scale=-1.0,
                                     bias=-math.log(PHI_DOWN)).then_inc(e_ready, 1)

            def values(i):
                for n in range(2 * CH):
                    c, half = n // 2, n % 2
                    act.wait_ge(v_done, count(i, 2 * CH, n + 1))
                    nc.scalar.activation(vh[:, c, 8 * half:8 * half + 8, 0:DH],
                                         pd[n % 2][:, :].rearrange("p (h e) -> p h e", e=DH), ACT.Copy,
                                         scale=1 / V_SCALE).then_inc(vh_ready, 1)

            def scores(i, c, quads):
                for q in quads:
                    n = 4 * c + q
                    act.wait_ge(sm_ready, count(i, 16, n + 1))
                    if c > 0:
                        act.wait_ge(o_done, count(i, 16, 4 * (c - 1) + (2 if q < 2 else 4)))
                    elif not (type(i) is int and i == 0):
                        act.wait_ge(o_done, count(i, 16, 0))
                    nc.scalar.activation(sh[:, q, :, :], sm[:, n % 2, :, :], ACT.Copy).then_inc(sh_ready, 1)

            def keys(i, c):
                act.wait_ge(kt_done, count(i, 2 * (CH - 1), 2 * c + 1))
                if c > 0 or not (type(i) is int and i == 0):
                    act.wait_ge(kv_done, count(i, NKV, 4 * c))
                nc.scalar.activation(kth[:, :, :], pT[:, :].rearrange("p (a b) -> p a b", b=P),
                                     ACT.Copy).then_inc(kth_ready, 1)

            def outputs(i, c, g):
                n = 4 * c + g
                act.wait_ge(on_ready, count(i, 16, n + 1))
                if n >= 2 or not (type(i) is int and i == 0):
                    act.wait_ge(ot_done, count(i, 16, n - 1))
                nc.scalar.activation(oh[:, n % 2, :], on[:, n % 2, :, :].rearrange("p a b -> p (a b)"),
                                     ACT.Copy).then_inc(oh_ready, 1)

            def sums(i, c, g):
                u = 4 * c + g
                act.wait_ge(kva_ready, count(i, NKV, u + 1))
                act.wait_ge(o_done, count(i, 16, u + 1))
                nc.scalar.activation(kvh[:, 2 * g:2 * g + 2, :, :], kvacc[:, 2 * g:2 * g + 2, :, :],
                                     ACT.Copy).then_inc(kvh_ready, 1)

            def turn(i, c, g):
                n = 4 * c + g
                act.wait_ge(ot_done, count(i, 16, n + 1))
                if not (type(i) is int and i == 0):
                    act.wait_ge(at_done, count(i, DT, 0))
                nc.scalar.activation(ot[:, :, 2 * g:2 * g + 2, c * P:(c + 1) * P],
                                     pT[:, 0:4 * P].rearrange("p (a b n) -> p a b n", a=2, b=2),
                                     ACT.Copy).then_inc(ot_ready, 1)

            def project(i, last):
                for m in range(DT):
                    act.wait_ge(at_done, count(i, DT, m + 1))
                    if not (type(i) is int and i == 0):
                        act.wait_ge(at_stored, count(i, 16, 0))
                    nc.scalar.activation(at[:, m, :], pd[m][:, :], ACT.Copy, scale=1 / WO_SCALE).then_inc(at_ready, 1)

            run(act, dict(mix=mix, mean=mean, var=var, features=features, values=values, scores=scores, keys=keys,
                          outputs=outputs, sums=sums, turn=turn, project=project))

        @block.vector
        def _(ve):
            def mix(i):
                pass

            def mean(i):
                ve.wait_ge(mean_done, count(i, 1, 1))
                if not (type(i) is int and i == 0):
                    ve.wait_ge(tn_ready, count(i, DT, 0))
                for m in range(DT):
                    nc.vector.tensor_tensor(xc[:, m, :], hT[:, m, :], pd[0][:, :], ALU.subtract).then_inc(xc_ready, 1)

            def var(i):
                ve.wait_ge(rs_step, count(i, 5, 2))
                ve.wait_ge(xc_ready, count(i, DT, DT))
                if not (type(i) is int and i == 0):
                    ve.wait_ge(x0_stored, count(i, 16, 0))
                for m in range(DT):
                    nc.vector.tensor_tensor(x0[:, m, :], xc[:, m, :], r0[:, :], ALU.mult).then_inc(x0_ready, 1)
                ve.wait_ge(rs_step, count(i, 5, 5))
                ve.wait_ge(x0_ready, count(i, DT, DT))
                if not (type(i) is int and i == 0):
                    ve.wait_ge(nh_ready, count(i, DT, 0))
                    ve.wait_ge(nl_ready, count(i, DT, 0))
                for m in range(DT):
                    nc.vector.scalar_tensor_tensor(tn[:, m, :], x0[:, m, :], g1[:, m:m + 1], r1[:, :],
                                                   ALU.mult, ALU.mult).then_inc(tn_ready, 1)
                for m in range(DT):
                    ve.wait_ge(tn_ready, count(i, DT, m + 1))
                    ve.wait_ge(nh_ready, count(i, DT, m + 1))
                    nc.vector.scalar_tensor_tensor(nl[:, m, :], tn[:, m, :], b1[:, m:m + 1], nh[:, m, :],
                                                   ALU.add, ALU.subtract).then_inc(nl_ready, 1)

            def features(i, first):
                for j in range(2 * QT):
                    s = j % 2
                    ve.wait_ge(e_ready, count(i, 2 * QT, j + 1))
                    if j >= 2 or not (type(i) is int and i == 0):
                        ve.wait_ge(fl_ready, count(i, 2 * QT, j - 1))
                    nc.vector.scalar_tensor_tensor(fz[:, s, :], pd[s][:, :], 0.0, ez[:, s, :],
                                                   ALU.max, ALU.add).then_inc(f_ready, 1)
                    ve.wait_ge(f_ready, count(i, 2 * QT, j + 1))
                    nc.vector.tensor_copy(qkh[:, j, :], fz[:, s, :]).then_inc(fh_ready, 1)

            def values(i):
                for n in range(2 * CH):
                    c, half = n // 2, n % 2
                    ve.wait_ge(vh_ready, count(i, 2 * CH, n + 1))
                    heads = slice(8 * half, 8 * half + 8)
                    nc.vector.scalar_tensor_tensor(vl[:, c, heads, 0:DH],
                                                   pd[n % 2][:, :].rearrange("p (h e) -> p h e", e=DH), 1 / V_SCALE,
                                                   vh[:, c, heads, 0:DH], ALU.mult, ALU.subtract).then_inc(vl_ready, 1)

            def scores(i, c, quads):
                for q in quads:
                    n = 4 * c + q
                    ve.wait_ge(s_done, count(i, 16, n + 1))
                    if n >= 2 or not (type(i) is int and i == 0):
                        ve.wait_ge(sh_ready, count(i, 16, n - 1))
                        ve.wait_ge(sl_ready, count(i, 16, n - 1))
                    nc.vector.tensor_tensor(sm[:, n % 2, :, :], pS[n % 2][:, :].rearrange("p (a b) -> p a b", b=P),
                                            mask[:, :].unsqueeze(1).broadcast_to([P, 4, P]),
                                            ALU.mult).then_inc(sm_ready, 1)

            def keys(i, c):
                ve.wait_ge(kt_done, count(i, 2 * (CH - 1), 2 * c + 2))
                if c > 0 or not (type(i) is int and i == 0):
                    ve.wait_ge(kv_done, count(i, NKV, 4 * c))
                nc.vector.tensor_copy(ktl[:, :, :], pT[:, :].rearrange("p (a b) -> p a b", b=P)).then_inc(ktl_ready, 1)

            def outputs(i, c, g):
                n = 4 * c + g
                s = n % 2
                heads = pO[g % 2][:, 0:4 * VW].rearrange("p (h e) -> p h e", e=VW)
                ve.wait_ge(o_done, count(i, 16, n + 1))
                nc.vector.tensor_scalar(dn[:, s, :], heads[:, :, DH], DEN_EPS / PHI_DOWN ** 2, None,
                                        ALU.add).then_inc(dn_ready, 1)
                ve.wait_ge(dn_ready, count(i, 16, n + 1))
                nc.vector.reciprocal(rd[:, s, :], dn[:, s, :]).then_inc(rd_ready, 1)
                ve.wait_ge(rd_ready, count(i, 16, n + 1))
                if n >= 2 or not (type(i) is int and i == 0):
                    ve.wait_ge(oh_ready, count(i, 16, n - 1))
                    ve.wait_ge(ol_ready, count(i, 16, n - 1))
                nc.vector.tensor_tensor(on[:, s, :, :], heads[:, :, 0:DH],
                                        rd[:, s, :].unsqueeze(2).broadcast_to([P, 4, DH]),
                                        ALU.mult).then_inc(on_ready, 1)

            def sums(i, c, g):
                u = 4 * c + g
                ve.wait_ge(kv_done, count(i, NKV, u + 1))
                pairs = slice(2 * g, 2 * g + 2)
                found = pKV[:, 0:4 * VW].rearrange("p (a b e) -> p a b e", a=2, b=2)
                if c == 0:
                    if not (type(i) is int and i == 0):
                        ve.wait_ge(kvh_ready, count(i, NKV, 0))
                        ve.wait_ge(kvl_ready, count(i, NKV, 0))
                    nc.vector.tensor_tensor(kvt[:, :, :, :], found, block_mask[:, :, :, :],
                                            ALU.mult).then_inc(kvt_ready, 1)
                    ve.wait_ge(kvt_ready, count(i, NKV, u + 1))
                    nc.vector.tensor_copy(kvacc[:, pairs, :, :], kvt[:, :, :, :]).then_inc(kva_ready, 1)
                else:
                    ve.wait_ge(kva_ready, count(i, NKV, u))
                    nc.vector.tensor_tensor(kvt[:, :, :, :], found, block_mask[:, :, :, :],
                                            ALU.mult).then_inc(kvt_ready, 1)
                    ve.wait_ge(kvt_ready, count(i, NKV, u + 1))
                    ve.wait_ge(kvh_ready, count(i, NKV, u - 3))
                    ve.wait_ge(kvl_ready, count(i, NKV, u - 3))
                    nc.vector.tensor_tensor(kvacc[:, pairs, :, :], kvacc[:, pairs, :, :], kvt[:, :, :, :],
                                            ALU.add).then_inc(kva_ready, 1)

            def turn(i, c, g):
                pass

            def project(i, last):
                pass

            run(ve, dict(mix=mix, mean=mean, var=var, features=features, values=values, scores=scores, keys=keys,
                         outputs=outputs, sums=sums, turn=turn, project=project))

        @block.gpsimd
        def _(gp):
            gp.memset(vh[:, :, :, DH:VW], 1.0).then_inc(v_ones, 1)
            gp.memset(vl[:, :, :, DH:VW], 0.0).then_inc(v_ones, 1)

            def mix(i):
                for k in range(XK):
                    s = k % XS
                    gp.wait_ge(xh_ready, count(i, XK, k + 1))
                    if k >= XS or not (type(i) is int and i == 0):
                        gp.wait_ge(tok_done, count(i, XK, k - XS + 1))
                    nc.gpsimd.tensor_tensor(xl[:, s, :], xs[:, s, :], xh[:, s, :], ALU.subtract).then_inc(xl_ready, 1)

            def nothing(i, *rest):
                pass

            def features(i, first):
                for j in range(2 * QT):
                    gp.wait_ge(fh_ready, count(i, 2 * QT, j + 1))
                    nc.gpsimd.tensor_tensor(qkl[:, j, :], fz[:, j % 2, :], qkh[:, j, :],
                                            ALU.subtract).then_inc(fl_ready, 1)

            def scores(i, c, quads):
                for q in quads:
                    n = 4 * c + q
                    gp.wait_ge(sh_ready, count(i, 16, n + 1))
                    nc.gpsimd.tensor_tensor(sl[:, q, :, :], sm[:, n % 2, :, :], sh[:, q, :, :],
                                            ALU.subtract).then_inc(sl_ready, 1)

            def outputs(i, c, g):
                n = 4 * c + g
                gp.wait_ge(oh_ready, count(i, 16, n + 1))
                nc.gpsimd.tensor_tensor(ol[:, n % 2, :], on[:, n % 2, :, :].rearrange("p a b -> p (a b)"),
                                        oh[:, n % 2, :], ALU.subtract).then_inc(ol_ready, 1)

            def sums(i, c, g):
                u = 4 * c + g
                gp.wait_ge(kvh_ready, count(i, NKV, u + 1))
                pairs = slice(2 * g, 2 * g + 2)
                nc.gpsimd.tensor_tensor(kvl[:, pairs, :, :], kvacc[:, pairs, :, :], kvh[:, pairs, :, :],
                                        ALU.subtract).then_inc(kvl_ready, 1)

            run(gp, dict(mix=mix, mean=nothing, var=nothing, features=features, values=nothing, scores=scores,
                         keys=nothing, outputs=outputs, sums=sums, turn=nothing, project=nothing))
FT = 8
EXPERTS = 8
SLOTS = 1280
TILES = SLOTS // P
TOP = 4
ST = 4
TOKENS = SEQS * T
DUMMIES = P
W1_SCALE = 64.0
W2_SCALE = 64.0
GATE_SCALE = 8.0
SH_SCALE = 16.0
SHD_SCALE = 16.0
FAR = 1.0e6


def mlp_phase(nc, io):
    with ExitStack() as ctx:
        def sb(name, shape, dt=F32):
            return ctx.enter_context(nc.sbuf_tensor(name, [P, *shape], dt))

        def sem(name):
            return ctx.enter_context(nc.semaphore(name))

        w1_h, w1_l = sb("w1_h", [DT, FT * P], F16), sb("w1_l", [DT, FT * P], F16)
        w2_h, w2_l = sb("w2_h", [FT, D], F16), sb("w2_l", [FT, D], F16)
        sg_h, sg_l = sb("sg_h", [DT, 2 * ST * P], F16), sb("sg_l", [DT, 2 * ST * P], F16)
        sd_h, sd_l = sb("sd_h", [ST, D], F16), sb("sd_l", [ST, D], F16)
        gw_h, gw_l = sb("gw_h", [DT, EXPERTS + 1], F16), sb("gw_l", [DT, EXPERTS + 1], F16)
        ones = sb("ones2", [P])
        ones16 = sb("ones16", [P], F16)
        ident = sb("ident2", [P])
        ident16 = sb("ident16", [P], F16)
        upto = sb("upto", [P])
        upto16 = sb("upto16", [P], F16)
        earlier = sb("earlier", [EXPERTS, EXPERTS])
        first_slot = sb("first_slot", [EXPERTS])
        rank_no = sb("rank_no", [TOP, EXPERTS])
        tid = sb("tid", [CH])
        carry = sb("carry", [EXPERTS])
        vecs = sb("vecs", [4, DT])
        b1m = sb("b1m", [FT])
        mb2 = vecs[:, 2, :]
        empty = sb("empty", [EXPERTS * SLOTS // P, 2], U32)
        zrow = sb("zrow", [D])

        with ExitStack() as pre:
            def tmp(name, shape, dt=F32):
                return pre.enter_context(nc.sbuf_tensor(name, [P, *shape], dt))

            w1_w, w2_w = tmp("w1_w", [DT, FT * P]), tmp("w2_w", [FT, D])
            sg_w, sd_w = tmp("sg_w", [DT, 2 * ST * P]), tmp("sd_w", [ST, D])
            gw_w = tmp("gw_w", [DT, EXPERTS + 1])
            dummy_id = tmp("dummy_id", [1])
            loaded = pre.enter_context(nc.semaphore("w2_loaded"))
            hi_ready = pre.enter_context(nc.semaphore("w2_hi"))
            made = pre.enter_context(nc.semaphore("made2"))
            filled = pre.enter_context(nc.semaphore("filled"))
            cleared = pre.enter_context(nc.semaphore("cleared"))
            splits = [(w1_w, w1_h, w1_l, W1_SCALE), (w2_w, w2_h, w2_l, W2_SCALE), (sg_w, sg_h, sg_l, SH_SCALE),
                      (sd_w, sd_h, sd_l, SHD_SCALE), (gw_w, gw_h, gw_l, GATE_SCALE)]
            with nc.Block() as block:
                @block.sync
                def _(sp):
                    sp.dma_start(w1_w[:, :, :], io["w1"].rearrange("(t p) n -> p t n", p=P)).then_inc(loaded, 16)
                    sp.dma_start(w2_w[:, :, :], io["w2"].rearrange("(t p) n -> p t n", p=P)).then_inc(loaded, 16)
                    sp.dma_start(sg_w[:, :, 0:ST * P], io["shgT"].rearrange("(t p) n -> p t n", p=P)).then_inc(loaded, 16)
                    sp.dma_start(sg_w[:, :, ST * P:], io["shuT"].rearrange("(t p) n -> p t n", p=P)).then_inc(loaded, 16)
                    sp.dma_start(sd_w[:, :, :], io["shdT"].rearrange("(t p) n -> p t n", p=P)).then_inc(loaded, 16)
                    sp.dma_start(gw_w[:, :, :], io["gateT"].rearrange("(t p) n -> p t n", p=P)).then_inc(loaded, 16)
                    sp.dma_start(vecs[:, 0, :], io["g2"]).then_inc(loaded, 16)
                    sp.dma_start(vecs[:, 1, :], io["beta2"]).then_inc(loaded, 16)
                    sp.dma_start(vecs[:, 2, :], io["b2"]).then_inc(loaded, 16)
                    sp.dma_start(b1m[:, :], io["b1"]).then_inc(loaded, 16)
                    sp.wait_ge(filled, 1)
                    sp.dma_start(io["out"][TOKENS:TOKENS + DUMMIES, :], zrow[:, :]).then_inc(cleared, 16)
                    sp.dma_start(io["xrow_dram"][TOKENS:TOKENS + DUMMIES, :], zrow[:, :].bitcast(F16)).then_inc(cleared, 16)
                    sp.wait_ge(cleared, 32)
                    sp.wait_ge(loaded, 160)

                @block.gpsimd
                def _(gp):
                    gp.memset(ones[:, :], 1.0 / D).then_inc(made, 1)
                    identity(nc, gp, ident[:, :], made, 1)
                    causal_mask(nc, gp, upto[:, :], made, 3)
                    gp.memset(earlier[:, :, :], 1.0).then_inc(made, 1)
                    gp.wait_ge(made, 6)
                    gp.affine_select(out=earlier[:, :, :], in_=earlier[:, :, :], compare_op=ALU.is_gt, fill=0.0,
                                     base=0, pattern=[[1, EXPERTS], [-1, EXPERTS]],
                                     channel_multiplier=0).then_inc(made, 1)
                    gp.iota(first_slot[:, :], [[SLOTS, EXPERTS]], base=0, channel_multiplier=0,
                            allow_small_or_imprecise_dtypes=True).then_inc(made, 1)
                    gp.iota(rank_no[:, :, :], [[1, TOP], [0, EXPERTS]], base=0, channel_multiplier=0,
                            allow_small_or_imprecise_dtypes=True).then_inc(made, 1)
                    gp.iota(tid[:, :], [[P, CH]], base=0, channel_multiplier=1,
                            allow_small_or_imprecise_dtypes=True).then_inc(made, 1)
                    gp.iota(dummy_id[:, :], [[0, 1]], base=TOKENS, channel_multiplier=1,
                            allow_small_or_imprecise_dtypes=True).then_inc(made, 1)

                @block.vector
                def _(ve):
                    ve.memset(carry[:, :], 0.0)
                    ve.memset(ones16[:, :], 1.0)
                    ve.memset(zrow[:, :], 0.0).then_inc(filled, 1)
                    ve.memset(empty[:, :, :], 0).then_inc(filled, 1)
                    ve.wait_ge(made, 11)
                    ve.wait_ge(filled, 2)
                    nc.vector.tensor_copy(ident16[:, :], ident[:, :])
                    nc.vector.tensor_copy(upto16[:, :], upto[:, :]).then_inc(filled, 1)
                    nc.vector.tensor_copy(empty[:, :, 0],
                                          dummy_id[:, :].broadcast_to([P, EXPERTS * SLOTS // P])).then_inc(filled, 1)
                    ve.wait_ge(loaded, 160)
                    for n, (w, h, l, scale) in enumerate(splits):
                        ve.wait_ge(hi_ready, n + 1)
                        nc.vector.scalar_tensor_tensor(l[:, :, :], w[:, :, :], scale, h[:, :, :],
                                                       ALU.mult, ALU.subtract)

                @block.scalar
                def _(act):
                    act.wait_ge(loaded, 160)
                    for w, h, l, scale in splits:
                        nc.scalar.activation(h[:, :, :], w[:, :, :], ACT.Copy, scale=scale).then_inc(hi_ready, 1)

        x0b, hb_in, atb = sb("x0b", [DT, T]), sb("hb_in", [DT, T]), sb("atb", [DT, T])
        x1, hb, hx = sb("x1", [DT, T]), sb("hb", [DT, T]), sb("hx", [DT, T])
        xc2, sq2, ln2, rs2, tn2 = sb("xc2", [DT, T]), sb("sq2", [DT, T]), sb("ln2", [T]), sb("rs2", [T]), sb("tn2", [DT, T])
        n2h, n2l = sb("n2h", [DT, T], F16), sb("n2l", [DT, T], F16)
        gz = sb("gz", [2, T])
        gh, gl = sb("gh", [FT, T], F16), sb("gl", [FT, T], F16)
        hp = sb("hp", [DT, T])
        xc3, sq3, ln3, rs3, xn = sb("xc3", [DT, T]), sb("sq3", [DT, T]), sb("ln3", [T]), sb("rs3", [T]), sb("xn", [DT, T])
        xnh, xnl = sb("xnh", [DT, T], F16), sb("xnl", [DT, T], F16)
        xt = sb("xt", [CH, 2 * D], F16)
        ht = sb("ht", [CH, D])
        sz, az = sb("sz", [2, T]), sb("az", [2, T])
        ah, al = sb("ah", [ST, T], F16), sb("al", [ST, T], F16)
        ob = sb("ob", [CH, D])
        lg = sb("lg", [CH, EXPERTS + 1])
        pair = [sb(f"pair{i}", [CH * EXPERTS, EXPERTS]) for i in range(5)]
        few = [sb(f"few{i}", [CH, EXPERTS]) for i in range(9)]
        one = [sb(f"one{i}", [CH]) for i in range(6)]
        ml9, e9 = sb("ml9", [CH, EXPERTS + 1]), sb("e9", [CH, EXPERTS + 1])
        rw, m0, rank = sb("rw", [CH, EXPERTS]), sb("m0", [CH, EXPERTS]), sb("rank", [CH, EXPERTS])
        m16 = sb("m16", [CH, EXPERTS], F16)
        w8 = sb("w8", [CH])
        slot_f, w_f = sb("slot_f", [CH, TOP]), sb("w_f", [CH, TOP])
        slot_u = sb("slot_u", [CH, TOP], U32)
        entry = sb("entry", [CH, TOP, 2], U32)

        def bank(name):
            return ctx.enter_context(nc.psum_tensor(name, [P, 512], F32))

        pW = [bank("pW0"), bank("pW1")]
        pY = [bank("pY0"), bank("pY1")]
        pA = [bank("pA0"), bank("pA1")]
        pL = bank("pL")
        cum_at = 64

        (x0_in, h_in, at_in, x1_ready, hb_ready, hx_ready, mean2_done, xc2_ready, sq2_ready, var2_done, rs2_step,
         tn2_ready, n2h_ready, n2l_ready) = [sem(n) for n in (
             "x0_in", "h_in", "at_in", "x1_ready", "hb_ready", "hx_ready", "mean2_done", "xc2_ready", "sq2_ready",
             "var2_done", "rs2_step", "tn2_ready", "n2h_ready", "n2l_ready")]
        (w1_done, gz_ready, gh_ready, gl_ready, w2_done, hp_ready, mean3_done, xc3_ready, sq3_ready, var3_done,
         rs3_step, xn_ready, xnh_ready, xnl_ready) = [sem(n) for n in (
             "w1_done", "gz_ready", "gh_ready", "gl_ready", "w2_done", "hp_ready", "mean3_done", "xc3_ready",
             "sq3_ready", "var3_done", "rs3_step", "xn_ready", "xnh_ready", "xnl_ready")]
        (lg_done, lg_ready, xt_done, xt_ready, xt_stored, ht_done, ht_ready, gu_done, sz_ready, az_ready, ah_ready,
         al_ready, down_done, ob_ready, ob_stored) = [sem(n) for n in (
             "lg_done", "lg_ready", "xt_done", "xt_ready", "xt_stored", "ht_done", "ht_ready", "gu_done", "sz_ready",
             "az_ready", "ah_ready", "al_ready", "down_done", "ob_ready", "ob_stored")]
        (route, route_exp, mask_ready, cum_done, cum_read, routed, list_ready, list_sent, lists_cleared) = [sem(n) for n in (
            "route", "route_exp", "mask_ready", "cum_done", "cum_read", "routed", "list_ready", "list_sent", "lists_cleared")]

        passed = sem("passed2")

        def run(engine, s):
            def body(i, before, after):
                if after:
                    s["mean2"](i + 1)
                s["w1"](i, before)
                if before:
                    s["counts"](i - 1)
                if after:
                    s["var2"](i + 1)
                s["w2"](i)
                s["mean3"](i, before)
                if before:
                    s["gate_up"](i - 1, after)
                s["var3"](i)
                if before:
                    s["down"](i - 1)
                s["logits"](i)
                s["turns"](i, before)

            s["mean2"](0)
            s["var2"](0)
            body(0, False, True)
            body(1, True, True)
            with engine.Fori(2, SEQS - 1) as i:
                body(i, True, True)
            body(SEQS - 1, True, False)
            s["counts"](SEQS - 1)
            s["gate_up"](SEQS - 1, None)
            s["down"](SEQS - 1)

        def at_start(i):
            return type(i) is int and i == 0

        block = ctx.enter_context(nc.Block())

        @block.sync
        def _(sp):
            def load(i):
                if not at_start(i):
                    sp.wait_ge(x1_ready, count(i, DT, 0))
                    sp.wait_ge(hb_ready, count(i, DT, 0))
                for dst, name, arrived in ((x0b, "x0_dram", x0_in), (atb, "at_dram", at_in), (hb_in, "h_dram", h_in)):
                    sp.dma_start(dst[:, :, :], io[name][i].rearrange("t p n -> p t n")).then_inc(arrived, 16)

            def store_rows(i):
                for half in range(2):
                    sp.wait_ge(xt_ready, count(i, 2, half + 1))
                    rows = io["xrow_dram"][0:TOKENS, :].rearrange("(s c p) n -> s p c n", c=CH, p=P)
                    sp.dma_start(rows[i, :, 2 * half:2 * half + 2, :],
                                 xt[:, 2 * half:2 * half + 2, :]).then_inc(xt_stored, 16)

            def store_out(i):
                rows = io["out"][0:TOKENS, :].rearrange("(s c p) n -> s p c n", c=CH, p=P)
                sp.wait_ge(ob_ready, count(i, CH, CH))
                sp.dma_start(rows[i], ob[:, :, :]).then_inc(ob_stored, 16)

            sp.dma_start(io["list_dram"].rearrange("(e p n) w -> p e n w", p=P, n=TILES),
                         empty[:, :, :].rearrange("p (e n) w -> p e n w", n=TILES)).then_inc(lists_cleared, 16)
            load(0)
            load(1)
            load(2)
            store_rows(0)
            load(3)
            store_out(0)
            store_rows(1)
            with sp.Fori(2, SEQS - 2) as i:
                load(i + 2)
                store_out(i - 1)
                store_rows(i)
            store_out(SEQS - 3)
            store_rows(SEQS - 2)
            store_out(SEQS - 2)
            store_rows(SEQS - 1)
            store_out(SEQS - 1)
            sp.wait_ge(xt_stored, 32 * SEQS)
            sp.wait_ge(ob_stored, 16 * SEQS)

        @block.tensor
        def _(pe):
            def three(out, wh, wl, mh, ml, first, last):
                pe.matmul(out, wh, mh, start=first, stop=False, skip_group_check=True)
                pe.matmul(out, wl, mh, start=False, stop=False, skip_group_check=True)
                return pe.matmul(out, wh, ml, start=False, stop=last, skip_group_check=True)

            def mean2(i):
                pe.wait_ge(x1_ready, count(i, DT, DT))
                if not (type(i) is int and i < 2):
                    pe.wait_ge(ht_ready, count(i, 2, -2))
                for t in range(DT):
                    mm = pe.matmul(pA[0][:, :], ones[:, :], x1[:, t, :], start=(t == 0), stop=(t == DT - 1))
                mm.then_inc(mean2_done, 1)

            def var2(i):
                pe.wait_ge(sq2_ready, count(i, DT, DT))
                for t in range(DT):
                    mm = pe.matmul(pA[1][:, :], ones[:, :], sq2[:, t, :], start=(t == 0), stop=(t == DT - 1))
                mm.then_inc(var2_done, 1)

            def w1(i, before):
                pe.wait_ge(n2h_ready, count(i, DT, DT))
                pe.wait_ge(n2l_ready, count(i, DT, DT))
                for j in range(FT):
                    if j >= 2:
                        pe.wait_ge(gz_ready, count(i, FT, j - 1))
                    elif not (type(i) is int and i < 2):
                        pe.wait_ge(az_ready, count(i, ST, -ST))
                    cols = slice(j * P, (j + 1) * P)
                    for t in range(DT):
                        mm = three(pW[j % 2][:, :], w1_h[:, t, cols], w1_l[:, t, cols], n2h[:, t, :], n2l[:, t, :],
                                   t == 0, t == DT - 1)
                    mm.then_inc(w1_done, 1)

            def w2(i):
                if not (type(i) is int and i < 2):
                    pe.wait_ge(ob_ready, count(i, CH, -CH))
                for j in range(FT):
                    pe.wait_ge(gh_ready, count(i, FT, j + 1))
                    pe.wait_ge(gl_ready, count(i, FT, j + 1))
                    for m in range(DT):
                        cols = slice(m * P, (m + 1) * P)
                        mm = three(pY[m][:, :], w2_h[:, j, cols], w2_l[:, j, cols], gh[:, j, :], gl[:, j, :],
                                   j == 0, j == FT - 1)
                mm.then_inc(w2_done, 1)

            def mean3(i, before):
                pe.wait_ge(hp_ready, count(i, DT, DT))
                if before:
                    pe.wait_ge(cum_read, count(i, 1, 0))
                for t in range(DT):
                    mm = pe.matmul(pL[:, :], ones[:, :], hp[:, t, :], start=(t == 0), stop=(t == DT - 1))
                mm.then_inc(mean3_done, 1)

            def gate_up(i, after):
                for j in range(ST):
                    g, u = (pW[0], pW[1]) if j % 2 == 0 else (pA[0], pA[1])
                    if j >= 2:
                        pe.wait_ge(az_ready, count(i, ST, j - 1))
                    elif j == 0 and after is not None:
                        pe.wait_ge(gz_ready, count(i + 1, FT, FT))
                    elif j == 0:
                        pe.wait_ge(gz_ready, FT * SEQS)
                    elif after:
                        pe.wait_ge(xc2_ready, count(i + 2, DT, DT))
                        pe.wait_ge(rs2_step, count(i + 2, 2, 1))
                    else:
                        pe.wait_ge(ht_ready, count(i, 2, 2))
                    for out, base in ((g, 0), (u, ST * P)):
                        cols = slice(base + j * P, base + (j + 1) * P)
                        for t in range(DT):
                            mm = three(out[:, :], sg_h[:, t, cols], sg_l[:, t, cols], xnh[:, t, :], xnl[:, t, :],
                                       t == 0, t == DT - 1)
                        mm.then_inc(gu_done, 1)

            def var3(i):
                pe.wait_ge(sq3_ready, count(i, DT, DT))
                pe.wait_ge(xc3_ready, count(i, DT, DT))
                for t in range(DT):
                    mm = pe.matmul(pL[:, :], ones[:, :], sq3[:, t, :], start=(t == 0), stop=(t == DT - 1))
                mm.then_inc(var3_done, 1)

            def down(i):
                for c in range(CH):
                    if c >= 2:
                        pe.wait_ge(ob_ready, count(i, CH, c - 1))
                    elif c == 0:
                        pe.wait_ge(hp_ready, DT * SEQS if type(i) is int and i == SEQS - 1 else count(i + 1, DT, DT))
                        pe.wait_ge(ah_ready, count(i, ST, ST))
                        pe.wait_ge(al_ready, count(i, ST, ST))
                    toks = slice(c * P, (c + 1) * P)
                    for k in range(ST):
                        mm = three(pY[c % 2][:, 0:D], ah[:, k, toks], al[:, k, toks], sd_h[:, k, :], sd_l[:, k, :],
                                   k == 0, k == ST - 1)
                    mm.then_inc(down_done, 1)

            def logits(i):
                pe.wait_ge(rs3_step, count(i, 2, 1))
                pe.wait_ge(xnh_ready, count(i, DT, DT))
                pe.wait_ge(xnl_ready, count(i, DT, DT))
                n = EXPERTS + 1
                for c in range(CH):
                    toks = slice(c * P, (c + 1) * P)
                    for t in range(DT):
                        mm = three(pL[:, c * n:(c + 1) * n], xnh[:, t, toks], xnl[:, t, toks], gw_h[:, t, :],
                                   gw_l[:, t, :], c == 0 and t == 0, t == DT - 1)
                mm.then_inc(lg_done, 1)

            def turns(i, before):
                for half in range(2):
                    if half == 0:
                        if before:
                            pe.wait_ge(az_ready, count(i, ST, 0))
                        else:
                            pe.wait_ge(xc2_ready, count(i + 1, DT, DT))
                            pe.wait_ge(rs2_step, count(i + 1, 2, 1))
                    bank16 = pA[half][:, :].bitcast(F16)
                    for c in range(2):
                        toks = slice((2 * half + c) * P, (2 * half + c + 1) * P)
                        for part, src in enumerate((xnh, xnl)):
                            for t in range(DT):
                                w = (c * 2 + part) * DT + t
                                mm = pe.transpose(bank16[:, w * P:(w + 1) * P], src[:, t, toks], ident16[:, :])
                    mm.then_inc(xt_done, 1)
                for half in range(2):
                    pe.wait_ge(xt_ready, count(i, 2, half + 1))
                    for c in range(2):
                        toks = slice((2 * half + c) * P, (2 * half + c + 1) * P)
                        for t in range(DT):
                            w = c * DT + t
                            mm = pe.transpose(pA[half][:, w * P:(w + 1) * P], hp[:, t, toks], ident[:, :])
                    mm.then_inc(ht_done, 1)

            def counts(i):
                pe.wait_ge(mask_ready, count(i, 1, 1))
                pe.wait_ge(lg_ready, count(i, 1, 1))
                first = True
                for c in range(CH + 1):
                    out = pL[:, cum_at + c * EXPERTS:cum_at + (c + 1) * EXPERTS]
                    for before in range(c):
                        mm = pe.matmul(out, ones16[:, :], m16[:, before, :], start=first, stop=before == CH - 1,
                                       skip_group_check=True)
                        first = False
                    if c < CH:
                        mm = pe.matmul(out, upto16[:, :], m16[:, c, :], start=first, stop=True, skip_group_check=True)
                        first = False
                mm.then_inc(cum_done, 1)

            run(pe, dict(mean2=mean2, var2=var2, w1=w1, w2=w2, mean3=mean3, gate_up=gate_up, var3=var3, down=down,
                         logits=logits, turns=turns, counts=counts))

        @block.scalar
        def _(act):
            def mean2(i):
                act.wait_ge(h_in, count(i, 16, 16))
                if not at_start(i):
                    act.wait_ge(hx_ready, count(i, DT, 0))
                for m in range(DT):
                    nc.scalar.activation(hb[:, m, :], hb_in[:, m, :], ACT.Identity,
                                         bias=vecs[:, 2, m:m + 1]).then_inc(hb_ready, 1)
                for m in range(DT):
                    act.wait_ge(xc2_ready, count(i, DT, m + 1))
                    nc.scalar.activation(sq2[:, m, :], xc2[:, m, :], ACT.Square).then_inc(sq2_ready, 1)

            def var2(i):
                act.wait_ge(var2_done, count(i, 1, 1))
                nc.scalar.activation(ln2[:, :], pA[1][:, :], ACT.Ln, bias=EPS).then_inc(rs2_step, 1)
                act.wait_ge(rs2_step, count(i, 2, 1))
                if not at_start(i):
                    act.wait_ge(tn2_ready, count(i, DT, 0))
                nc.scalar.activation(rs2[:, :], ln2[:, :], ACT.Exp, scale=-0.5).then_inc(rs2_step, 1)
                for m in range(DT):
                    act.wait_ge(tn2_ready, count(i, DT, m + 1))
                    if not at_start(i):
                        act.wait_ge(w1_done, count(i, FT, 0))
                    nc.scalar.activation(n2h[:, m, :], tn2[:, m, :], ACT.Identity,
                                         bias=vecs[:, 1, m:m + 1]).then_inc(n2h_ready, 1)

            def w1(i, before):
                for j in range(FT):
                    act.wait_ge(w1_done, count(i, FT, j + 1))
                    if j >= 2 or not at_start(i):
                        act.wait_ge(gl_ready, count(i, FT, j - 1))
                    nc.scalar.activation(gz[:, j % 2, :], pW[j % 2][:, :], ACT.Gelu, scale=1 / W1_SCALE,
                                         bias=b1m[:, j:j + 1]).then_inc(gz_ready, 1)

            def mean3(i, before):
                for m in range(DT):
                    act.wait_ge(xc3_ready, count(i, DT, m + 1))
                    nc.scalar.activation(sq3[:, m, :], xc3[:, m, :], ACT.Square).then_inc(sq3_ready, 1)

            def gate_up(i, after):
                for j in range(ST):
                    g = pW[0] if j % 2 == 0 else pA[0]
                    act.wait_ge(gu_done, count(i, 2 * ST, 2 * j + 1))
                    if j >= 2 or not at_start(i):
                        act.wait_ge(az_ready, count(i, ST, j - 1))
                    nc.scalar.activation(sz[:, j % 2, :], g[:, :], ACT.Silu, scale=1 / SH_SCALE).then_inc(sz_ready, 1)

            def var3(i):
                act.wait_ge(var3_done, count(i, 1, 1))
                nc.scalar.activation(ln3[:, :], pL[:, :], ACT.Ln, bias=EPS).then_inc(rs3_step, 1)
                act.wait_ge(rs3_step, count(i, 2, 1))
                if not at_start(i):
                    act.wait_ge(xn_ready, count(i, DT, 0))
                nc.scalar.activation(rs3[:, :], ln3[:, :], ACT.Exp, scale=-0.5).then_inc(rs3_step, 1)

            def logits(i):
                act.wait_ge(lg_done, count(i, 1, 1))
                if not at_start(i):
                    act.wait_ge(routed, count(i, 1, 0))
                nc.scalar.activation(lg[:, :, :], pL[:, 0:CH * (EXPERTS + 1)].rearrange("p (c e) -> p c e", c=CH),
                                     ACT.Copy, scale=1 / GATE_SCALE).then_inc(lg_ready, 1)
                act.wait_ge(route, count(i, ROUTE_STEPS, EXP1_AFTER))
                nc.scalar.activation(few[1][:, :, :], few[0][:, :, :], ACT.Exp).then_inc(route_exp, 1)

            def turns(i, before):
                for half in range(2):
                    act.wait_ge(xt_done, count(i, 2, half + 1))
                    if not at_start(i):
                        act.wait_ge(xt_stored, count(i, 32, 0))
                    nc.scalar.activation(xt[:, 2 * half:2 * half + 2, :],
                                         pA[half][:, :].bitcast(F16).rearrange("p (c n) -> p c n", c=2),
                                         ACT.Copy).then_inc(xt_ready, 1)
                for half in range(2):
                    act.wait_ge(ht_done, count(i, 2, half + 1))
                    if not at_start(i):
                        act.wait_ge(ob_ready, count(i, CH, 0))
                    nc.scalar.activation(ht[:, 2 * half:2 * half + 2, :],
                                         pA[half][:, :].rearrange("p (c n) -> p c n", c=2), ACT.Copy).then_inc(ht_ready, 1)

            def counts(i):
                act.wait_ge(route, count(i, ROUTE_STEPS, EXP2_AFTER))
                nc.scalar.activation(e9[:, :, :], ml9[:, :, :], ACT.Exp).then_inc(route_exp, 1)

            def nothing(i, *rest):
                pass

            run(act, dict(mean2=mean2, var2=var2, w1=w1, w2=nothing, mean3=mean3, gate_up=gate_up, var3=var3,
                          down=nothing, logits=logits, turns=turns, counts=counts))

        @block.vector
        def _(ve):
            def mean2(i):
                ve.wait_ge(mean2_done, count(i, 1, 1))
                if not at_start(i):
                    ve.wait_ge(tn2_ready, count(i, DT, 0))
                for m in range(DT):
                    nc.vector.tensor_tensor(xc2[:, m, :], x1[:, m, :], pA[0][:, :], ALU.subtract).then_inc(xc2_ready, 1)

            def var2(i):
                ve.wait_ge(rs2_step, count(i, 2, 2))
                ve.wait_ge(xc2_ready, count(i, DT, DT))
                if not at_start(i):
                    ve.wait_ge(n2h_ready, count(i, DT, 0))
                    ve.wait_ge(n2l_ready, count(i, DT, 0))
                for m in range(DT):
                    nc.vector.scalar_tensor_tensor(tn2[:, m, :], xc2[:, m, :], vecs[:, 0, m:m + 1], rs2[:, :],
                                                   ALU.mult, ALU.mult).then_inc(tn2_ready, 1)
                for m in range(DT):
                    ve.wait_ge(tn2_ready, count(i, DT, m + 1))
                    ve.wait_ge(n2h_ready, count(i, DT, m + 1))
                    nc.vector.scalar_tensor_tensor(n2l[:, m, :], tn2[:, m, :], vecs[:, 1, m:m + 1], n2h[:, m, :],
                                                   ALU.add, ALU.subtract).then_inc(n2l_ready, 1)

            def w1(i, before):
                if not at_start(i):
                    ve.wait_ge(w2_done, count(i, 1, 0))
                for j in range(FT):
                    ve.wait_ge(gz_ready, count(i, FT, j + 1))
                    nc.vector.tensor_copy(gh[:, j, :], gz[:, j % 2, :]).then_inc(gh_ready, 1)

            def w2(i):
                ve.wait_ge(w2_done, count(i, 1, 1))
                ve.wait_ge(hx_ready, count(i, DT, DT))
                if not at_start(i):
                    ve.wait_ge(ht_done, count(i, 2, 0))
                for m in range(DT):
                    nc.vector.scalar_tensor_tensor(hp[:, m, :], pY[m][:, :], 1 / W2_SCALE, hx[:, m, :],
                                                   ALU.mult, ALU.add).then_inc(hp_ready, 1)

            def mean3(i, before):
                ve.wait_ge(mean3_done, count(i, 1, 1))
                ve.wait_ge(hp_ready, count(i, DT, DT))
                for m in range(DT):
                    nc.vector.tensor_tensor(xc3[:, m, :], hp[:, m, :], pL[:, :], ALU.subtract).then_inc(xc3_ready, 1)

            def gate_up(i, after):
                for j in range(ST):
                    u = pW[1] if j % 2 == 0 else pA[1]
                    ve.wait_ge(gu_done, count(i, 2 * ST, 2 * j + 2))
                    ve.wait_ge(sz_ready, count(i, ST, j + 1))
                    if j >= 2 or not at_start(i):
                        ve.wait_ge(al_ready, count(i, ST, j - 1))
                    nc.vector.scalar_tensor_tensor(az[:, j % 2, :], u[:, :], 1 / SH_SCALE, sz[:, j % 2, :],
                                                   ALU.mult, ALU.mult).then_inc(az_ready, 1)
                    ve.wait_ge(az_ready, count(i, ST, j + 1))
                    if not at_start(i):
                        ve.wait_ge(down_done, count(i, CH, 0))
                    nc.vector.tensor_copy(ah[:, j, :], az[:, j % 2, :]).then_inc(ah_ready, 1)

            def var3(i):
                ve.wait_ge(rs3_step, count(i, 2, 2))
                ve.wait_ge(xc3_ready, count(i, DT, DT))
                if not at_start(i):
                    ve.wait_ge(xnl_ready, count(i, DT, 0))
                    ve.wait_ge(xt_done, count(i, 2, 0))
                    ve.wait_ge(gu_done, count(i, 2 * ST, 0))
                for m in range(DT):
                    nc.vector.tensor_tensor(xn[:, m, :], xc3[:, m, :], rs3[:, :], ALU.mult).then_inc(xn_ready, 1)
                for m in range(DT):
                    ve.wait_ge(xn_ready, count(i, DT, m + 1))
                    nc.vector.tensor_copy(xnh[:, m, :], xn[:, m, :]).then_inc(xnh_ready, 1)

            def down(i):
                ve.wait_ge(routed, count(i, 1, 1))
                ve.wait_ge(ht_ready, count(i, 2, 2))
                if not at_start(i):
                    ve.wait_ge(ob_stored, count(i, 16, 0))
                for c in range(CH):
                    ve.wait_ge(down_done, count(i, CH, c + 1))
                    nc.vector.scalar_tensor_tensor(ob[:, c, :], pY[c % 2][:, 0:D], w8[:, c:c + 1], ht[:, c, :],
                                                   ALU.mult, ALU.add).then_inc(ob_ready, 1)

            def flat(t):
                return t[:, :, :].rearrange("p c e -> p (c e)")

            def routing(i, lo, hi):
                E = EXPERTS
                state = [0]

                def link(make):
                    state[0] += 1
                    if lo < state[0] <= hi:
                        make().then_inc(route, 1)
                        ve.wait_ge(route, count(i, ROUTE_STEPS, state[0]))

                def wait(sem_, per, k):
                    if lo <= state[0] < hi:
                        ve.wait_ge(sem_, count(i, per, k))

                V = nc.vector
                mine = lg[:, :, 0:E].unsqueeze(3).broadcast_to([P, CH, E, E])
                other = lg[:, :, 0:E].unsqueeze(2).broadcast_to([P, CH, E, E])

                def cube(t):
                    return t[:, :, :].rearrange("p (c e) f -> p c e f", c=CH)

                def over_mine(t):
                    return t[:, :, :].unsqueeze(2).broadcast_to([P, CH, E, E])

                def per_chunk(t):
                    return t[:, :].unsqueeze(2).broadcast_to([P, CH, E])

                before, scr, near, a, b = pair
                lead, ex, cprev, su, mu, mf, t1, t2, gd = few
                mx, z, zq, s1, r1_, zd = one
                link(lambda: V.tensor_reduce(mx[:, :], lg[:, :, 0:E], AX.X, ALU.max))
                link(lambda: V.tensor_tensor(lead[:, :, :], lg[:, :, 0:E], per_chunk(mx), ALU.subtract))
                link(lambda: V.tensor_tensor(cube(scr), other, mine, ALU.is_equal))
                link(lambda: V.tensor_tensor(cube(scr), cube(scr),
                                             earlier[:, :, :].unsqueeze(1).broadcast_to([P, CH, E, E]), ALU.mult))
                link(lambda: V.tensor_tensor(cube(before), other, mine, ALU.is_gt))
                link(lambda: V.tensor_tensor(before[:, :, :], before[:, :, :], scr[:, :, :], ALU.add))
                link(lambda: V.tensor_reduce(flat(rank), before[:, :, :], AX.X, ALU.add))
                link(lambda: V.scalar_tensor_tensor(mu[:, :, :], lg[:, :, 0:E], -1.0, lg[:, :, 0:E], ALU.mult, ALU.max))
                link(lambda: V.tensor_tensor(cube(a), over_mine(mu),
                                             mu[:, :, :].unsqueeze(3).broadcast_to([P, CH, E, E]), ALU.max))
                link(lambda: V.tensor_tensor(cube(b), mine, other, ALU.subtract))
                link(lambda: V.scalar_tensor_tensor(near[:, :, :], a[:, :, :], 0.2, b[:, :, :], ALU.mult, ALU.is_ge))
                link(lambda: V.scalar_tensor_tensor(near[:, :, :], before[:, :, :], 0.5, near[:, :, :],
                                                    ALU.is_lt, ALU.mult))
                wait(route_exp, 2, 1)
                link(lambda: V.tensor_tensor(cube(a), cube(near), over_mine(ex), ALU.mult))
                link(lambda: V.tensor_reduce(flat(su), a[:, :, :], AX.X, ALU.add))
                link(lambda: V.tensor_scalar(su[:, :, :], su[:, :, :], 1e-37, None, ALU.max))
                link(lambda: V.reciprocal(t1[:, :, :], su[:, :, :]))
                link(lambda: V.tensor_tensor(mu[:, :, :], ex[:, :, :], t1[:, :, :], ALU.mult))
                link(lambda: V.tensor_tensor(cube(b), cube(before), over_mine(ex), ALU.mult))
                link(lambda: V.tensor_reduce(flat(cprev), b[:, :, :], AX.X, ALU.add))
                link(lambda: V.tensor_reduce(z[:, :], ex[:, :, :], AX.X, ALU.add))
                link(lambda: V.tensor_scalar(zq[:, :], z[:, :], 0.75, None, ALU.mult))
                link(lambda: V.tensor_tensor(t2[:, :, :], cprev[:, :, :], per_chunk(zq), ALU.is_lt))
                link(lambda: V.scalar_tensor_tensor(t2[:, :, :], rank[:, :, :], TOP - 0.5, t2[:, :, :],
                                                    ALU.is_lt, ALU.mult))
                link(lambda: V.tensor_tensor(rw[:, :, :], mu[:, :, :], t2[:, :, :], ALU.mult))
                link(lambda: V.tensor_reduce(s1[:, :], rw[:, :, :], AX.X, ALU.add))
                link(lambda: V.reciprocal(r1_[:, :], s1[:, :]))
                link(lambda: V.tensor_tensor(rw[:, :, :], rw[:, :, :], per_chunk(r1_), ALU.mult))
                link(lambda: V.tensor_scalar(m0[:, :, :], rw[:, :, :], 0.0, None, ALU.is_gt))
                assert state[0] == MASK_AFTER
                if lo < MASK_AFTER <= hi:
                    V.tensor_copy(m16[:, :, :], m0[:, :, :]).then_inc(mask_ready, 1)
                wait(cum_done, 1, 1)
                link(lambda: V.tensor_tensor(t1[:, :, :], pL[:, cum_at:cum_at + CH * E].rearrange("p (c e) -> p c e", c=CH),
                                             carry[:, :].unsqueeze(1).broadcast_to([P, CH, E]), ALU.add))
                link(lambda: V.tensor_tensor(carry[:, :], carry[:, :], pL[:, cum_at + CH * E:cum_at + (CH + 1) * E], ALU.add))
                if lo < state[0] <= hi:
                    V.scalar_tensor_tensor(mf[:, :, :], t1[:, :, :], SLOTS + 0.5, m0[:, :, :],
                                           ALU.is_lt, ALU.mult).then_inc(cum_read, 1)
                    ve.wait_ge(cum_read, count(i, 1, 1))
                link(lambda: V.tensor_scalar(t2[:, :, :], mf[:, :, :], 1.0, 1e30, ALU.subtract, ALU.mult))
                link(lambda: V.tensor_tensor(ml9[:, :, 0:E], lg[:, :, 0:E], mf[:, :, :], ALU.mult))
                link(lambda: V.tensor_tensor(ml9[:, :, 0:E], ml9[:, :, 0:E], t2[:, :, :], ALU.add))
                link(lambda: V.tensor_copy(ml9[:, :, E], lg[:, :, E]))
                link(lambda: V.tensor_reduce(mx[:, :], ml9[:, :, :], AX.X, ALU.max))
                link(lambda: V.tensor_tensor(ml9[:, :, :], ml9[:, :, :], mx[:, :].unsqueeze(2).broadcast_to([P, CH, E + 1]),
                                             ALU.subtract))
                assert state[0] == EXP2_AFTER
                link(lambda: V.tensor_tensor(t1[:, :, :], t1[:, :, :],
                                             first_slot[:, :].unsqueeze(1).broadcast_to([P, CH, E]), ALU.add))
                link(lambda: V.tensor_tensor(t1[:, :, :], t1[:, :, :], mf[:, :, :], ALU.mult))
                wait(route_exp, 2, 2)
                link(lambda: V.tensor_reduce(zd[:, :], e9[:, :, 0:E], AX.X, ALU.add))
                link(lambda: V.tensor_tensor(z[:, :], zd[:, :], e9[:, :, E], ALU.add))
                link(lambda: V.reciprocal(zq[:, :], z[:, :]))
                link(lambda: V.scalar_tensor_tensor(w8[:, :], e9[:, :, E], 1 / SHD_SCALE, zq[:, :], ALU.mult, ALU.mult))
                link(lambda: V.tensor_tensor(s1[:, :], zd[:, :], zq[:, :], ALU.mult))
                link(lambda: V.tensor_tensor(gd[:, :, :], rw[:, :, :], per_chunk(s1), ALU.mult))
                link(lambda: V.tensor_tensor(gd[:, :, :], gd[:, :, :], mf[:, :, :], ALU.mult))
                by_rank = a[:, 0:CH * TOP, :].rearrange("p (c k) e -> p c k e", c=CH)
                picked = b[:, 0:CH * TOP, :].rearrange("p (c k) e -> p c k e", c=CH)

                def over_ranks(t):
                    return t[:, :, :].unsqueeze(2).broadcast_to([P, CH, TOP, E])

                link(lambda: V.tensor_tensor(by_rank, over_ranks(rank),
                                             rank_no[:, :, :].unsqueeze(1).broadcast_to([P, CH, TOP, E]), ALU.is_equal))
                link(lambda: V.tensor_tensor(picked, by_rank, over_ranks(t1), ALU.mult))
                link(lambda: V.tensor_reduce(flat(slot_f), b[:, 0:CH * TOP, :], AX.X, ALU.add))
                link(lambda: V.tensor_tensor(picked, by_rank, over_ranks(gd), ALU.mult))
                if lo <= state[0] < hi and not at_start(i):
                    ve.wait_ge(list_sent, count(i, 16 * CH * TOP, 0))
                link(lambda: V.tensor_reduce(w_f[:, :, :].rearrange("p c k -> p (c k)"), b[:, 0:CH * TOP, :], AX.X, ALU.add))
                link(lambda: V.tensor_copy(entry[:, :, :, 1].bitcast(F32), w_f[:, :, :]))
                link(lambda: V.tensor_copy(entry[:, :, :, 0], tid[:, :].unsqueeze(2).broadcast_to([P, CH, TOP])))
                link(lambda: V.tensor_scalar(tid[:, :], tid[:, :], float(T), None, ALU.add))
                link(lambda: V.tensor_scalar(w_f[:, :, :], slot_f[:, :, :], 0.0, FAR, ALU.is_equal, ALU.mult))
                if hi == ROUTE_STEPS:
                    V.scalar_tensor_tensor(slot_u[:, :, :], slot_f[:, :, :], -1.0, w_f[:, :, :],
                                           ALU.add, ALU.add).then_inc(routed, 1)
                assert state[0] == ROUTE_STEPS, state

            def logits(i):
                ve.wait_ge(lg_ready, count(i, 1, 1))
                routing(i, 0, MASK_AFTER)

            def counts(i):
                routing(i, MASK_AFTER, ROUTE_STEPS)

            def nothing(i, *rest):
                pass

            run(ve, dict(mean2=mean2, var2=var2, w1=w1, w2=w2, mean3=mean3, gate_up=gate_up, var3=var3, down=down,
                         logits=logits, turns=nothing, counts=counts))

        @block.gpsimd
        def _(gp):
            def mean2(i):
                gp.wait_ge(x0_in, count(i, 16, 16))
                gp.wait_ge(at_in, count(i, 16, 16))
                if not at_start(i):
                    gp.wait_ge(xc2_ready, count(i, DT, 0))
                    gp.wait_ge(mean2_done, count(i, 1, 0))
                    gp.wait_ge(hx_ready, count(i, DT, 0))
                for m in range(DT):
                    nc.gpsimd.tensor_tensor(x1[:, m, :], x0b[:, m, :], atb[:, m, :], ALU.add).then_inc(x1_ready, 1)

            def w1(i, before):
                for j in range(FT):
                    gp.wait_ge(gh_ready, count(i, FT, j + 1))
                    nc.gpsimd.tensor_tensor(gl[:, j, :], gz[:, j % 2, :], gh[:, j, :], ALU.subtract).then_inc(gl_ready, 1)

            def sums(i):
                gp.wait_ge(hb_ready, count(i, DT, DT))
                gp.wait_ge(x1_ready, count(i, DT, DT))
                if not at_start(i):
                    gp.wait_ge(hp_ready, count(i, DT, 0))
                for m in range(DT):
                    nc.gpsimd.tensor_tensor(hx[:, m, :], hb[:, m, :], x1[:, m, :], ALU.add).then_inc(hx_ready, 1)

            def gate_up(i, after):
                for j in range(ST):
                    gp.wait_ge(ah_ready, count(i, ST, j + 1))
                    nc.gpsimd.tensor_tensor(al[:, j, :], az[:, j % 2, :], ah[:, j, :], ALU.subtract).then_inc(al_ready, 1)

            def var3(i):
                for m in range(DT):
                    gp.wait_ge(xnh_ready, count(i, DT, m + 1))
                    nc.gpsimd.tensor_tensor(xnl[:, m, :], xn[:, m, :], xnh[:, m, :], ALU.subtract).then_inc(xnl_ready, 1)

            def send(i):
                gp.wait_ge(lists_cleared, 16)
                gp.wait_ge(routed, count(i, 1, 1))
                gp.sem_inc(passed, 1)
                for c in range(CH):
                    for k in range(TOP):
                        nc.gpsimd.indirect_dma_start(
                            io["list_dram"], bass.IndirectOffsetOnAxis(slot_u[:, c, k:k + 1], 0), entry[:, c, k, :],
                            None, bounds_check=EXPERTS * SLOTS - 1, oob_is_err=False).then_inc(list_sent, 16)

            def nothing(i, *rest):
                pass

            def mean3(i, before):
                if type(i) is int and i == SEQS - 1:
                    return
                sums(i + 1)

            def var2(i):
                if at_start(i):
                    sums(0)

            def counts(i):
                pass

            def down(i):
                send(i)

            run(gp, dict(mean2=mean2, var2=var2, w1=w1, w2=nothing, mean3=mean3, gate_up=gate_up, var3=var3,
                         down=down, logits=nothing, turns=nothing, counts=counts))
            gp.wait_ge(list_sent, 16 * CH * TOP * SEQS)


ROUTE_STEPS = 54
EXP1_AFTER = 2
MASK_AFTER = 28
EXP2_AFTER = 36
DYN_SCALE = 8.0
WCOLS = 2 * DT * P + D
GROUPS = TILES // 2
PG = 2 * GROUPS
PT = 2 * TILES
RING = 10


def routed_phase(nc, io):
    with ExitStack() as ctx:
        def sb(name, shape, dt=F32):
            return ctx.enter_context(nc.sbuf_tensor(name, [P, *shape], dt))

        def sem(name):
            return ctx.enter_context(nc.semaphore(name))

        def bank(name):
            return ctx.enter_context(nc.psum_tensor(name, [P, 512], F32))

        ident = sb("ident3", [P], F16)
        wf = sb("wf", [2, WCOLS])
        wh, wl = sb("wh", [2, WCOLS], F16), sb("wl", [2, WCOLS], F16)
        gid = sb("gid", [TILES * 2, 2], U32)
        sid = sb("sid", [TILES * 2, 2], U32)
        lw = sb("lw", [TILES * 2])
        xg = sb("xg", [RING, 2 * D], F16)
        xf = sb("xf", [2, 2 * DT, 2 * P], F16)
        sz, az = sb("sz3", [2, 2 * P]), sb("az3", [2, 2 * P])
        ah, al = sb("ah3", [2, 2 * P], F16), sb("al3", [2, 2 * P], F16)
        yb = sb("yb", [4, D])
        pT = [bank("pT3a"), bank("pT3b")]
        pG = [bank("pG3a"), bank("pG3b")]
        pD = [bank("pD3a"), bank("pD3b")]

        made, gid_in, sid_in, lw_ready = sem("made3"), sem("gid_in"), sem("sid_in"), sem("lw_ready")
        w_in = [sem("w_in0"), sem("w_in1")]
        wh_ready, wl_ready = sem("wh_ready"), sem("wl_ready")
        gathered = [sem(f"gathered{n}") for n in range(RING)]
        t_done, xf_ready, gu_done = sem("t_done"), sem("xf_ready"), sem("gu_done3")
        sz_ready, az_ready, ah_ready, al_ready = sem("sz_ready3"), sem("az_ready3"), sem("ah_ready3"), sem("al_ready3")
        d_done, y_ready = sem("d_done"), sem("y_ready")
        added = [sem(f"added{n}") for n in range(4)]
        passed = sem("passed")
        PAIRS = EXPERTS // 2
        lists = io["list_dram"].rearrange("(e two p n) w -> e p two n w", two=2, p=P, n=TILES)

        def at_start(i):
            return type(i) is int and i == 0

        def run(engine, body):
            body(0, True)
            with engine.Fori(1, PAIRS - 1) as i:
                body(i, True)
            body(PAIRS - 1, False)

        block = ctx.enter_context(nc.Block())

        @block.sync
        def _(sp):
            def gather_list(i):
                if not at_start(i):
                    for n in range(RING):
                        sp.wait_ge(gathered[n], count(i, 32, 0))
                sp.dma_start(gid[:, :, :].rearrange("p (two n) w -> p two n w", two=2), lists[i]).then_inc(gid_in, 16)

            def scatter_list(i):
                if not at_start(i):
                    for n in range(4):
                        sp.wait_ge(added[n], count(i, 80, 0))
                    sp.wait_ge(lw_ready, count(i, 1, 0))
                sp.dma_start(sid[:, :, :].rearrange("p (two n) w -> p two n w", two=2), lists[i]).then_inc(sid_in, 16)

            def weights(i, s):
                if not at_start(i):
                    sp.wait_ge(wl_ready, count(i, 2, s - 1))
                pairs = io["dyn_w"].rearrange("(e two) p n -> e two p n", two=2)
                sp.dma_start(wf[:, s, :], pairs[i, s]).then_inc(w_in[s], 16)

            def body(i, more):
                if more:
                    weights(i + 1, 0)
                    gather_list(i + 1)
                    weights(i + 1, 1)
                    scatter_list(i + 1)

            gather_list(0)
            weights(0, 0)
            weights(0, 1)
            scatter_list(0)
            run(sp, body)

        @block.tensor
        def _(pe):
            def three(out, wh_, wl_, mh, ml, first, last):
                pe.matmul(out, wh_, mh, start=first, stop=False, skip_group_check=True)
                pe.matmul(out, wl_, mh, start=False, stop=False, skip_group_check=True)
                return pe.matmul(out, wh_, ml, start=False, stop=last, skip_group_check=True)

            def turn(i, g):
                if g >= 2 or not at_start(i):
                    pe.wait_ge(xf_ready, count(i, PG, g - 1))
                out = pT[g % 2][:, :].bitcast(F16)
                for b in range(2):
                    slot = (2 * g + b) % RING
                    pe.wait_ge(gathered[slot], count(i, 32, 16 * ((2 * g + b) // RING + 1)))
                    for w in range(2 * DT):
                        at = w * 2 * P + b * P
                        mm = pe.transpose(out[:, at:at + P], xg[:, slot, w * P:(w + 1) * P], ident[:, :])
                mm.then_inc(t_done, 1)

            def gate_up(i, g):
                e = g // GROUPS
                if g % GROUPS == 0:
                    pe.wait_ge(wh_ready, count(i, 2, e + 1))
                    pe.wait_ge(wl_ready, count(i, 2, e + 1))
                pe.wait_ge(xf_ready, count(i, PG, g + 1))
                if g >= 2 or not at_start(i):
                    pe.wait_ge(az_ready, count(i, PG, g - 1))
                for half in range(2):
                    for t in range(DT):
                        at = (half * DT + t) * P
                        mm = three(pG[g % 2][:, half * 2 * P:(half + 1) * 2 * P], wh[:, e, at:at + P], wl[:, e, at:at + P],
                                   xf[:, g % 2, t, :], xf[:, g % 2, DT + t, :], half == 0 and t == 0, t == DT - 1)
                mm.then_inc(gu_done, 1)

            def down(i, g):
                e = g // GROUPS
                pe.wait_ge(ah_ready, count(i, PG, g + 1))
                pe.wait_ge(al_ready, count(i, PG, g + 1))
                if g >= 2 or not at_start(i):
                    pe.wait_ge(y_ready, count(i, PT, 2 * (g - 1)))
                cols = slice(2 * DT * P, WCOLS)
                for b in range(2):
                    toks = slice(b * P, (b + 1) * P)
                    mm = three(pD[g % 2][:, b * D:(b + 1) * D], ah[:, g % 2, toks], al[:, g % 2, toks],
                               wh[:, e, cols], wl[:, e, cols], b == 0, True)
                mm.then_inc(d_done, 1)

            def body(i, more):
                turn(i, 0)
                for g in range(PG):
                    if g + 1 < PG:
                        turn(i, g + 1)
                    gate_up(i, g)
                    if g > 0:
                        down(i, g - 1)
                down(i, PG - 1)

            pe.wait_ge(made, 2)
            run(pe, body)

        @block.scalar
        def _(act):
            def split(i, e):
                act.wait_ge(w_in[e], count(i, 16, 16))
                if not at_start(i):
                    act.wait_ge(d_done, count(i, PG, (e - 1) * GROUPS))
                nc.scalar.activation(wh[:, e, :], wf[:, e, :], ACT.Copy, scale=DYN_SCALE).then_inc(wh_ready, 1)

            def silu(i, g):
                act.wait_ge(gu_done, count(i, PG, g + 1))
                if g >= 2 or not at_start(i):
                    act.wait_ge(az_ready, count(i, PG, g - 1))
                nc.scalar.activation(sz[:, g % 2, :], pG[g % 2][:, 0:2 * P], ACT.Silu,
                                     scale=1 / DYN_SCALE).then_inc(sz_ready, 1)

            def weigh(i, g):
                act.wait_ge(d_done, count(i, PG, g + 1))
                if g == 0:
                    act.wait_ge(lw_ready, count(i, 1, 1))
                for b in range(2):
                    n = 2 * g + b
                    if n >= 4 or not at_start(i):
                        act.wait_ge(added[n % 4], count(i, 80, 16 * (n // 4)))
                    nc.scalar.activation(yb[:, n % 4, :], pD[g % 2][:, b * D:(b + 1) * D], ACT.Copy,
                                         scale=lw[:, n:n + 1]).then_inc(y_ready, 1)

            def body(i, more):
                for g in range(PG):
                    if g == 1:
                        split(i, 1)
                    if g == GROUPS + 1 and more:
                        split(i + 1, 0)
                    silu(i, g)
                    if g > 0:
                        weigh(i, g - 1)
                weigh(i, PG - 1)

            split(0, 0)
            run(act, body)

        @block.vector
        def _(ve):
            def split(i, e):
                ve.wait_ge(wh_ready, count(i, 2, e + 1))
                nc.vector.scalar_tensor_tensor(wl[:, e, :], wf[:, e, :], DYN_SCALE, wh[:, e, :],
                                               ALU.mult, ALU.subtract).then_inc(wl_ready, 1)

            def weights_of_list(i):
                ve.wait_ge(sid_in, count(i, 16, 16))
                if not at_start(i):
                    ve.wait_ge(y_ready, count(i, PT, 0))
                nc.vector.tensor_scalar(lw[:, :], sid[:, :, 1].bitcast(F32), 1 / DYN_SCALE, None,
                                        ALU.mult).then_inc(lw_ready, 1)

            def features(i, g):
                ve.wait_ge(t_done, count(i, PG, g + 1))
                if g >= 2 or not at_start(i):
                    ve.wait_ge(gu_done, count(i, PG, g - 1))
                nc.vector.tensor_copy(xf[:, g % 2, :, :], pT[g % 2][:, :].bitcast(F16).rearrange(
                    "p (w n) -> p w n", n=2 * P)).then_inc(xf_ready, 1)

            def hidden(i, g):
                s = g % 2
                ve.wait_ge(sz_ready, count(i, PG, g + 1))
                nc.vector.scalar_tensor_tensor(az[:, s, :], pG[s][:, 2 * P:], 1 / DYN_SCALE, sz[:, s, :],
                                               ALU.mult, ALU.mult).then_inc(az_ready, 1)
                ve.wait_ge(az_ready, count(i, PG, g + 1))
                if g >= 2 or not at_start(i):
                    ve.wait_ge(d_done, count(i, PG, g - 1))
                nc.vector.tensor_copy(ah[:, s, :], az[:, s, :]).then_inc(ah_ready, 1)
                ve.wait_ge(ah_ready, count(i, PG, g + 1))
                nc.vector.tensor_tensor(al[:, s, :], az[:, s, :], ah[:, s, :], ALU.subtract).then_inc(al_ready, 1)

            def body(i, more):
                features(i, 0)
                weights_of_list(i)
                for g in range(PG):
                    if g + 1 < PG:
                        features(i, g + 1)
                    if g == 1:
                        split(i, 1)
                    if g == GROUPS + 1 and more:
                        split(i + 1, 0)
                    hidden(i, g)

            split(0, 0)
            run(ve, body)

        @block.gpsimd
        def _(gp):
            identity(nc, gp, ident[:, :], made, 0)

            def gather(i, n):
                if n == 0:
                    gp.wait_ge(gid_in, count(i, 16, 16))
                if n >= RING or not at_start(i):
                    gp.wait_ge(t_done, count(i, PG, (n - RING) // 2 + 1))
                gp.sem_inc(passed, 1)
                nc.gpsimd.indirect_dma_start(xg[:, n % RING, :], None, io["xrow_dram"],
                                             bass.IndirectOffsetOnAxis(gid[:, n, 0:1], 0)).then_inc(gathered[n % RING], 16)

            def add(i, g):
                for b in range(2):
                    n = 2 * g + b
                    gp.wait_ge(y_ready, count(i, PT, n + 1))
                    if n % TILES == 0 and (n > 0 or not at_start(i)):
                        for s in range(4):
                            done = len([m for m in range(n) if m % 4 == s])
                            gp.wait_ge(added[s], count(i, 80, 16 * done))
                    gp.sem_inc(passed, 1)
                    nc.gpsimd.indirect_dma_start(io["out"], bass.IndirectOffsetOnAxis(sid[:, n, 0:1], 0),
                                                 yb[:, n % 4, :], None, compute_op=ALU.add,
                                                 ).then_inc(added[n % 4], 16)

            def body(i, more):
                for g in range(PG):
                    for b in range(2):
                        n = 2 * g + b + RING
                        if n < PT:
                            gather(i, n)
                        elif more:
                            gather(i + 1, n - PT)
                    if g > 0:
                        add(i, g - 1)
                add(i, PG - 1)

            for n in range(RING):
                gather(0, n)
            run(gp, body)
            for n in range(4):
                gp.wait_ge(added[n], 80 * PAIRS)


def build(nc, io):
    attention_phase(nc, io)
    mlp_phase(nc, io)
    routed_phase(nc, io)




def kernel(**inputs):
    import numpy as np
    import concourse.bacc as bacc
    from concourse.bass_utils import run_bass_kernel_spmd

    def plain(a):
        return np.ascontiguousarray(a)

    def columns(v):
        return plain(np.reshape(v, (-1, P)).T)

    def per_partition(w):
        e, k, n = w.shape
        return np.reshape(np.transpose(np.reshape(w, (e, k // P, P, n)), (0, 2, 1, 3)), (e, P, -1))

    a = {k: np.asarray(v) for k, v in inputs.items()}
    x = np.transpose(np.reshape(a["x"], (SEQS, T, DT, P, 4)), (0, 4, 2, 3, 1))
    arrays = {
        "x": plain(x).reshape(SEQS, XK, P, T),
        "wsT": plain(a["L0_tok_weighted_sum"].T),
        "wT": plain(a["L0_tok_weight"].T),
        "wqT": plain(a["L0_attn_wq"].T),
        "wkT": plain(a["L0_attn_wk"].T),
        "wv": plain(a["L0_attn_wv"]),
        "wo": plain(a["L0_attn_wo"]),
        "proj": plain(a["L0_attn_proj"]),
        "g1": columns(a["L0_attn_g1"]),
        "beta1": columns(a["L0_attn_beta1"]),
        "w1": plain(a["L0_attn_w1"]),
        "b1": columns(a["L0_attn_b1"]),
        "w2": plain(a["L0_attn_w2"]),
        "b2": columns(a["L0_attn_b2"]),
        "g2": columns(a["L0_attn_g2"]),
        "beta2": columns(a["L0_attn_beta2"]),
        "gateT": plain(a["L0_ffn_gate_w"].T),
        "shgT": plain(a["L0_ffn_sh_gate_w"][0].T),
        "shuT": plain(a["L0_ffn_sh_up_w"][0].T),
        "shdT": plain(a["L0_ffn_sh_down_w"][0].T),
        "dyn_w": plain(np.concatenate([per_partition(np.transpose(a[n], (0, 2, 1))) for n in (
            "L0_ffn_dyn_gate_w", "L0_ffn_dyn_up_w", "L0_ffn_dyn_down_w")], axis=2)),
    }
    nc = bacc.Bacc("TRN2", target_bir_lowering=False, num_devices=1)
    io, launch = {}, {}
    for name, v in arrays.items():
        launch[f"in_{name}"] = v
        io[name] = nc.dram_tensor(f"in_{name}", list(v.shape), mybir.dt.from_np(v.dtype), kind="ExternalInput").ap()
    io["out"] = nc.dram_tensor("out_rows", [TOKENS + DUMMIES, D], F32, kind="ExternalOutput").ap()
    for name in ("h_dram", "x0_dram", "at_dram"):
        io[name] = nc.dram_tensor(name, [SEQS, DT, P, T], F32, kind="Internal").ap()
    io["xrow_dram"] = nc.dram_tensor("xrow_dram", [TOKENS + DUMMIES, 2 * D], F16, kind="Internal").ap()
    io["list_dram"] = nc.dram_tensor("list_dram", [EXPERTS * SLOTS, 2], U32, kind="Internal").ap()
    build(nc, io)
    r = run_bass_kernel_spmd(nc, [launch], core_ids=[0])
    return np.reshape(r.results[0]["out_rows"][:TOKENS], (SEQS, T, D))
```

```python
import math
from contextlib import ExitStack

import concourse.bass as bass
from concourse import mybir

F32 = mybir.dt.float32
F16 = mybir.dt.float16
U32 = mybir.dt.uint32
ALU = mybir.AluOpType
ACT = mybir.ActivationFunctionType
AX = mybir.AxisListType

P = 128
T = 512
SEQS = 16
D = 256
DT = D // P
XK = 8
HEADS = 16
DH = 64
QT = HEADS * DH // P
VW = DH + 1
CH = 4
EPS = 1e-5
DEN_EPS = 1e-6
HALF = T // 2
XS = XK // 2
FEATS = 8
VALS = 4
FEAT_ORDER = (0, 4, 1, 5, 2, 6, 3, 7)
DENSE = ((("f", 0),), (("p", 0), ("f", 1)), (("f", 2), ("v", 0)), (("f", 3), ("f", 4)), (("v", 1), ("f", 5)),
         (("v", 2), ("f", 6)), (("f", 7),), (("v", 3),))
TURNS = 6 * CH - 2
EXP_LN_SET = 6
EXP_LN_SET = 6

TOK_SCALE = 256.0
V_SCALE = 64.0
WO_SCALE = 64.0
PHI_DOWN = 16.0
QK_SCALE = 1 / PHI_DOWN


def count(i, per, k):
    return i * per + k


def units(u, per, k):
    return count(u[0], 2 * per, u[1] * per + k)


def after(u, n):
    return u[0] + (u[1] + n) // 2, (u[1] + n) % 2


def some(value):
    return type(value) is not int or value > 0


def exp_ln_tables(nc, act):
    act.add_instruction(mybir.InstLoadActFuncSet(name=nc.get_next_instruction_name(), act_func_set_id=EXP_LN_SET))


def causal_mask(nc, gp, mask, made, n):
    gp.memset(mask, 1.0).then_inc(made, 1)
    gp.wait_ge(made, n + 1)
    gp.affine_select(out=mask, in_=mask, compare_op=ALU.is_ge, fill=0.0, base=0,
                     pattern=[[1, P]], channel_multiplier=-1).then_inc(made, 1)


def identity(nc, gp, ident, made, n):
    gp.memset(ident, 0.0).then_inc(made, 1)
    gp.wait_ge(made, n + 1)
    gp.affine_select(out=ident, in_=ident, compare_op=ALU.not_equal, fill=1.0, base=0,
                     pattern=[[-1, P]], channel_multiplier=1).then_inc(made, 1)


def attention_phase(nc, io):
    with ExitStack() as ctx:
        def sb(name, shape, dt=F32):
            return ctx.enter_context(nc.sbuf_tensor(name, [P, *shape], dt))

        def sem(name):
            return ctx.enter_context(nc.semaphore(name))

        tok_h, tok_l = sb("tok_h", [XK, D], F16), sb("tok_l", [XK, D], F16)
        qk_h, qk_l = sb("qk_h", [DT, 2 * QT * P], F16), sb("qk_l", [DT, 2 * QT * P], F16)
        wv_h, wv_l = sb("wv_h", [DT, HEADS * DH], F16), sb("wv_l", [DT, HEADS * DH], F16)
        wo_h, wo_l = sb("wo_h", [QT, D], F16), sb("wo_l", [QT, D], F16)
        ones = sb("ones", [P])
        ident = sb("ident", [P], F16)
        mask = sb("mask", [P])
        block_mask = sb("block_mask", [2, 2, VW])
        g1 = sb("g1", [DT])
        b1 = sb("b1", [DT])

        with ExitStack() as pre:
            def tmp(name, shape, dt=F32):
                return pre.enter_context(nc.sbuf_tensor(name, [P, *shape], dt))

            ws = tmp("ws", [DT, D])
            wd = tmp("wd", [4, D])
            tok_w = tmp("tok_w", [2, D])
            wqkT = tmp("wqkT", [2 * QT, D])
            proj2 = tmp("proj2", [P])
            qk_w = tmp("qk_w", [2, P])
            wv_w = tmp("wv_w", [DT, HEADS * DH])
            wo_w = tmp("wo_w", [QT, D])
            ps = [pre.enter_context(nc.psum_tensor(f"pre_ps{i}", [P, 512], F32)) for i in range(2)]
            loaded = pre.enter_context(nc.semaphore("w_loaded"))
            made = pre.enter_context(nc.semaphore("const_made"))
            zeroed = pre.enter_context(nc.semaphore("proj_zeroed"))
            tok_mul = pre.enter_context(nc.semaphore("tok_mul"))
            tok_hi = pre.enter_context(nc.semaphore("tok_hi"))
            tok_lo = pre.enter_context(nc.semaphore("tok_lo"))
            qk_mm = pre.enter_context(nc.semaphore("qk_mm"))
            qk_hi = pre.enter_context(nc.semaphore("qk_hi"))
            qk_lo = pre.enter_context(nc.semaphore("qk_lo"))
            vo_hi = pre.enter_context(nc.semaphore("vo_hi"))
            proj_loaded = pre.enter_context(nc.semaphore("proj_loaded"))
            with nc.Block() as block:
                @block.sync
                def _(sp):
                    sp.dma_start(ws[:, :, :], io["wsT"].rearrange("(t p) o -> p t o", p=P)).then_inc(loaded, 16)
                    sp.dma_start(wd[:, :, :].rearrange("p d o -> p (d o)"), io["wT"].rearrange("d o -> (d o)").partition_broadcast(P)).then_inc(loaded, 16)
                    sp.dma_start(wv_w[:, :, :], io["wv"].rearrange("(t p) n -> p t n", p=P)).then_inc(loaded, 16)
                    sp.dma_start(wo_w[:, :, :], io["wo"].rearrange("(t p) n -> p t n", p=P)).then_inc(loaded, 16)
                    sp.dma_start(g1[:, :], io["g1"]).then_inc(loaded, 16)
                    sp.dma_start(b1[:, :], io["beta1"]).then_inc(loaded, 16)
                    sp.wait_ge(zeroed, 1)
                    sp.dma_start(proj2[0:DH, 0:DH], io["proj"]).then_inc(proj_loaded, 16)
                    sp.dma_start(proj2[DH:P, DH:P], io["proj"]).then_inc(proj_loaded, 16)
                    sp.wait_ge(loaded, 96)
                    sp.wait_ge(proj_loaded, 64)

                @block.gpsimd
                def _(gp):
                    gp.memset(ones[:, :], 1.0 / D).then_inc(made, 1)
                    identity(nc, gp, ident[:, :], made, 1)
                    causal_mask(nc, gp, mask[:, :], made, 3)
                    gp.memset(block_mask[:, :, :, :], 0.0).then_inc(made, 1)
                    gp.wait_ge(made, 6)
                    gp.memset(block_mask[0:DH, :, 0, :], 1.0).then_inc(made, 1)
                    gp.memset(block_mask[DH:P, :, 1, :], 1.0).then_inc(made, 1)

                @block.tensor
                def _(pe):
                    pe.wait_ge(proj_loaded, 64)
                    for n in range(2 * QT * DT):
                        t, m = n // DT, n % DT
                        if n >= 2:
                            pe.wait_ge(qk_lo, n - 1)
                        pe.matmul(ps[n % 2][:, 0:P], wqkT[:, t, m * P:(m + 1) * P], proj2[:, :],
                                  start=True, stop=True).then_inc(qk_mm, 1)

                @block.scalar
                def _(act):
                    act.dma_start(wqkT[:, 0:QT, :], io["wqT"].rearrange("(t p) n -> p t n", p=P)).then_inc(proj_loaded, 16)
                    act.dma_start(wqkT[:, QT:2 * QT, :], io["wkT"].rearrange("(t p) n -> p t n", p=P)).then_inc(proj_loaded, 16)
                    for k in range(XK):
                        act.wait_ge(tok_mul, k + 1)
                        nc.scalar.activation(tok_h[:, k, :], tok_w[:, k % 2, :], ACT.Copy).then_inc(tok_hi, 1)
                    act.wait_ge(loaded, 96)
                    nc.scalar.activation(wv_h[:, :, :], wv_w[:, :, :], ACT.Copy, scale=V_SCALE).then_inc(vo_hi, 1)
                    nc.scalar.activation(wo_h[:, :, :], wo_w[:, :, :], ACT.Copy, scale=WO_SCALE).then_inc(vo_hi, 1)
                    for n in range(2 * QT * DT):
                        t, m = n // DT, n % DT
                        act.wait_ge(qk_mm, n + 1)
                        nc.scalar.activation(qk_h[:, m, t * P:(t + 1) * P], ps[n % 2][:, 0:P], ACT.Copy,
                                             scale=QK_SCALE).then_inc(qk_hi, 1)

                @block.vector
                def _(ve):
                    ve.memset(proj2[:, :], 0.0).then_inc(zeroed, 1)
                    ve.wait_ge(loaded, 96)
                    for k in range(XK):
                        d, t = k // DT, k % DT
                        if k >= 2:
                            ve.wait_ge(tok_hi, k - 1)
                            ve.wait_ge(tok_lo, k - 1)
                        nc.vector.scalar_tensor_tensor(tok_w[:, k % 2, :], ws[:, t, :], TOK_SCALE, wd[:, d, :],
                                                       ALU.mult, ALU.mult).then_inc(tok_mul, 1)
                        ve.wait_ge(tok_mul, k + 1)
                        ve.wait_ge(tok_hi, k + 1)
                        nc.vector.tensor_tensor(tok_l[:, k, :], tok_w[:, k % 2, :], tok_h[:, k, :],
                                                ALU.subtract).then_inc(tok_lo, 1)
                    ve.wait_ge(vo_hi, 1)
                    nc.vector.scalar_tensor_tensor(wv_l[:, :, :], wv_w[:, :, :], V_SCALE, wv_h[:, :, :],
                                                   ALU.mult, ALU.subtract)
                    ve.wait_ge(vo_hi, 2)
                    nc.vector.scalar_tensor_tensor(wo_l[:, :, :], wo_w[:, :, :], WO_SCALE, wo_h[:, :, :],
                                                   ALU.mult, ALU.subtract)
                    for n in range(2 * QT * DT):
                        t, m = n // DT, n % DT
                        ve.wait_ge(qk_hi, n + 1)
                        nc.vector.scalar_tensor_tensor(qk_l[:, m, t * P:(t + 1) * P], ps[n % 2][:, 0:P], QK_SCALE,
                                                       qk_h[:, m, t * P:(t + 1) * P], ALU.mult,
                                                       ALU.subtract).then_inc(qk_lo, 1)

        xs = sb("xs", [XS, 2, HALF])
        xh, xl = sb("xh", [XS, 2, HALF], F16), sb("xl", [XS, 2, HALF], F16)
        hT = sb("hT", [DT, HALF])
        xc = sb("xc", [DT, HALF])
        sq = sb("sq", [DT, HALF])
        lnt = sb("lnt", [HALF])
        r0 = sb("r0", [HALF])
        r1 = sb("r1", [HALF])
        x0 = sb("x0", [DT, HALF])
        tn = sb("tn", [DT, HALF])
        nh, nl = sb("nh", [DT, T], F16), sb("nl", [DT, T], F16)
        ez, rz, fz = sb("ez", [2, 2, HALF]), sb("rz", [2, 2, HALF]), sb("fz", [2, 2, HALF])
        qkh, qkl = sb("qkh", [2 * QT, T], F16), sb("qkl", [2 * QT, T], F16)
        vh, vl = sb("vh", [CH, HEADS, VW], F16), sb("vl", [CH, HEADS, VW], F16)
        kt = sb("kt", [2, QT, P], F16)
        kvt = sb("kvt", [2, 2, VW])
        kvacc = sb("kvacc", [QT, 2, VW])
        kvh, kvl = sb("kvh", [QT, 2, VW], F16), sb("kvl", [QT, 2, VW], F16)
        sm = sb("sm", [2, 4, P])
        sh, sl = sb("sh", [4, 4, P], F16), sb("sl", [4, 4, P], F16)
        dn, rd = sb("dn", [2, 4]), sb("rd", [2, 4])
        on = sb("on", [2, 4, DH])
        oh, ol = sb("oh", [2, 4 * DH], F16), sb("ol", [2, 4 * DH], F16)
        ot = sb("ot", [2, QT, T], F16)
        at = sb("at", [DT, HALF])

        def bank(name, dt=F32):
            return ctx.enter_context(nc.psum_tensor(name, [P, 2048 // (4 if dt == F32 else 2)], dt))

        pM = bank("pM")
        pF = bank("pF")
        pS = [bank("pS0"), bank("pS1")]
        pO = [bank("pO0"), bank("pO1")]
        pT = bank("pT", F16)
        pKV = bank("pKV")

        x_loaded = [sem(f"x_loaded{i}") for i in range(XS)]
        xh_ready, xl_ready, tok_done = sem("xh_ready"), sem("xl_ready"), sem("tok_done")
        h_ready, mean_done, xc_ready, sq_ready, var_done = (
            sem("h_ready"), sem("mean_done"), sem("xc_ready"), sem("sq_ready"), sem("var_done"))
        rs_step = sem("rs_step")
        x0_ready, tn_ready, nh_ready, nl_ready = sem("x0_ready"), sem("tn_ready"), sem("nh_ready"), sem("nl_ready")
        h_stored, x0_stored = sem("h_stored"), sem("x0_stored")
        qk_done, e_ready, z_read, f_ready, fh_ready, fl_ready = (
            sem("qk_done"), sem("e_ready"), sem("z_read"), sem("f_ready"), sem("fh_ready"), sem("fl_ready"))
        v_done, vh_ready, vl_ready, v_ones = sem("v_done"), sem("vh_ready"), sem("vl_ready"), sem("v_ones")
        s_done, sm_ready, sh_ready, sl_ready = sem("s_done"), sem("sm_ready"), sem("sh_ready"), sem("sl_ready")
        o_done, dn_ready, rd_ready, on_ready, oh_ready, ol_ready = (
            sem("o_done"), sem("dn_ready"), sem("rd_ready"), sem("on_ready"), sem("oh_ready"), sem("ol_ready"))
        turned, turn_read = sem("turned"), sem("turn_read")
        kv_done, kvt_ready, kva_ready, kvh_ready, kvl_ready = (
            sem("kv_done"), sem("kvt_ready"), sem("kva_ready"), sem("kvh_ready"), sem("kvl_ready"))
        at_done, at_ready, at_stored = sem("at_done"), sem("at_ready"), sem("at_stored")

        NKV = 4 * (CH - 1)
        UNITS = 2 * SEQS

        def quad_heads(q):
            return [8 * (q // 2) + q % 2 + 2 * k for k in range(4)]

        def score_place(h):
            return 2 * (h // 8) + h % 2, (h % 8) // 2

        def key_turn(i, c, part):
            return count(i, TURNS, 6 * c + part + 1)

        def output_turn(i, c, g):
            return count(i, TURNS, 6 * c + g + (3 if c < CH - 1 else 1))

        def run(engine, steps):
            def step(name, *args):
                if name in steps:
                    steps[name](*args)

            def use(u, what, before):
                kind, n = what
                if kind == "p":
                    step("project", after(u, -1), before)
                elif kind == "f":
                    step("features", after(u, 1), n, before)
                else:
                    step("values", after(u, 1), n, before)

            def finish(u, what):
                if what[0] == "f":
                    step("phi", after(u, 1), what[1])
                elif what[0] == "p":
                    step("project_read", after(u, -1))

            def norm(u, s):
                if s < XS:
                    step("mix", u, s)
                    if s < XS - 1:
                        step("split", u, s + 1)
                    else:
                        step("h", u)
                elif s == 4:
                    step("mean", u)
                    step("centre", u)
                elif s == 5:
                    step("var", u)
                    step("rstd", u)
                elif s == 6:
                    step("x0", u)
                    step("normed", u)

            def dense(first, last):
                slots, before = [], ("v", VALS - 1)
                for s in range(8):
                    uses = []
                    for what in DENSE[s]:
                        if (what[0] == "p" and first) or (what[0] != "p" and last):
                            continue
                        uses.append((what, before))
                        before = what
                    slots.append(uses)
                return slots

            def unit(u, start=False, mix=True, last=False):
                i, h = u
                slots = dense(start, last)
                if mix:
                    step("split", after(u, 2), 0)
                for s in range(8):
                    c, g = 2 * h + s // 4, s % 4
                    uses = slots[s]
                    if uses:
                        use(u, *uses[0])
                    if g == 0:
                        if not (start and c == 0):
                            step("turn", *((i, c - 1) if c > 0 else (i - 1, CH - 1)), 3)
                        if c > 0:
                            step("sums", i, c - 1, 3)
                    step("outputs", i, c, g)
                    if g == 0 and c < CH - 1:
                        step("keys", i, c, 0)
                    if uses:
                        finish(u, uses[0][0])
                    if g == 0:
                        step("scores", i, c, (2, 3))
                    if g > 0 and c < CH - 1:
                        step("sums", i, c, g - 1)
                    if g == 1 and c < CH - 1:
                        step("keys", i, c, 1)
                    if g == 2 and c < CH - 1:
                        step("scores", i, c + 1, (0, 1))
                    if g == 2 and c == CH - 1 and not last:
                        step("scores", i + 1, 0, (0, 1))
                    step("outputs_split", i, c, g)
                    if len(uses) > 1:
                        use(u, *uses[1])
                    if g == 0:
                        step("scores_split", i, c, (2, 3))
                    if g > 0 and c < CH - 1:
                        step("sums_split", i, c, g - 1)
                    if g == 0 and c > 0:
                        step("sums_split", i, c - 1, 3)
                    if g == 2 and c < CH - 1:
                        step("scores_split", i, c + 1, (0, 1))
                    if g == 2 and c == CH - 1 and not last:
                        step("scores_split", i + 1, 0, (0, 1))
                    if mix:
                        norm(after(u, 2), s)
                    if g > 0:
                        step("turn", i, c, g - 1)
                    if len(uses) > 1:
                        finish(u, uses[1][0])

            step("split", (0, 0), 0)
            for s in range(8):
                norm((0, 0), s)
            step("split", (0, 1), 0)
            slots = dense(True, False)
            for s in range(8):
                for what, before in slots[s]:
                    use((0, -1), what, before)
                    finish((0, -1), what)
                norm((0, 1), s)
            step("scores", 0, 0, (0, 1))
            step("scores_split", 0, 0, (0, 1))
            unit((0, 0), start=True)
            unit((0, 1))
            with engine.Fori(1, SEQS - 1) as i:
                unit((i, 0))
                unit((i, 1))
            unit((SEQS - 1, 0), mix=False)
            unit((SEQS - 1, 1), mix=False, last=True)
            step("turn", SEQS - 1, CH - 1, 3)
            step("project", (SEQS - 1, 1), ("p", 0))
            step("project_read", (SEQS - 1, 1))

        block = ctx.enter_context(nc.Block())

        @block.sync
        def _(sp):
            def load(u, k):
                if some(units(u, XS, k + 1 - XS)):
                    sp.wait_ge(xh_ready, units(u, XS, k + 1 - XS))
                    sp.wait_ge(xl_ready, units(u, XS, k + 1 - XS))
                sp.dma_start(xs[:, k, :, :].rearrange("p a n -> p (a n)"),
                             io["x"].rearrange("(s h) k p n -> s h k p n", h=2)[u[0], u[1], k]).then_inc(x_loaded[k], 16)

            def rows(name, u):
                return io[name][u[0], :, :, u[1] * HALF:(u[1] + 1) * HALF].rearrange("t p n -> p t n")

            def store_rows(u):
                sp.wait_ge(h_ready, units(u, 1, 1))
                sp.dma_start(rows("h_dram", u), hT[:, :, :]).then_inc(h_stored, 16)
                sp.wait_ge(x0_ready, units(u, 1, 1))
                sp.dma_start(rows("x0_dram", u), x0[:, :, :]).then_inc(x0_stored, 16)

            def store_attention(u):
                sp.wait_ge(at_ready, units(u, 1, 1))
                sp.dma_start(rows("at_dram", u), at[:, :, :]).then_inc(at_stored, 16)

            def unit(u, start=False, load_more=True, mix=True):
                if load_more:
                    load(after(u, 3), 0)
                    load(after(u, 3), 1)
                if not start:
                    store_attention(after(u, -1))
                if load_more:
                    load(after(u, 3), 2)
                    load(after(u, 3), 3)
                if mix:
                    store_rows(after(u, 2))

            for u in ((0, 0), (0, 1)):
                for k in range(XS):
                    load(u, k)
            store_rows((0, 0))
            for k in range(XS):
                load((1, 0), k)
            store_rows((0, 1))
            unit((0, 0), start=True)
            unit((0, 1))
            with sp.Fori(1, SEQS - 2) as i:
                unit((i, 0))
                unit((i, 1))
            unit((SEQS - 2, 0))
            unit((SEQS - 2, 1), load_more=False)
            unit((SEQS - 1, 0), load_more=False, mix=False)
            unit((SEQS - 1, 1), load_more=False, mix=False)
            store_attention((SEQS - 1, 1))
            sp.wait_ge(h_stored, 16 * UNITS)
            sp.wait_ge(x0_stored, 16 * UNITS)
            sp.wait_ge(at_stored, 16 * UNITS)

        @block.tensor
        def _(pe):
            def three(out, wh, wl, mh, ml, first, last):
                pe.matmul(out, wh, mh, start=first, stop=False, skip_group_check=True)
                pe.matmul(out, wl, mh, start=False, stop=False, skip_group_check=True)
                return pe.matmul(out, wh, ml, start=False, stop=last, skip_group_check=True)

            def half(u):
                return slice(u[1] * HALF, (u[1] + 1) * HALF)

            def mix(u, k):
                if k == 0 and some(units(u, 5, -4)):
                    pe.wait_ge(rs_step, units(u, 5, -4))
                pe.wait_ge(xh_ready, units(u, XS, k + 1))
                pe.wait_ge(xl_ready, units(u, XS, k + 1))
                for t in range(2):
                    for m in range(DT):
                        cols = slice(m * P, (m + 1) * P)
                        mm = three(pM[:, m * HALF:(m + 1) * HALF], tok_h[:, 2 * k + t, cols], tok_l[:, 2 * k + t, cols],
                                   xh[:, k, t, :], xl[:, k, t, :], k == t == m == 0, k == XS - 1 and t == 1)
                mm.then_inc(tok_done, 1)

            def mean(u):
                pe.wait_ge(h_ready, units(u, 1, 1))
                for t in range(DT):
                    mm = pe.matmul(pM[:, 0:HALF], ones[:, :], hT[:, t, :], start=(t == 0), stop=(t == DT - 1))
                mm.then_inc(mean_done, 1)

            def var(u):
                pe.wait_ge(sq_ready, units(u, 1, 1))
                for t in range(DT):
                    mm = pe.matmul(pM[:, 0:HALF], ones[:, :], sq[:, t, :], start=(t == 0), stop=(t == DT - 1))
                mm.then_inc(var_done, 1)

            def bank_free(w, before):
                kind, n = before
                if kind == "f":
                    pe.wait_ge(f_ready, units(w, FEATS, n + 1))
                elif kind == "p":
                    pe.wait_ge(at_ready, units(w, 1, -1))
                elif n < VALS - 1:
                    pe.wait_ge(vl_ready, units(w, VALS, n + 1))
                elif some(units(w, VALS, 0)):
                    pe.wait_ge(vl_ready, units(w, VALS, 0))

            def features(w, n, before):
                if n == 0:
                    pe.wait_ge(nh_ready, units(w, DT, DT))
                    pe.wait_ge(nl_ready, units(w, DT, DT))
                bank_free(w, before)
                for b in range(2):
                    j = 2 * FEAT_ORDER[n] + b
                    cols = slice(j * P, (j + 1) * P)
                    for t in range(DT):
                        mm = three(pF[:, b * HALF:(b + 1) * HALF], qk_h[:, t, cols], qk_l[:, t, cols],
                                   nh[:, t, half(w)], nl[:, t, half(w)], b == t == 0, t == DT - 1)
                mm.then_inc(qk_done, 1)

            def values(w, n, before):
                bank_free(w, before)
                c = 2 * w[1] + n // 2
                toks, cols = slice(c * P, (c + 1) * P), slice(n % 2 * T, (n % 2 + 1) * T)
                for t in range(DT):
                    mm = three(pF[:, :], nh[:, t, toks], nl[:, t, toks], wv_h[:, t, cols], wv_l[:, t, cols],
                               t == 0, t == DT - 1)
                mm.then_inc(v_done, 1)

            def project(u, before):
                if before[0] == "p":
                    pe.wait_ge(at_ready, units(u, 1, 0))
                else:
                    bank_free(after(u, 2), before)
                pe.wait_ge(turn_read, output_turn(u[0], 2 * u[1] + 1, 3))
                for m in range(DT):
                    cols = slice(m * P, (m + 1) * P)
                    for t in range(QT):
                        mm = three(pF[:, m * HALF:(m + 1) * HALF], wo_h[:, t, cols], wo_l[:, t, cols],
                                   ot[:, 0, t, half(u)], ot[:, 1, t, half(u)], m == t == 0, t == QT - 1)
                mm.then_inc(at_done, 1)

            def scores(i, c, quads):
                toks = slice(c * P, (c + 1) * P)
                pe.wait_ge(fl_ready, units((i, c // 2), FEATS, 4 if quads[0] == 0 else FEATS))
                for q in quads:
                    n = 4 * c + q
                    if some(count(i, 16, n - 1)):
                        pe.wait_ge(sm_ready, count(i, 16, n - 1))
                    for k, h in enumerate(quad_heads(q)):
                        rows = slice(DH * (h % 2), DH * (h % 2) + DH)
                        key, qry = QT + h // 2, h // 2
                        mm = three(pS[n % 2][:, k * P:(k + 1) * P], qkh[rows, key, toks], qkl[rows, key, toks],
                                   qkh[rows, qry, toks], qkl[rows, qry, toks], k == 0, True)
                    mm.then_inc(s_done, 1)

            def keys(i, c, part):
                toks = slice(c * P, (c + 1) * P)
                if part == 1:
                    pe.wait_ge(fl_ready, units((i, c // 2), FEATS, FEATS))
                if some(key_turn(i, c, part) - 1):
                    pe.wait_ge(turn_read, key_turn(i, c, part) - 1)
                for half_no, src in enumerate((qkh, qkl)):
                    for p in range(4):
                        w = 4 * half_no + p
                        mm = pe.transpose(pT[:, w * P:(w + 1) * P], src[:, QT + 4 * part + p, toks], ident[:, :])
                mm.then_inc(turned, 1)

            def outputs(i, c, g):
                n = 4 * c + g
                toks = slice(c * P, (c + 1) * P)
                out = pO[g % 2]
                if some(count(i, 16, n - 1)):
                    pe.wait_ge(on_ready, count(i, 16, n - 1))
                first = True
                if c > 0:
                    pe.wait_ge(kvh_ready, count(i, NKV, 4 * (c - 1) + g + 1))
                    pe.wait_ge(kvl_ready, count(i, NKV, 4 * (c - 1) + g + 1))
                    for k in range(2):
                        p = 2 * g + k
                        mm = three(out[:, 2 * VW * k:2 * VW * (k + 1)], qkh[:, p, toks], qkl[:, p, toks],
                                   kvh[:, p, :, :], kvl[:, p, :, :], first, True)
                        first = False
                if g % 2 == 0:
                    pe.wait_ge(sh_ready, count(i, 16, 4 * c + g + 2))
                    pe.wait_ge(sl_ready, count(i, 16, 4 * c + g + 2))
                if g == 0:
                    if type(i) is int and i == 0 and c == 0:
                        pe.wait_ge(v_ones, 2)
                    pe.wait_ge(vh_ready, count(i, 2 * VALS, 2 * c + 2))
                    pe.wait_ge(vl_ready, count(i, 2 * VALS, 2 * c + 2))
                for k in range(4):
                    h = 4 * g + k
                    q, w = score_place(h)
                    mm = three(out[:, VW * k:VW * (k + 1)], sh[:, q, w, :], sl[:, q, w, :],
                               vh[:, c, h, :], vl[:, c, h, :], first, True)
                    first = False
                mm.then_inc(o_done, 1)

            def sums(i, c, g):
                u = 4 * c + g
                pe.wait_ge(turn_read, key_turn(i, c, g // 2))
                if some(count(i, NKV, u)):
                    pe.wait_ge(kvt_ready, count(i, NKV, u))
                for k in range(2):
                    p = 2 * g + k
                    mm = three(pKV[:, 2 * VW * k:2 * VW * (k + 1)], kt[:, 0, p, :], kt[:, 1, p, :],
                               vh[:, c, 2 * p:2 * p + 2, :], vl[:, c, 2 * p:2 * p + 2, :], k == 0, True)
                mm.then_inc(kv_done, 1)

            def turn(i, c, g):
                n = 4 * c + g
                if some(output_turn(i, c, g) - 1):
                    pe.wait_ge(turn_read, output_turn(i, c, g) - 1)
                pe.wait_ge(oh_ready, count(i, 16, n + 1))
                pe.wait_ge(ol_ready, count(i, 16, n + 1))
                for part, src in enumerate((oh, ol)):
                    for f in range(2):
                        w = 2 * part + f
                        mm = pe.transpose(pT[:, w * P:(w + 1) * P], src[:, n % 2, f * P:(f + 1) * P], ident[:, :])
                mm.then_inc(turned, 1)

            run(pe, dict(mix=mix, mean=mean, var=var, features=features, values=values, scores=scores, keys=keys,
                         outputs=outputs, sums=sums, turn=turn, project=project))

        @block.scalar
        def _(act):
            exp_ln_tables(nc, act)

            def split(u, k):
                act.wait_ge(x_loaded[k], units(u, 16, 16))
                if some(units(u, XS, k + 1 - XS)):
                    act.wait_ge(tok_done, units(u, XS, k + 1 - XS))
                nc.scalar.activation(xh[:, k, :, :], xs[:, k, :, :], ACT.Copy).then_inc(xh_ready, 1)

            def h(u):
                act.wait_ge(tok_done, units(u, XS, XS))
                if some(units(u, 1, 0)):
                    act.wait_ge(h_stored, units(u, 16, 0))
                    act.wait_ge(xc_ready, units(u, 1, 0))
                nc.scalar.activation(hT[:, :, :], pM[:, :].rearrange("p (m n) -> p m n", m=DT), ACT.Copy,
                                     scale=1 / TOK_SCALE).then_inc(h_ready, 1)

            def centre(u):
                act.wait_ge(xc_ready, units(u, 1, 1))
                nc.scalar.activation(sq[:, :, :], xc[:, :, :], ACT.Square).then_inc(sq_ready, 1)

            def rstd(u):
                act.wait_ge(var_done, units(u, 1, 1))
                if some(units(u, DT, 0)):
                    act.wait_ge(tn_ready, units(u, DT, 0))
                nc.scalar.activation(lnt[:, :], pM[:, 0:HALF], ACT.Ln, bias=EPS).then_inc(rs_step, 1)
                act.wait_ge(rs_step, units(u, 5, 1))
                nc.scalar.activation(r0[:, :], lnt[:, :], ACT.Exp, scale=-0.5).then_inc(rs_step, 1)
                act.wait_ge(rs_step, units(u, 5, 2))
                nc.scalar.activation(r1[:, :], r0[:, :], ACT.Square).then_inc(rs_step, 1)
                act.wait_ge(rs_step, units(u, 5, 3))
                nc.scalar.activation(lnt[:, :], r1[:, :], ACT.Ln, scale=-EPS, bias=1.0 + EPS).then_inc(rs_step, 1)
                act.wait_ge(rs_step, units(u, 5, 4))
                nc.scalar.activation(r1[:, :], lnt[:, :], ACT.Exp, scale=-0.5).then_inc(rs_step, 1)

            def normed(u):
                if some(units(u, VALS, -VALS)):
                    act.wait_ge(v_done, units(u, VALS, -VALS))
                for m in range(DT):
                    act.wait_ge(tn_ready, units(u, DT, m + 1))
                    nc.scalar.activation(nh[:, m, u[1] * HALF:(u[1] + 1) * HALF], tn[:, m, :], ACT.Identity,
                                         bias=b1[:, m:m + 1]).then_inc(nh_ready, 1)

            def features(w, n, before):
                s = n % 2
                act.wait_ge(qk_done, units(w, FEATS, n + 1))
                if some(units(w, FEATS, n - 1)):
                    act.wait_ge(e_ready, units(w, FEATS, n - 1))
                nc.scalar.activation(rz[:, s, :, :], pF[:, :].rearrange("p (b n) -> p b n", b=2), ACT.Relu,
                                     scale=-PHI_DOWN).then_inc(z_read, 1)
                act.wait_ge(z_read, units(w, FEATS, n + 1))
                if some(units(w, FEATS, n - 1)):
                    act.wait_ge(f_ready, units(w, FEATS, n - 1))
                nc.scalar.activation(ez[:, s, :, :], rz[:, s, :, :], ACT.Exp, scale=-1.0,
                                     bias=-math.log(PHI_DOWN)).then_inc(e_ready, 1)

            def values(w, n, before):
                c, eight = 2 * w[1] + n // 2, n % 2
                act.wait_ge(v_done, units(w, VALS, n + 1))
                nc.scalar.activation(vh[:, c, 8 * eight:8 * eight + 8, 0:DH],
                                     pF[:, :].rearrange("p (h e) -> p h e", e=DH), ACT.Copy,
                                     scale=1 / V_SCALE).then_inc(vh_ready, 1)

            def scores_split(i, c, quads):
                for q in quads:
                    n = 4 * c + q
                    act.wait_ge(sm_ready, count(i, 16, n + 1))
                    last = count(i, 16, 4 * (c - 1) + (2 if q < 2 else 4))
                    if some(last):
                        act.wait_ge(o_done, last)
                    nc.scalar.activation(sh[:, q, :, :], sm[:, n % 2, :, :], ACT.Copy).then_inc(sh_ready, 1)

            def turn(i, c, g):
                act.wait_ge(turned, output_turn(i, c, g))
                if some(units((i, c // 2), 1, -1)):
                    act.wait_ge(at_done, units((i, c // 2), 1, -1))
                nc.scalar.activation(ot[:, :, 2 * g:2 * g + 2, c * P:(c + 1) * P],
                                     pT[:, 0:4 * P].rearrange("p (a f n) -> p a f n", a=2, f=2),
                                     ACT.Copy).then_inc(turn_read, 1)

            def outputs_split(i, c, g):
                n = 4 * c + g
                act.wait_ge(on_ready, count(i, 16, n + 1))
                if g >= 2:
                    last = output_turn(i, c, g - 2)
                elif c > 0:
                    last = output_turn(i, c - 1, g + 2)
                else:
                    last = count(i, TURNS, g - 1)
                if some(last):
                    act.wait_ge(turned, last)
                nc.scalar.activation(oh[:, n % 2, :], on[:, n % 2, :, :].rearrange("p a b -> p (a b)"),
                                     ACT.Copy).then_inc(oh_ready, 1)

            def sums_split(i, c, g):
                u = 4 * c + g
                act.wait_ge(kva_ready, count(i, NKV, u + 1))
                act.wait_ge(o_done, count(i, 16, u + 1))
                nc.scalar.activation(kvh[:, 2 * g:2 * g + 2, :, :], kvacc[:, 2 * g:2 * g + 2, :, :],
                                     ACT.Copy).then_inc(kvh_ready, 1)

            run(act, dict(split=split, h=h, centre=centre, rstd=rstd, normed=normed, features=features, values=values,
                          scores_split=scores_split, turn=turn, outputs_split=outputs_split,
                          sums_split=sums_split))

        @block.vector
        def _(ve):
            def centre(u):
                ve.wait_ge(mean_done, units(u, 1, 1))
                if some(units(u, 1, 0)):
                    ve.wait_ge(sq_ready, units(u, 1, 0))
                    ve.wait_ge(x0_ready, units(u, 1, 0))
                nc.vector.tensor_tensor(xc[:, :, :], hT[:, :, :],
                                        pM[:, 0:HALF].unsqueeze(1).broadcast_to([P, DT, HALF]),
                                        ALU.subtract).then_inc(xc_ready, 1)

            def x0_rows(u):
                ve.wait_ge(rs_step, units(u, 5, 2))
                ve.wait_ge(xc_ready, units(u, 1, 1))
                if some(units(u, 1, 0)):
                    ve.wait_ge(x0_stored, units(u, 16, 0))
                    ve.wait_ge(tn_ready, units(u, DT, 0))
                nc.vector.tensor_tensor(x0[:, :, :], xc[:, :, :], r0[:, :].unsqueeze(1).broadcast_to([P, DT, HALF]),
                                        ALU.mult).then_inc(x0_ready, 1)

            def normed(u):
                ve.wait_ge(rs_step, units(u, 5, 5))
                ve.wait_ge(x0_ready, units(u, 1, 1))
                if some(units(u, DT, 0)):
                    ve.wait_ge(nh_ready, units(u, DT, 0))
                    ve.wait_ge(nl_ready, units(u, DT, 0))
                for m in range(DT):
                    nc.vector.scalar_tensor_tensor(tn[:, m, :], x0[:, m, :], g1[:, m:m + 1], r1[:, :],
                                                   ALU.mult, ALU.mult).then_inc(tn_ready, 1)
                for m in range(DT):
                    cols = slice(u[1] * HALF, (u[1] + 1) * HALF)
                    ve.wait_ge(tn_ready, units(u, DT, m + 1))
                    ve.wait_ge(nh_ready, units(u, DT, m + 1))
                    nc.vector.scalar_tensor_tensor(nl[:, m, cols], tn[:, m, :], b1[:, m:m + 1], nh[:, m, cols],
                                                   ALU.add, ALU.subtract).then_inc(nl_ready, 1)

            def phi(w, n):
                s = n % 2
                pair = 2 * FEAT_ORDER[n]
                ve.wait_ge(e_ready, units(w, FEATS, n + 1))
                if some(units(w, FEATS, n - 1)):
                    ve.wait_ge(fl_ready, units(w, FEATS, n - 1))
                nc.vector.scalar_tensor_tensor(fz[:, s, :, :], pF[:, :].rearrange("p (b n) -> p b n", b=2), 0.0,
                                               ez[:, s, :, :], ALU.max, ALU.add).then_inc(f_ready, 1)
                ve.wait_ge(f_ready, units(w, FEATS, n + 1))
                nc.vector.tensor_copy(qkh[:, pair:pair + 2, w[1] * HALF:(w[1] + 1) * HALF],
                                      fz[:, s, :, :]).then_inc(fh_ready, 1)

            def values(w, n, before):
                c, heads = 2 * w[1] + n // 2, slice(n % 2 * 8, n % 2 * 8 + 8)
                ve.wait_ge(vh_ready, units(w, VALS, n + 1))
                nc.vector.scalar_tensor_tensor(vl[:, c, heads, 0:DH], pF[:, :].rearrange("p (h e) -> p h e", e=DH),
                                               1 / V_SCALE, vh[:, c, heads, 0:DH],
                                               ALU.mult, ALU.subtract).then_inc(vl_ready, 1)

            def project_read(u):
                ve.wait_ge(at_done, units(u, 1, 1))
                if some(units(u, 1, 0)):
                    ve.wait_ge(at_stored, units(u, 16, 0))
                nc.vector.tensor_scalar(at[:, :, :], pF[:, :].rearrange("p (m n) -> p m n", m=DT), 1 / WO_SCALE, None,
                                        ALU.mult).then_inc(at_ready, 1)

            def scores(i, c, quads):
                for q in quads:
                    n = 4 * c + q
                    ve.wait_ge(s_done, count(i, 16, n + 1))
                    if some(count(i, 16, n - 1)):
                        ve.wait_ge(sh_ready, count(i, 16, n - 1))
                        ve.wait_ge(sl_ready, count(i, 16, n - 1))
                    nc.vector.tensor_tensor(sm[:, n % 2, :, :], pS[n % 2][:, :].rearrange("p (a b) -> p a b", b=P),
                                            mask[:, :].unsqueeze(1).broadcast_to([P, 4, P]),
                                            ALU.mult).then_inc(sm_ready, 1)

            def keys(i, c, part):
                ve.wait_ge(turned, key_turn(i, c, part))
                if some(count(i, NKV, 4 * c - 2 + 2 * part)):
                    ve.wait_ge(kv_done, count(i, NKV, 4 * c - 2 + 2 * part))
                nc.vector.tensor_copy(kt[:, :, 4 * part:4 * part + 4, :],
                                      pT[:, :].rearrange("p (a f n) -> p a f n", a=2, f=4)).then_inc(turn_read, 1)

            def outputs(i, c, g):
                n = 4 * c + g
                s = n % 2
                heads = pO[g % 2][:, 0:4 * VW].rearrange("p (h e) -> p h e", e=VW)
                ve.wait_ge(o_done, count(i, 16, n + 1))
                nc.vector.tensor_scalar(dn[:, s, :], heads[:, :, DH], DEN_EPS / PHI_DOWN ** 2, None,
                                        ALU.add).then_inc(dn_ready, 1)
                ve.wait_ge(dn_ready, count(i, 16, n + 1))
                nc.vector.reciprocal(rd[:, s, :], dn[:, s, :]).then_inc(rd_ready, 1)
                ve.wait_ge(rd_ready, count(i, 16, n + 1))
                if some(count(i, 16, n - 1)):
                    ve.wait_ge(oh_ready, count(i, 16, n - 1))
                    ve.wait_ge(ol_ready, count(i, 16, n - 1))
                nc.vector.tensor_tensor(on[:, s, :, :], heads[:, :, 0:DH],
                                        rd[:, s, :].unsqueeze(2).broadcast_to([P, 4, DH]),
                                        ALU.mult).then_inc(on_ready, 1)

            def sums(i, c, g):
                u = 4 * c + g
                ve.wait_ge(kv_done, count(i, NKV, u + 1))
                pairs = slice(2 * g, 2 * g + 2)
                found = pKV[:, 0:4 * VW].rearrange("p (a b e) -> p a b e", a=2, b=2)
                if c == 0:
                    if some(count(i, NKV, 0)):
                        ve.wait_ge(kvh_ready, count(i, NKV, 0))
                        ve.wait_ge(kvl_ready, count(i, NKV, 0))
                    nc.vector.tensor_tensor(kvt[:, :, :, :], found, block_mask[:, :, :, :],
                                            ALU.mult).then_inc(kvt_ready, 1)
                    ve.wait_ge(kvt_ready, count(i, NKV, u + 1))
                    nc.vector.tensor_copy(kvacc[:, pairs, :, :], kvt[:, :, :, :]).then_inc(kva_ready, 1)
                else:
                    ve.wait_ge(kva_ready, count(i, NKV, u))
                    nc.vector.tensor_tensor(kvt[:, :, :, :], found, block_mask[:, :, :, :],
                                            ALU.mult).then_inc(kvt_ready, 1)
                    ve.wait_ge(kvt_ready, count(i, NKV, u + 1))
                    ve.wait_ge(kvh_ready, count(i, NKV, u - 3))
                    ve.wait_ge(kvl_ready, count(i, NKV, u - 3))
                    nc.vector.tensor_tensor(kvacc[:, pairs, :, :], kvacc[:, pairs, :, :], kvt[:, :, :, :],
                                            ALU.add).then_inc(kva_ready, 1)

            run(ve, dict(centre=centre, x0=x0_rows, normed=normed, phi=phi, values=values, project_read=project_read,
                         scores=scores, keys=keys, outputs=outputs, sums=sums))

        @block.gpsimd
        def _(gp):
            gp.memset(vh[:, :, :, DH:VW], 1.0).then_inc(v_ones, 1)
            gp.memset(vl[:, :, :, DH:VW], 0.0).then_inc(v_ones, 1)

            def split(u, k):
                gp.wait_ge(xh_ready, units(u, XS, k + 1))
                if some(units(u, XS, k + 1 - XS)):
                    gp.wait_ge(tok_done, units(u, XS, k + 1 - XS))
                nc.gpsimd.tensor_tensor(xl[:, k, :, :], xs[:, k, :, :], xh[:, k, :, :], ALU.subtract).then_inc(xl_ready, 1)

            def phi(w, n):
                pair = 2 * FEAT_ORDER[n]
                cols = slice(w[1] * HALF, (w[1] + 1) * HALF)
                gp.wait_ge(fh_ready, units(w, FEATS, n + 1))
                nc.gpsimd.tensor_tensor(qkl[:, pair:pair + 2, cols], fz[:, n % 2, :, :], qkh[:, pair:pair + 2, cols],
                                        ALU.subtract).then_inc(fl_ready, 1)

            def scores_split(i, c, quads):
                for q in quads:
                    n = 4 * c + q
                    gp.wait_ge(sh_ready, count(i, 16, n + 1))
                    nc.gpsimd.tensor_tensor(sl[:, q, :, :], sm[:, n % 2, :, :], sh[:, q, :, :],
                                            ALU.subtract).then_inc(sl_ready, 1)

            def outputs_split(i, c, g):
                n = 4 * c + g
                gp.wait_ge(oh_ready, count(i, 16, n + 1))
                nc.gpsimd.tensor_tensor(ol[:, n % 2, :], on[:, n % 2, :, :].rearrange("p a b -> p (a b)"),
                                        oh[:, n % 2, :], ALU.subtract).then_inc(ol_ready, 1)

            def sums_split(i, c, g):
                u = 4 * c + g
                gp.wait_ge(kvh_ready, count(i, NKV, u + 1))
                pairs = slice(2 * g, 2 * g + 2)
                nc.gpsimd.tensor_tensor(kvl[:, pairs, :, :], kvacc[:, pairs, :, :], kvh[:, pairs, :, :],
                                        ALU.subtract).then_inc(kvl_ready, 1)

            run(gp, dict(split=split, phi=phi, scores_split=scores_split, outputs_split=outputs_split,
                         sums_split=sums_split))


FT = 8
EXPERTS = 8
SLOTS = 1280
TILES = SLOTS // P
TOP = 4
ST = 4
TOKENS = SEQS * T
DUMMIES = P
W1_SCALE = 64.0
W2_SCALE = 64.0
GATE_SCALE = 8.0
SH_SCALE = 16.0
SHD_SCALE = 16.0
FAR = 1.0e6


def mlp_phase(nc, io):
    with ExitStack() as ctx:
        def sb(name, shape, dt=F32):
            return ctx.enter_context(nc.sbuf_tensor(name, [P, *shape], dt))

        def sem(name):
            return ctx.enter_context(nc.semaphore(name))

        w1_h, w1_l = sb("w1_h", [DT, FT * P], F16), sb("w1_l", [DT, FT * P], F16)
        w2_h, w2_l = sb("w2_h", [FT, D], F16), sb("w2_l", [FT, D], F16)
        sg_h, sg_l = sb("sg_h", [DT, 2 * ST * P], F16), sb("sg_l", [DT, 2 * ST * P], F16)
        sd_h, sd_l = sb("sd_h", [ST, D], F16), sb("sd_l", [ST, D], F16)
        gw_h, gw_l = sb("gw_h", [DT, EXPERTS + 1], F16), sb("gw_l", [DT, EXPERTS + 1], F16)
        ones = sb("ones2", [P])
        ones16 = sb("ones16", [P], F16)
        ident = sb("ident2", [P])
        ident16 = sb("ident16", [P], F16)
        upto = sb("upto", [P])
        upto16 = sb("upto16", [P], F16)
        earlier = sb("earlier", [EXPERTS, EXPERTS])
        first_slot = sb("first_slot", [EXPERTS])
        rank_no = sb("rank_no", [TOP, EXPERTS])
        tid = sb("tid", [CH])
        carry = sb("carry", [EXPERTS])
        vecs = sb("vecs", [4, DT])
        b1m = sb("b1m", [FT])
        mb2 = vecs[:, 2, :]
        empty = sb("empty", [EXPERTS * SLOTS // P, 2], U32)
        zrow = sb("zrow", [D])

        with ExitStack() as pre:
            def tmp(name, shape, dt=F32):
                return pre.enter_context(nc.sbuf_tensor(name, [P, *shape], dt))

            w1_w, w2_w = tmp("w1_w", [DT, FT * P]), tmp("w2_w", [FT, D])
            sg_w, sd_w = tmp("sg_w", [DT, 2 * ST * P]), tmp("sd_w", [ST, D])
            gw_w = tmp("gw_w", [DT, EXPERTS + 1])
            dummy_id = tmp("dummy_id", [1])
            loaded = pre.enter_context(nc.semaphore("w2_loaded"))
            hi_ready = pre.enter_context(nc.semaphore("w2_hi"))
            made = pre.enter_context(nc.semaphore("made2"))
            filled = pre.enter_context(nc.semaphore("filled"))
            cleared = pre.enter_context(nc.semaphore("cleared"))
            splits = [(w1_w, w1_h, w1_l, W1_SCALE), (w2_w, w2_h, w2_l, W2_SCALE), (sg_w, sg_h, sg_l, SH_SCALE),
                      (sd_w, sd_h, sd_l, SHD_SCALE), (gw_w, gw_h, gw_l, GATE_SCALE)]
            with nc.Block() as block:
                @block.sync
                def _(sp):
                    sp.dma_start(w1_w[:, :, :], io["w1"].rearrange("(t p) n -> p t n", p=P)).then_inc(loaded, 16)
                    sp.dma_start(w2_w[:, :, :], io["w2"].rearrange("(t p) n -> p t n", p=P)).then_inc(loaded, 16)
                    sp.dma_start(sg_w[:, :, 0:ST * P], io["shgT"].rearrange("(t p) n -> p t n", p=P)).then_inc(loaded, 16)
                    sp.dma_start(sg_w[:, :, ST * P:], io["shuT"].rearrange("(t p) n -> p t n", p=P)).then_inc(loaded, 16)
                    sp.dma_start(sd_w[:, :, :], io["shdT"].rearrange("(t p) n -> p t n", p=P)).then_inc(loaded, 16)
                    sp.dma_start(gw_w[:, :, :], io["gateT"].rearrange("(t p) n -> p t n", p=P)).then_inc(loaded, 16)
                    sp.dma_start(vecs[:, 0, :], io["g2"]).then_inc(loaded, 16)
                    sp.dma_start(vecs[:, 1, :], io["beta2"]).then_inc(loaded, 16)
                    sp.dma_start(vecs[:, 2, :], io["b2"]).then_inc(loaded, 16)
                    sp.dma_start(b1m[:, :], io["b1"]).then_inc(loaded, 16)
                    sp.wait_ge(filled, 1)
                    sp.dma_start(io["out"][TOKENS:TOKENS + DUMMIES, :], zrow[:, :]).then_inc(cleared, 16)
                    sp.dma_start(io["xrow_dram"][TOKENS:TOKENS + DUMMIES, :], zrow[:, :].bitcast(F16)).then_inc(cleared, 16)
                    sp.wait_ge(cleared, 32)
                    sp.wait_ge(loaded, 160)

                @block.gpsimd
                def _(gp):
                    gp.memset(ones[:, :], 1.0 / D).then_inc(made, 1)
                    identity(nc, gp, ident[:, :], made, 1)
                    causal_mask(nc, gp, upto[:, :], made, 3)
                    gp.memset(earlier[:, :, :], 1.0).then_inc(made, 1)
                    gp.wait_ge(made, 6)
                    gp.affine_select(out=earlier[:, :, :], in_=earlier[:, :, :], compare_op=ALU.is_gt, fill=0.0,
                                     base=0, pattern=[[1, EXPERTS], [-1, EXPERTS]],
                                     channel_multiplier=0).then_inc(made, 1)
                    gp.iota(first_slot[:, :], [[SLOTS, EXPERTS]], base=0, channel_multiplier=0,
                            allow_small_or_imprecise_dtypes=True).then_inc(made, 1)
                    gp.iota(rank_no[:, :, :], [[1, TOP], [0, EXPERTS]], base=0, channel_multiplier=0,
                            allow_small_or_imprecise_dtypes=True).then_inc(made, 1)
                    gp.iota(tid[:, :], [[P, CH]], base=0, channel_multiplier=1,
                            allow_small_or_imprecise_dtypes=True).then_inc(made, 1)
                    gp.iota(dummy_id[:, :], [[0, 1]], base=TOKENS, channel_multiplier=1,
                            allow_small_or_imprecise_dtypes=True).then_inc(made, 1)

                @block.vector
                def _(ve):
                    ve.memset(carry[:, :], 0.0)
                    ve.memset(ones16[:, :], 1.0)
                    ve.memset(zrow[:, :], 0.0).then_inc(filled, 1)
                    ve.memset(empty[:, :, :], 0).then_inc(filled, 1)
                    ve.wait_ge(made, 11)
                    ve.wait_ge(filled, 2)
                    nc.vector.tensor_copy(ident16[:, :], ident[:, :])
                    nc.vector.tensor_copy(upto16[:, :], upto[:, :]).then_inc(filled, 1)
                    nc.vector.tensor_copy(empty[:, :, 0],
                                          dummy_id[:, :].broadcast_to([P, EXPERTS * SLOTS // P])).then_inc(filled, 1)
                    ve.wait_ge(loaded, 160)
                    for n, (w, h, l, scale) in enumerate(splits):
                        ve.wait_ge(hi_ready, n + 1)
                        nc.vector.scalar_tensor_tensor(l[:, :, :], w[:, :, :], scale, h[:, :, :],
                                                       ALU.mult, ALU.subtract)

                @block.scalar
                def _(act):
                    act.wait_ge(loaded, 160)
                    for w, h, l, scale in splits:
                        nc.scalar.activation(h[:, :, :], w[:, :, :], ACT.Copy, scale=scale).then_inc(hi_ready, 1)

        x0b, hb_in, atb = sb("x0b", [DT, T]), sb("hb_in", [DT, T]), sb("atb", [DT, T])
        x1, hb, hx = sb("x1", [DT, T]), sb("hb", [DT, T]), sb("hx", [DT, T])
        xc2, sq2, ln2, rs2, tn2 = sb("xc2", [DT, T]), sb("sq2", [DT, T]), sb("ln2", [T]), sb("rs2", [T]), sb("tn2", [DT, T])
        n2h, n2l = sb("n2h", [DT, T], F16), sb("n2l", [DT, T], F16)
        gz = sb("gz", [2, T])
        gh, gl = sb("gh", [FT, T], F16), sb("gl", [FT, T], F16)
        hp = sb("hp", [DT, T])
        xc3, sq3, ln3, rs3, xn = sb("xc3", [DT, T]), sb("sq3", [DT, T]), sb("ln3", [T]), sb("rs3", [T]), sb("xn", [DT, T])
        xnh, xnl = sb("xnh", [DT, T], F16), sb("xnl", [DT, T], F16)
        xt = sb("xt", [CH, 2 * D], F16)
        ht = sb("ht", [CH, D])
        sz, az = sb("sz", [2, T]), sb("az", [2, T])
        ah, al = sb("ah", [ST, T], F16), sb("al", [ST, T], F16)
        ob = sb("ob", [CH, D])
        lg = sb("lg", [CH, EXPERTS + 1])
        pair = [sb(f"pair{i}", [CH * EXPERTS, EXPERTS]) for i in range(5)]
        few = [sb(f"few{i}", [CH, EXPERTS]) for i in range(9)]
        one = [sb(f"one{i}", [CH]) for i in range(6)]
        ml9, e9 = sb("ml9", [CH, EXPERTS + 1]), sb("e9", [CH, EXPERTS + 1])
        rw, m0, rank = sb("rw", [CH, EXPERTS]), sb("m0", [CH, EXPERTS]), sb("rank", [CH, EXPERTS])
        m16 = sb("m16", [CH, EXPERTS], F16)
        w8 = sb("w8", [CH])
        slot_f, w_f = sb("slot_f", [CH, TOP]), sb("w_f", [CH, TOP])
        slot_u = sb("slot_u", [CH, TOP], U32)
        entry = sb("entry", [CH, TOP, 2], U32)

        def bank(name):
            return ctx.enter_context(nc.psum_tensor(name, [P, 512], F32))

        pW = [bank("pW0"), bank("pW1")]
        pY = [bank("pY0"), bank("pY1")]
        pA = [bank("pA0"), bank("pA1")]
        pL = bank("pL")
        cum_at = 64

        (x0_in, h_in, at_in, x1_ready, hb_ready, hx_ready, mean2_done, xc2_ready, sq2_ready, var2_done, rs2_step,
         tn2_ready, n2h_ready, n2l_ready) = [sem(n) for n in (
             "x0_in", "h_in", "at_in", "x1_ready", "hb_ready", "hx_ready", "mean2_done", "xc2_ready", "sq2_ready",
             "var2_done", "rs2_step", "tn2_ready", "n2h_ready", "n2l_ready")]
        (w1_done, gz_ready, gh_ready, gl_ready, w2_done, hp_ready, mean3_done, xc3_ready, sq3_ready, var3_done,
         rs3_step, xn_ready, xnh_ready, xnl_ready) = [sem(n) for n in (
             "w1_done", "gz_ready", "gh_ready", "gl_ready", "w2_done", "hp_ready", "mean3_done", "xc3_ready",
             "sq3_ready", "var3_done", "rs3_step", "xn_ready", "xnh_ready", "xnl_ready")]
        (lg_done, lg_ready, xt_done, xt_ready, xt_stored, ht_done, ht_ready, gu_done, sz_ready, az_ready, ah_ready,
         al_ready, down_done, ob_ready, ob_stored) = [sem(n) for n in (
             "lg_done", "lg_ready", "xt_done", "xt_ready", "xt_stored", "ht_done", "ht_ready", "gu_done", "sz_ready",
             "az_ready", "ah_ready", "al_ready", "down_done", "ob_ready", "ob_stored")]
        (route, route_exp, mask_ready, cum_done, cum_read, routed, list_ready, list_sent, lists_cleared) = [sem(n) for n in (
            "route", "route_exp", "mask_ready", "cum_done", "cum_read", "routed", "list_ready", "list_sent", "lists_cleared")]

        passed = sem("passed2")

        def run(engine, s):
            def body(i, before, after):
                if after:
                    s["mean2"](i + 1)
                s["w1"](i, before)
                if before:
                    s["counts"](i - 1)
                if after:
                    s["var2"](i + 1)
                s["w2"](i)
                s["mean3"](i, before)
                if before:
                    s["gate_up"](i - 1, after)
                s["var3"](i)
                if before:
                    s["down"](i - 1)
                s["logits"](i)
                s["turns"](i, before)

            s["mean2"](0)
            s["var2"](0)
            body(0, False, True)
            body(1, True, True)
            with engine.Fori(2, SEQS - 1) as i:
                body(i, True, True)
            body(SEQS - 1, True, False)
            s["counts"](SEQS - 1)
            s["gate_up"](SEQS - 1, None)
            s["down"](SEQS - 1)

        def at_start(i):
            return type(i) is int and i == 0

        block = ctx.enter_context(nc.Block())

        @block.sync
        def _(sp):
            def load(i):
                if not at_start(i):
                    sp.wait_ge(x1_ready, count(i, DT, 0))
                    sp.wait_ge(hb_ready, count(i, DT, 0))
                for dst, name, arrived in ((x0b, "x0_dram", x0_in), (atb, "at_dram", at_in), (hb_in, "h_dram", h_in)):
                    sp.dma_start(dst[:, :, :], io[name][i].rearrange("t p n -> p t n")).then_inc(arrived, 16)

            def store_rows(i):
                for half in range(2):
                    sp.wait_ge(xt_ready, count(i, 2, half + 1))
                    rows = io["xrow_dram"][0:TOKENS, :].rearrange("(s c p) n -> s p c n", c=CH, p=P)
                    sp.dma_start(rows[i, :, 2 * half:2 * half + 2, :],
                                 xt[:, 2 * half:2 * half + 2, :]).then_inc(xt_stored, 16)

            def store_out(i):
                rows = io["out"][0:TOKENS, :].rearrange("(s c p) n -> s p c n", c=CH, p=P)
                sp.wait_ge(ob_ready, count(i, CH, CH))
                sp.dma_start(rows[i], ob[:, :, :]).then_inc(ob_stored, 16)

            sp.dma_start(io["list_dram"].rearrange("(e p n) w -> p e n w", p=P, n=TILES),
                         empty[:, :, :].rearrange("p (e n) w -> p e n w", n=TILES)).then_inc(lists_cleared, 16)
            load(0)
            load(1)
            load(2)
            store_rows(0)
            load(3)
            store_out(0)
            store_rows(1)
            with sp.Fori(2, SEQS - 2) as i:
                load(i + 2)
                store_out(i - 1)
                store_rows(i)
            store_out(SEQS - 3)
            store_rows(SEQS - 2)
            store_out(SEQS - 2)
            store_rows(SEQS - 1)
            store_out(SEQS - 1)
            sp.wait_ge(xt_stored, 32 * SEQS)
            sp.wait_ge(ob_stored, 16 * SEQS)

        @block.tensor
        def _(pe):
            def three(out, wh, wl, mh, ml, first, last):
                pe.matmul(out, wh, mh, start=first, stop=False, skip_group_check=True)
                pe.matmul(out, wl, mh, start=False, stop=False, skip_group_check=True)
                return pe.matmul(out, wh, ml, start=False, stop=last, skip_group_check=True)

            def mean2(i):
                pe.wait_ge(x1_ready, count(i, DT, DT))
                if not (type(i) is int and i < 2):
                    pe.wait_ge(ht_ready, count(i, 2, -2))
                for t in range(DT):
                    mm = pe.matmul(pA[0][:, :], ones[:, :], x1[:, t, :], start=(t == 0), stop=(t == DT - 1))
                mm.then_inc(mean2_done, 1)

            def var2(i):
                pe.wait_ge(sq2_ready, count(i, DT, DT))
                for t in range(DT):
                    mm = pe.matmul(pA[1][:, :], ones[:, :], sq2[:, t, :], start=(t == 0), stop=(t == DT - 1))
                mm.then_inc(var2_done, 1)

            def w1(i, before):
                pe.wait_ge(n2h_ready, count(i, DT, DT))
                pe.wait_ge(n2l_ready, count(i, DT, DT))
                for j in range(FT):
                    if j >= 2:
                        pe.wait_ge(gz_ready, count(i, FT, j - 1))
                    elif not (type(i) is int and i < 2):
                        pe.wait_ge(az_ready, count(i, ST, -ST))
                    cols = slice(j * P, (j + 1) * P)
                    for t in range(DT):
                        mm = three(pW[j % 2][:, :], w1_h[:, t, cols], w1_l[:, t, cols], n2h[:, t, :], n2l[:, t, :],
                                   t == 0, t == DT - 1)
                    mm.then_inc(w1_done, 1)

            def w2(i):
                if not (type(i) is int and i < 2):
                    pe.wait_ge(ob_ready, count(i, CH, -CH))
                for j in range(FT):
                    pe.wait_ge(gh_ready, count(i, FT, j + 1))
                    pe.wait_ge(gl_ready, count(i, FT, j + 1))
                    for m in range(DT):
                        cols = slice(m * P, (m + 1) * P)
                        mm = three(pY[m][:, :], w2_h[:, j, cols], w2_l[:, j, cols], gh[:, j, :], gl[:, j, :],
                                   j == 0, j == FT - 1)
                mm.then_inc(w2_done, 1)

            def mean3(i, before):
                pe.wait_ge(hp_ready, count(i, DT, DT))
                if before:
                    pe.wait_ge(cum_read, count(i, 1, 0))
                for t in range(DT):
                    mm = pe.matmul(pL[:, :], ones[:, :], hp[:, t, :], start=(t == 0), stop=(t == DT - 1))
                mm.then_inc(mean3_done, 1)

            def gate_up(i, after):
                for j in range(ST):
                    g, u = (pW[0], pW[1]) if j % 2 == 0 else (pA[0], pA[1])
                    if j >= 2:
                        pe.wait_ge(az_ready, count(i, ST, j - 1))
                    elif j == 0 and after is not None:
                        pe.wait_ge(gz_ready, count(i + 1, FT, FT))
                    elif j == 0:
                        pe.wait_ge(gz_ready, FT * SEQS)
                    elif after:
                        pe.wait_ge(xc2_ready, count(i + 2, DT, DT))
                        pe.wait_ge(rs2_step, count(i + 2, 2, 1))
                    else:
                        pe.wait_ge(ht_ready, count(i, 2, 2))
                    for out, base in ((g, 0), (u, ST * P)):
                        cols = slice(base + j * P, base + (j + 1) * P)
                        for t in range(DT):
                            mm = three(out[:, :], sg_h[:, t, cols], sg_l[:, t, cols], xnh[:, t, :], xnl[:, t, :],
                                       t == 0, t == DT - 1)
                        mm.then_inc(gu_done, 1)

            def var3(i):
                pe.wait_ge(sq3_ready, count(i, DT, DT))
                pe.wait_ge(xc3_ready, count(i, DT, DT))
                for t in range(DT):
                    mm = pe.matmul(pL[:, :], ones[:, :], sq3[:, t, :], start=(t == 0), stop=(t == DT - 1))
                mm.then_inc(var3_done, 1)

            def down(i):
                for c in range(CH):
                    if c >= 2:
                        pe.wait_ge(ob_ready, count(i, CH, c - 1))
                    elif c == 0:
                        pe.wait_ge(hp_ready, DT * SEQS if type(i) is int and i == SEQS - 1 else count(i + 1, DT, DT))
                        pe.wait_ge(ah_ready, count(i, ST, ST))
                        pe.wait_ge(al_ready, count(i, ST, ST))
                    toks = slice(c * P, (c + 1) * P)
                    for k in range(ST):
                        mm = three(pY[c % 2][:, 0:D], ah[:, k, toks], al[:, k, toks], sd_h[:, k, :], sd_l[:, k, :],
                                   k == 0, k == ST - 1)
                    mm.then_inc(down_done, 1)

            def logits(i):
                pe.wait_ge(rs3_step, count(i, 2, 1))
                pe.wait_ge(xnh_ready, count(i, DT, DT))
                pe.wait_ge(xnl_ready, count(i, DT, DT))
                n = EXPERTS + 1
                for c in range(CH):
                    toks = slice(c * P, (c + 1) * P)
                    for t in range(DT):
                        mm = three(pL[:, c * n:(c + 1) * n], xnh[:, t, toks], xnl[:, t, toks], gw_h[:, t, :],
                                   gw_l[:, t, :], c == 0 and t == 0, t == DT - 1)
                mm.then_inc(lg_done, 1)

            def turns(i, before):
                for half in range(2):
                    if half == 0:
                        if before:
                            pe.wait_ge(az_ready, count(i, ST, 0))
                        else:
                            pe.wait_ge(xc2_ready, count(i + 1, DT, DT))
                            pe.wait_ge(rs2_step, count(i + 1, 2, 1))
                    bank16 = pA[half][:, :].bitcast(F16)
                    for c in range(2):
                        toks = slice((2 * half + c) * P, (2 * half + c + 1) * P)
                        for part, src in enumerate((xnh, xnl)):
                            for t in range(DT):
                                w = (c * 2 + part) * DT + t
                                mm = pe.transpose(bank16[:, w * P:(w + 1) * P], src[:, t, toks], ident16[:, :])
                    mm.then_inc(xt_done, 1)
                for half in range(2):
                    pe.wait_ge(xt_ready, count(i, 2, half + 1))
                    for c in range(2):
                        toks = slice((2 * half + c) * P, (2 * half + c + 1) * P)
                        for t in range(DT):
                            w = c * DT + t
                            mm = pe.transpose(pA[half][:, w * P:(w + 1) * P], hp[:, t, toks], ident[:, :])
                    mm.then_inc(ht_done, 1)

            def counts(i):
                pe.wait_ge(mask_ready, count(i, 1, 1))
                pe.wait_ge(lg_ready, count(i, 1, 1))
                first = True
                for c in range(CH + 1):
                    out = pL[:, cum_at + c * EXPERTS:cum_at + (c + 1) * EXPERTS]
                    for before in range(c):
                        mm = pe.matmul(out, ones16[:, :], m16[:, before, :], start=first, stop=before == CH - 1,
                                       skip_group_check=True)
                        first = False
                    if c < CH:
                        mm = pe.matmul(out, upto16[:, :], m16[:, c, :], start=first, stop=True, skip_group_check=True)
                        first = False
                mm.then_inc(cum_done, 1)

            run(pe, dict(mean2=mean2, var2=var2, w1=w1, w2=w2, mean3=mean3, gate_up=gate_up, var3=var3, down=down,
                         logits=logits, turns=turns, counts=counts))

        @block.scalar
        def _(act):
            def mean2(i):
                act.wait_ge(h_in, count(i, 16, 16))
                if not at_start(i):
                    act.wait_ge(hx_ready, count(i, DT, 0))
                for m in range(DT):
                    nc.scalar.activation(hb[:, m, :], hb_in[:, m, :], ACT.Identity,
                                         bias=vecs[:, 2, m:m + 1]).then_inc(hb_ready, 1)
                for m in range(DT):
                    act.wait_ge(xc2_ready, count(i, DT, m + 1))
                    nc.scalar.activation(sq2[:, m, :], xc2[:, m, :], ACT.Square).then_inc(sq2_ready, 1)

            def var2(i):
                act.wait_ge(var2_done, count(i, 1, 1))
                if type(i) is int and i < 2:
                    exp_ln_tables(nc, act)
                nc.scalar.activation(ln2[:, :], pA[1][:, :], ACT.Ln, bias=EPS).then_inc(rs2_step, 1)
                act.wait_ge(rs2_step, count(i, 2, 1))
                if not at_start(i):
                    act.wait_ge(tn2_ready, count(i, DT, 0))
                nc.scalar.activation(rs2[:, :], ln2[:, :], ACT.Exp, scale=-0.5).then_inc(rs2_step, 1)
                for m in range(DT):
                    act.wait_ge(tn2_ready, count(i, DT, m + 1))
                    if not at_start(i):
                        act.wait_ge(w1_done, count(i, FT, 0))
                    nc.scalar.activation(n2h[:, m, :], tn2[:, m, :], ACT.Identity,
                                         bias=vecs[:, 1, m:m + 1]).then_inc(n2h_ready, 1)

            def w1(i, before):
                for j in range(FT):
                    act.wait_ge(w1_done, count(i, FT, j + 1))
                    if j >= 2 or not at_start(i):
                        act.wait_ge(gl_ready, count(i, FT, j - 1))
                    nc.scalar.activation(gz[:, j % 2, :], pW[j % 2][:, :], ACT.Gelu, scale=1 / W1_SCALE,
                                         bias=b1m[:, j:j + 1]).then_inc(gz_ready, 1)

            def mean3(i, before):
                for m in range(DT):
                    act.wait_ge(xc3_ready, count(i, DT, m + 1))
                    nc.scalar.activation(sq3[:, m, :], xc3[:, m, :], ACT.Square).then_inc(sq3_ready, 1)

            def gate_up(i, after):
                for j in range(ST):
                    g = pW[0] if j % 2 == 0 else pA[0]
                    act.wait_ge(gu_done, count(i, 2 * ST, 2 * j + 1))
                    if j >= 2 or not at_start(i):
                        act.wait_ge(az_ready, count(i, ST, j - 1))
                    nc.scalar.activation(sz[:, j % 2, :], g[:, :], ACT.Silu, scale=1 / SH_SCALE).then_inc(sz_ready, 1)

            def var3(i):
                exp_ln_tables(nc, act)
                act.wait_ge(var3_done, count(i, 1, 1))
                nc.scalar.activation(ln3[:, :], pL[:, :], ACT.Ln, bias=EPS).then_inc(rs3_step, 1)
                act.wait_ge(rs3_step, count(i, 2, 1))
                if not at_start(i):
                    act.wait_ge(xn_ready, count(i, DT, 0))
                nc.scalar.activation(rs3[:, :], ln3[:, :], ACT.Exp, scale=-0.5).then_inc(rs3_step, 1)

            def logits(i):
                act.wait_ge(lg_done, count(i, 1, 1))
                if not at_start(i):
                    act.wait_ge(routed, count(i, 1, 0))
                nc.scalar.activation(lg[:, :, :], pL[:, 0:CH * (EXPERTS + 1)].rearrange("p (c e) -> p c e", c=CH),
                                     ACT.Copy, scale=1 / GATE_SCALE).then_inc(lg_ready, 1)
                act.wait_ge(route, count(i, ROUTE_STEPS, EXP1_AFTER))
                nc.scalar.activation(few[1][:, :, :], few[0][:, :, :], ACT.Exp).then_inc(route_exp, 1)

            def turns(i, before):
                for half in range(2):
                    act.wait_ge(xt_done, count(i, 2, half + 1))
                    if not at_start(i):
                        act.wait_ge(xt_stored, count(i, 32, 0))
                    nc.scalar.activation(xt[:, 2 * half:2 * half + 2, :],
                                         pA[half][:, :].bitcast(F16).rearrange("p (c n) -> p c n", c=2),
                                         ACT.Copy).then_inc(xt_ready, 1)
                for half in range(2):
                    act.wait_ge(ht_done, count(i, 2, half + 1))
                    if not at_start(i):
                        act.wait_ge(ob_ready, count(i, CH, 0))
                    nc.scalar.activation(ht[:, 2 * half:2 * half + 2, :],
                                         pA[half][:, :].rearrange("p (c n) -> p c n", c=2), ACT.Copy).then_inc(ht_ready, 1)

            def counts(i):
                exp_ln_tables(nc, act)
                act.wait_ge(route, count(i, ROUTE_STEPS, EXP2_AFTER))
                nc.scalar.activation(e9[:, :, :], ml9[:, :, :], ACT.Exp).then_inc(route_exp, 1)

            def nothing(i, *rest):
                pass

            run(act, dict(mean2=mean2, var2=var2, w1=w1, w2=nothing, mean3=mean3, gate_up=gate_up, var3=var3,
                          down=nothing, logits=logits, turns=turns, counts=counts))

        @block.vector
        def _(ve):
            def mean2(i):
                ve.wait_ge(mean2_done, count(i, 1, 1))
                if not at_start(i):
                    ve.wait_ge(tn2_ready, count(i, DT, 0))
                for m in range(DT):
                    nc.vector.tensor_tensor(xc2[:, m, :], x1[:, m, :], pA[0][:, :], ALU.subtract).then_inc(xc2_ready, 1)

            def var2(i):
                ve.wait_ge(rs2_step, count(i, 2, 2))
                ve.wait_ge(xc2_ready, count(i, DT, DT))
                if not at_start(i):
                    ve.wait_ge(n2h_ready, count(i, DT, 0))
                    ve.wait_ge(n2l_ready, count(i, DT, 0))
                for m in range(DT):
                    nc.vector.scalar_tensor_tensor(tn2[:, m, :], xc2[:, m, :], vecs[:, 0, m:m + 1], rs2[:, :],
                                                   ALU.mult, ALU.mult).then_inc(tn2_ready, 1)
                for m in range(DT):
                    ve.wait_ge(tn2_ready, count(i, DT, m + 1))
                    ve.wait_ge(n2h_ready, count(i, DT, m + 1))
                    nc.vector.scalar_tensor_tensor(n2l[:, m, :], tn2[:, m, :], vecs[:, 1, m:m + 1], n2h[:, m, :],
                                                   ALU.add, ALU.subtract).then_inc(n2l_ready, 1)

            def w1(i, before):
                if not at_start(i):
                    ve.wait_ge(w2_done, count(i, 1, 0))
                for j in range(FT):
                    ve.wait_ge(gz_ready, count(i, FT, j + 1))
                    nc.vector.tensor_copy(gh[:, j, :], gz[:, j % 2, :]).then_inc(gh_ready, 1)

            def w2(i):
                ve.wait_ge(w2_done, count(i, 1, 1))
                ve.wait_ge(hx_ready, count(i, DT, DT))
                if not at_start(i):
                    ve.wait_ge(ht_done, count(i, 2, 0))
                for m in range(DT):
                    nc.vector.scalar_tensor_tensor(hp[:, m, :], pY[m][:, :], 1 / W2_SCALE, hx[:, m, :],
                                                   ALU.mult, ALU.add).then_inc(hp_ready, 1)

            def mean3(i, before):
                ve.wait_ge(mean3_done, count(i, 1, 1))
                ve.wait_ge(hp_ready, count(i, DT, DT))
                for m in range(DT):
                    nc.vector.tensor_tensor(xc3[:, m, :], hp[:, m, :], pL[:, :], ALU.subtract).then_inc(xc3_ready, 1)

            def gate_up(i, after):
                for j in range(ST):
                    u = pW[1] if j % 2 == 0 else pA[1]
                    ve.wait_ge(gu_done, count(i, 2 * ST, 2 * j + 2))
                    ve.wait_ge(sz_ready, count(i, ST, j + 1))
                    if j >= 2 or not at_start(i):
                        ve.wait_ge(al_ready, count(i, ST, j - 1))
                    nc.vector.scalar_tensor_tensor(az[:, j % 2, :], u[:, :], 1 / SH_SCALE, sz[:, j % 2, :],
                                                   ALU.mult, ALU.mult).then_inc(az_ready, 1)
                    ve.wait_ge(az_ready, count(i, ST, j + 1))
                    if not at_start(i):
                        ve.wait_ge(down_done, count(i, CH, 0))
                    nc.vector.tensor_copy(ah[:, j, :], az[:, j % 2, :]).then_inc(ah_ready, 1)

            def var3(i):
                ve.wait_ge(rs3_step, count(i, 2, 2))
                ve.wait_ge(xc3_ready, count(i, DT, DT))
                if not at_start(i):
                    ve.wait_ge(xnl_ready, count(i, DT, 0))
                    ve.wait_ge(xt_done, count(i, 2, 0))
                    ve.wait_ge(gu_done, count(i, 2 * ST, 0))
                for m in range(DT):
                    nc.vector.tensor_tensor(xn[:, m, :], xc3[:, m, :], rs3[:, :], ALU.mult).then_inc(xn_ready, 1)
                for m in range(DT):
                    ve.wait_ge(xn_ready, count(i, DT, m + 1))
                    nc.vector.tensor_copy(xnh[:, m, :], xn[:, m, :]).then_inc(xnh_ready, 1)

            def down(i):
                ve.wait_ge(routed, count(i, 1, 1))
                ve.wait_ge(ht_ready, count(i, 2, 2))
                if not at_start(i):
                    ve.wait_ge(ob_stored, count(i, 16, 0))
                for c in range(CH):
                    ve.wait_ge(down_done, count(i, CH, c + 1))
                    nc.vector.scalar_tensor_tensor(ob[:, c, :], pY[c % 2][:, 0:D], w8[:, c:c + 1], ht[:, c, :],
                                                   ALU.mult, ALU.add).then_inc(ob_ready, 1)

            def flat(t):
                return t[:, :, :].rearrange("p c e -> p (c e)")

            def routing(i, lo, hi):
                E = EXPERTS
                state = [0]

                def link(make):
                    state[0] += 1
                    if lo < state[0] <= hi:
                        make().then_inc(route, 1)
                        ve.wait_ge(route, count(i, ROUTE_STEPS, state[0]))

                def wait(sem_, per, k):
                    if lo <= state[0] < hi:
                        ve.wait_ge(sem_, count(i, per, k))

                V = nc.vector
                mine = lg[:, :, 0:E].unsqueeze(3).broadcast_to([P, CH, E, E])
                other = lg[:, :, 0:E].unsqueeze(2).broadcast_to([P, CH, E, E])

                def cube(t):
                    return t[:, :, :].rearrange("p (c e) f -> p c e f", c=CH)

                def over_mine(t):
                    return t[:, :, :].unsqueeze(2).broadcast_to([P, CH, E, E])

                def per_chunk(t):
                    return t[:, :].unsqueeze(2).broadcast_to([P, CH, E])

                before, scr, near, a, b = pair
                lead, ex, cprev, su, mu, mf, t1, t2, gd = few
                mx, z, zq, s1, r1_, zd = one
                link(lambda: V.tensor_reduce(mx[:, :], lg[:, :, 0:E], AX.X, ALU.max))
                link(lambda: V.tensor_tensor(lead[:, :, :], lg[:, :, 0:E], per_chunk(mx), ALU.subtract))
                link(lambda: V.tensor_tensor(cube(scr), other, mine, ALU.is_equal))
                link(lambda: V.tensor_tensor(cube(scr), cube(scr),
                                             earlier[:, :, :].unsqueeze(1).broadcast_to([P, CH, E, E]), ALU.mult))
                link(lambda: V.tensor_tensor(cube(before), other, mine, ALU.is_gt))
                link(lambda: V.tensor_tensor(before[:, :, :], before[:, :, :], scr[:, :, :], ALU.add))
                link(lambda: V.tensor_reduce(flat(rank), before[:, :, :], AX.X, ALU.add))
                link(lambda: V.scalar_tensor_tensor(mu[:, :, :], lg[:, :, 0:E], -1.0, lg[:, :, 0:E], ALU.mult, ALU.max))
                link(lambda: V.tensor_tensor(cube(a), over_mine(mu),
                                             mu[:, :, :].unsqueeze(3).broadcast_to([P, CH, E, E]), ALU.max))
                link(lambda: V.tensor_tensor(cube(b), mine, other, ALU.subtract))
                link(lambda: V.scalar_tensor_tensor(near[:, :, :], a[:, :, :], 0.2, b[:, :, :], ALU.mult, ALU.is_ge))
                link(lambda: V.scalar_tensor_tensor(near[:, :, :], before[:, :, :], 0.5, near[:, :, :],
                                                    ALU.is_lt, ALU.mult))
                wait(route_exp, 2, 1)
                link(lambda: V.tensor_tensor(cube(a), cube(near), over_mine(ex), ALU.mult))
                link(lambda: V.tensor_reduce(flat(su), a[:, :, :], AX.X, ALU.add))
                link(lambda: V.tensor_scalar(su[:, :, :], su[:, :, :], 1e-37, None, ALU.max))
                link(lambda: V.reciprocal(t1[:, :, :], su[:, :, :]))
                link(lambda: V.tensor_tensor(mu[:, :, :], ex[:, :, :], t1[:, :, :], ALU.mult))
                link(lambda: V.tensor_tensor(cube(b), cube(before), over_mine(ex), ALU.mult))
                link(lambda: V.tensor_reduce(flat(cprev), b[:, :, :], AX.X, ALU.add))
                link(lambda: V.tensor_reduce(z[:, :], ex[:, :, :], AX.X, ALU.add))
                link(lambda: V.tensor_scalar(zq[:, :], z[:, :], 0.75, None, ALU.mult))
                link(lambda: V.tensor_tensor(t2[:, :, :], cprev[:, :, :], per_chunk(zq), ALU.is_lt))
                link(lambda: V.scalar_tensor_tensor(t2[:, :, :], rank[:, :, :], TOP - 0.5, t2[:, :, :],
                                                    ALU.is_lt, ALU.mult))
                link(lambda: V.tensor_tensor(rw[:, :, :], mu[:, :, :], t2[:, :, :], ALU.mult))
                link(lambda: V.tensor_reduce(s1[:, :], rw[:, :, :], AX.X, ALU.add))
                link(lambda: V.reciprocal(r1_[:, :], s1[:, :]))
                link(lambda: V.tensor_tensor(rw[:, :, :], rw[:, :, :], per_chunk(r1_), ALU.mult))
                link(lambda: V.tensor_scalar(m0[:, :, :], rw[:, :, :], 0.0, None, ALU.is_gt))
                assert state[0] == MASK_AFTER
                if lo < MASK_AFTER <= hi:
                    V.tensor_copy(m16[:, :, :], m0[:, :, :]).then_inc(mask_ready, 1)
                wait(cum_done, 1, 1)
                link(lambda: V.tensor_tensor(t1[:, :, :], pL[:, cum_at:cum_at + CH * E].rearrange("p (c e) -> p c e", c=CH),
                                             carry[:, :].unsqueeze(1).broadcast_to([P, CH, E]), ALU.add))
                link(lambda: V.tensor_tensor(carry[:, :], carry[:, :], pL[:, cum_at + CH * E:cum_at + (CH + 1) * E], ALU.add))
                if lo < state[0] <= hi:
                    V.scalar_tensor_tensor(mf[:, :, :], t1[:, :, :], SLOTS + 0.5, m0[:, :, :],
                                           ALU.is_lt, ALU.mult).then_inc(cum_read, 1)
                    ve.wait_ge(cum_read, count(i, 1, 1))
                link(lambda: V.tensor_scalar(t2[:, :, :], mf[:, :, :], 1.0, 1e30, ALU.subtract, ALU.mult))
                link(lambda: V.tensor_tensor(ml9[:, :, 0:E], lg[:, :, 0:E], mf[:, :, :], ALU.mult))
                link(lambda: V.tensor_tensor(ml9[:, :, 0:E], ml9[:, :, 0:E], t2[:, :, :], ALU.add))
                link(lambda: V.tensor_copy(ml9[:, :, E], lg[:, :, E]))
                link(lambda: V.tensor_reduce(mx[:, :], ml9[:, :, :], AX.X, ALU.max))
                link(lambda: V.tensor_tensor(ml9[:, :, :], ml9[:, :, :], mx[:, :].unsqueeze(2).broadcast_to([P, CH, E + 1]),
                                             ALU.subtract))
                assert state[0] == EXP2_AFTER
                link(lambda: V.tensor_tensor(t1[:, :, :], t1[:, :, :],
                                             first_slot[:, :].unsqueeze(1).broadcast_to([P, CH, E]), ALU.add))
                link(lambda: V.tensor_tensor(t1[:, :, :], t1[:, :, :], mf[:, :, :], ALU.mult))
                wait(route_exp, 2, 2)
                link(lambda: V.tensor_reduce(zd[:, :], e9[:, :, 0:E], AX.X, ALU.add))
                link(lambda: V.tensor_tensor(z[:, :], zd[:, :], e9[:, :, E], ALU.add))
                link(lambda: V.reciprocal(zq[:, :], z[:, :]))
                link(lambda: V.scalar_tensor_tensor(w8[:, :], e9[:, :, E], 1 / SHD_SCALE, zq[:, :], ALU.mult, ALU.mult))
                link(lambda: V.tensor_tensor(s1[:, :], zd[:, :], zq[:, :], ALU.mult))
                link(lambda: V.tensor_tensor(gd[:, :, :], rw[:, :, :], per_chunk(s1), ALU.mult))
                link(lambda: V.tensor_tensor(gd[:, :, :], gd[:, :, :], mf[:, :, :], ALU.mult))
                by_rank = a[:, 0:CH * TOP, :].rearrange("p (c k) e -> p c k e", c=CH)
                picked = b[:, 0:CH * TOP, :].rearrange("p (c k) e -> p c k e", c=CH)

                def over_ranks(t):
                    return t[:, :, :].unsqueeze(2).broadcast_to([P, CH, TOP, E])

                link(lambda: V.tensor_tensor(by_rank, over_ranks(rank),
                                             rank_no[:, :, :].unsqueeze(1).broadcast_to([P, CH, TOP, E]), ALU.is_equal))
                link(lambda: V.tensor_tensor(picked, by_rank, over_ranks(t1), ALU.mult))
                link(lambda: V.tensor_reduce(flat(slot_f), b[:, 0:CH * TOP, :], AX.X, ALU.add))
                link(lambda: V.tensor_tensor(picked, by_rank, over_ranks(gd), ALU.mult))
                if lo <= state[0] < hi and not at_start(i):
                    ve.wait_ge(list_sent, count(i, 16 * CH * TOP, 0))
                link(lambda: V.tensor_reduce(w_f[:, :, :].rearrange("p c k -> p (c k)"), b[:, 0:CH * TOP, :], AX.X, ALU.add))
                link(lambda: V.tensor_copy(entry[:, :, :, 1].bitcast(F32), w_f[:, :, :]))
                link(lambda: V.tensor_copy(entry[:, :, :, 0], tid[:, :].unsqueeze(2).broadcast_to([P, CH, TOP])))
                link(lambda: V.tensor_scalar(tid[:, :], tid[:, :], float(T), None, ALU.add))
                link(lambda: V.tensor_scalar(w_f[:, :, :], slot_f[:, :, :], 0.0, FAR, ALU.is_equal, ALU.mult))
                if hi == ROUTE_STEPS:
                    V.scalar_tensor_tensor(slot_u[:, :, :], slot_f[:, :, :], -1.0, w_f[:, :, :],
                                           ALU.add, ALU.add).then_inc(routed, 1)
                assert state[0] == ROUTE_STEPS, state

            def logits(i):
                ve.wait_ge(lg_ready, count(i, 1, 1))
                routing(i, 0, MASK_AFTER)

            def counts(i):
                routing(i, MASK_AFTER, ROUTE_STEPS)

            def nothing(i, *rest):
                pass

            run(ve, dict(mean2=mean2, var2=var2, w1=w1, w2=w2, mean3=mean3, gate_up=gate_up, var3=var3, down=down,
                         logits=logits, turns=nothing, counts=counts))

        @block.gpsimd
        def _(gp):
            def mean2(i):
                gp.wait_ge(x0_in, count(i, 16, 16))
                gp.wait_ge(at_in, count(i, 16, 16))
                if not at_start(i):
                    gp.wait_ge(xc2_ready, count(i, DT, 0))
                    gp.wait_ge(mean2_done, count(i, 1, 0))
                    gp.wait_ge(hx_ready, count(i, DT, 0))
                for m in range(DT):
                    nc.gpsimd.tensor_tensor(x1[:, m, :], x0b[:, m, :], atb[:, m, :], ALU.add).then_inc(x1_ready, 1)

            def w1(i, before):
                for j in range(FT):
                    gp.wait_ge(gh_ready, count(i, FT, j + 1))
                    nc.gpsimd.tensor_tensor(gl[:, j, :], gz[:, j % 2, :], gh[:, j, :], ALU.subtract).then_inc(gl_ready, 1)

            def sums(i):
                gp.wait_ge(hb_ready, count(i, DT, DT))
                gp.wait_ge(x1_ready, count(i, DT, DT))
                if not at_start(i):
                    gp.wait_ge(hp_ready, count(i, DT, 0))
                for m in range(DT):
                    nc.gpsimd.tensor_tensor(hx[:, m, :], hb[:, m, :], x1[:, m, :], ALU.add).then_inc(hx_ready, 1)

            def gate_up(i, after):
                for j in range(ST):
                    gp.wait_ge(ah_ready, count(i, ST, j + 1))
                    nc.gpsimd.tensor_tensor(al[:, j, :], az[:, j % 2, :], ah[:, j, :], ALU.subtract).then_inc(al_ready, 1)

            def var3(i):
                for m in range(DT):
                    gp.wait_ge(xnh_ready, count(i, DT, m + 1))
                    nc.gpsimd.tensor_tensor(xnl[:, m, :], xn[:, m, :], xnh[:, m, :], ALU.subtract).then_inc(xnl_ready, 1)

            def send(i):
                gp.wait_ge(lists_cleared, 16)
                gp.wait_ge(routed, count(i, 1, 1))
                gp.sem_inc(passed, 1)
                for c in range(CH):
                    for k in range(TOP):
                        nc.gpsimd.indirect_dma_start(
                            io["list_dram"], bass.IndirectOffsetOnAxis(slot_u[:, c, k:k + 1], 0), entry[:, c, k, :],
                            None, bounds_check=EXPERTS * SLOTS - 1, oob_is_err=False).then_inc(list_sent, 16)

            def nothing(i, *rest):
                pass

            def mean3(i, before):
                if type(i) is int and i == SEQS - 1:
                    return
                sums(i + 1)

            def var2(i):
                if at_start(i):
                    sums(0)

            def counts(i):
                pass

            def down(i):
                send(i)

            run(gp, dict(mean2=mean2, var2=var2, w1=w1, w2=nothing, mean3=mean3, gate_up=gate_up, var3=var3,
                         down=down, logits=nothing, turns=nothing, counts=counts))
            gp.wait_ge(list_sent, 16 * CH * TOP * SEQS)


ROUTE_STEPS = 54
EXP1_AFTER = 2
MASK_AFTER = 28
EXP2_AFTER = 36
DYN_SCALE = 8.0
WCOLS = 2 * DT * P + D
GROUPS = TILES // 2
PG = 2 * GROUPS
PT = 2 * TILES
RING = 10


def routed_phase(nc, io):
    with ExitStack() as ctx:
        def sb(name, shape, dt=F32):
            return ctx.enter_context(nc.sbuf_tensor(name, [P, *shape], dt))

        def sem(name):
            return ctx.enter_context(nc.semaphore(name))

        def bank(name):
            return ctx.enter_context(nc.psum_tensor(name, [P, 512], F32))

        ident = sb("ident3", [P], F16)
        wf = sb("wf", [2, WCOLS])
        wh, wl = sb("wh", [2, WCOLS], F16), sb("wl", [2, WCOLS], F16)
        gid = sb("gid", [TILES * 2, 2], U32)
        sid = sb("sid", [TILES * 2, 2], U32)
        lw = sb("lw", [TILES * 2])
        xg = sb("xg", [RING, 2 * D], F16)
        xf = sb("xf", [2, 2 * DT, 2 * P], F16)
        sz, az = sb("sz3", [2, 2 * P]), sb("az3", [2, 2 * P])
        ah, al = sb("ah3", [2, 2 * P], F16), sb("al3", [2, 2 * P], F16)
        yb = sb("yb", [4, D])
        pT = [bank("pT3a"), bank("pT3b")]
        pG = [bank("pG3a"), bank("pG3b")]
        pD = [bank("pD3a"), bank("pD3b")]

        made, gid_in, sid_in, lw_ready = sem("made3"), sem("gid_in"), sem("sid_in"), sem("lw_ready")
        w_in = [sem("w_in0"), sem("w_in1")]
        wh_ready, wl_ready = sem("wh_ready"), sem("wl_ready")
        gathered = [sem(f"gathered{n}") for n in range(RING)]
        t_done, xf_ready, gu_done = sem("t_done"), sem("xf_ready"), sem("gu_done3")
        sz_ready, az_ready, ah_ready, al_ready = sem("sz_ready3"), sem("az_ready3"), sem("ah_ready3"), sem("al_ready3")
        d_done, y_ready = sem("d_done"), sem("y_ready")
        added = [sem(f"added{n}") for n in range(4)]
        passed = sem("passed")
        PAIRS = EXPERTS // 2
        lists = io["list_dram"].rearrange("(e two p n) w -> e p two n w", two=2, p=P, n=TILES)

        def at_start(i):
            return type(i) is int and i == 0

        def run(engine, body):
            body(0, True)
            with engine.Fori(1, PAIRS - 1) as i:
                body(i, True)
            body(PAIRS - 1, False)

        block = ctx.enter_context(nc.Block())

        @block.sync
        def _(sp):
            def gather_list(i):
                if not at_start(i):
                    for n in range(RING):
                        sp.wait_ge(gathered[n], count(i, 32, 0))
                sp.dma_start(gid[:, :, :].rearrange("p (two n) w -> p two n w", two=2), lists[i]).then_inc(gid_in, 16)

            def scatter_list(i):
                if not at_start(i):
                    for n in range(4):
                        sp.wait_ge(added[n], count(i, 80, 0))
                    sp.wait_ge(lw_ready, count(i, 1, 0))
                sp.dma_start(sid[:, :, :].rearrange("p (two n) w -> p two n w", two=2), lists[i]).then_inc(sid_in, 16)

            def weights(i, s):
                if not at_start(i):
                    sp.wait_ge(wl_ready, count(i, 2, s - 1))
                pairs = io["dyn_w"].rearrange("(e two) p n -> e two p n", two=2)
                sp.dma_start(wf[:, s, :], pairs[i, s]).then_inc(w_in[s], 16)

            def body(i, more):
                if more:
                    weights(i + 1, 0)
                    gather_list(i + 1)
                    weights(i + 1, 1)
                    scatter_list(i + 1)

            gather_list(0)
            weights(0, 0)
            weights(0, 1)
            scatter_list(0)
            run(sp, body)

        @block.tensor
        def _(pe):
            def three(out, wh_, wl_, mh, ml, first, last):
                pe.matmul(out, wh_, mh, start=first, stop=False, skip_group_check=True)
                pe.matmul(out, wl_, mh, start=False, stop=False, skip_group_check=True)
                return pe.matmul(out, wh_, ml, start=False, stop=last, skip_group_check=True)

            def turn(i, g):
                if g >= 2 or not at_start(i):
                    pe.wait_ge(xf_ready, count(i, PG, g - 1))
                out = pT[g % 2][:, :].bitcast(F16)
                for b in range(2):
                    slot = (2 * g + b) % RING
                    pe.wait_ge(gathered[slot], count(i, 32, 16 * ((2 * g + b) // RING + 1)))
                    for w in range(2 * DT):
                        at = w * 2 * P + b * P
                        mm = pe.transpose(out[:, at:at + P], xg[:, slot, w * P:(w + 1) * P], ident[:, :])
                mm.then_inc(t_done, 1)

            def gate_up(i, g):
                e = g // GROUPS
                if g % GROUPS == 0:
                    pe.wait_ge(wh_ready, count(i, 2, e + 1))
                    pe.wait_ge(wl_ready, count(i, 2, e + 1))
                pe.wait_ge(xf_ready, count(i, PG, g + 1))
                if g >= 2 or not at_start(i):
                    pe.wait_ge(az_ready, count(i, PG, g - 1))
                for half in range(2):
                    for t in range(DT):
                        at = (half * DT + t) * P
                        mm = three(pG[g % 2][:, half * 2 * P:(half + 1) * 2 * P], wh[:, e, at:at + P], wl[:, e, at:at + P],
                                   xf[:, g % 2, t, :], xf[:, g % 2, DT + t, :], half == 0 and t == 0, t == DT - 1)
                mm.then_inc(gu_done, 1)

            def down(i, g):
                e = g // GROUPS
                pe.wait_ge(ah_ready, count(i, PG, g + 1))
                pe.wait_ge(al_ready, count(i, PG, g + 1))
                if g >= 2 or not at_start(i):
                    pe.wait_ge(y_ready, count(i, PT, 2 * (g - 1)))
                cols = slice(2 * DT * P, WCOLS)
                for b in range(2):
                    toks = slice(b * P, (b + 1) * P)
                    mm = three(pD[g % 2][:, b * D:(b + 1) * D], ah[:, g % 2, toks], al[:, g % 2, toks],
                               wh[:, e, cols], wl[:, e, cols], b == 0, True)
                mm.then_inc(d_done, 1)

            def body(i, more):
                turn(i, 0)
                for g in range(PG):
                    if g + 1 < PG:
                        turn(i, g + 1)
                    gate_up(i, g)
                    if g > 0:
                        down(i, g - 1)
                down(i, PG - 1)

            pe.wait_ge(made, 2)
            run(pe, body)

        @block.scalar
        def _(act):
            def split(i, e):
                act.wait_ge(w_in[e], count(i, 16, 16))
                if not at_start(i):
                    act.wait_ge(d_done, count(i, PG, (e - 1) * GROUPS))
                nc.scalar.activation(wh[:, e, :], wf[:, e, :], ACT.Copy, scale=DYN_SCALE).then_inc(wh_ready, 1)

            def silu(i, g):
                act.wait_ge(gu_done, count(i, PG, g + 1))
                if g >= 2 or not at_start(i):
                    act.wait_ge(az_ready, count(i, PG, g - 1))
                nc.scalar.activation(sz[:, g % 2, :], pG[g % 2][:, 0:2 * P], ACT.Silu,
                                     scale=1 / DYN_SCALE).then_inc(sz_ready, 1)

            def weigh(i, g):
                act.wait_ge(d_done, count(i, PG, g + 1))
                if g == 0:
                    act.wait_ge(lw_ready, count(i, 1, 1))
                for b in range(2):
                    n = 2 * g + b
                    if n >= 4 or not at_start(i):
                        act.wait_ge(added[n % 4], count(i, 80, 16 * (n // 4)))
                    nc.scalar.activation(yb[:, n % 4, :], pD[g % 2][:, b * D:(b + 1) * D], ACT.Copy,
                                         scale=lw[:, n:n + 1]).then_inc(y_ready, 1)

            def body(i, more):
                for g in range(PG):
                    if g == 1:
                        split(i, 1)
                    if g == GROUPS + 1 and more:
                        split(i + 1, 0)
                    silu(i, g)
                    if g > 0:
                        weigh(i, g - 1)
                weigh(i, PG - 1)

            split(0, 0)
            run(act, body)

        @block.vector
        def _(ve):
            def split(i, e):
                ve.wait_ge(wh_ready, count(i, 2, e + 1))
                nc.vector.scalar_tensor_tensor(wl[:, e, :], wf[:, e, :], DYN_SCALE, wh[:, e, :],
                                               ALU.mult, ALU.subtract).then_inc(wl_ready, 1)

            def weights_of_list(i):
                ve.wait_ge(sid_in, count(i, 16, 16))
                if not at_start(i):
                    ve.wait_ge(y_ready, count(i, PT, 0))
                nc.vector.tensor_scalar(lw[:, :], sid[:, :, 1].bitcast(F32), 1 / DYN_SCALE, None,
                                        ALU.mult).then_inc(lw_ready, 1)

            def features(i, g):
                ve.wait_ge(t_done, count(i, PG, g + 1))
                if g >= 2 or not at_start(i):
                    ve.wait_ge(gu_done, count(i, PG, g - 1))
                nc.vector.tensor_copy(xf[:, g % 2, :, :], pT[g % 2][:, :].bitcast(F16).rearrange(
                    "p (w n) -> p w n", n=2 * P)).then_inc(xf_ready, 1)

            def hidden(i, g):
                s = g % 2
                ve.wait_ge(sz_ready, count(i, PG, g + 1))
                nc.vector.scalar_tensor_tensor(az[:, s, :], pG[s][:, 2 * P:], 1 / DYN_SCALE, sz[:, s, :],
                                               ALU.mult, ALU.mult).then_inc(az_ready, 1)
                ve.wait_ge(az_ready, count(i, PG, g + 1))
                if g >= 2 or not at_start(i):
                    ve.wait_ge(d_done, count(i, PG, g - 1))
                nc.vector.tensor_copy(ah[:, s, :], az[:, s, :]).then_inc(ah_ready, 1)
                ve.wait_ge(ah_ready, count(i, PG, g + 1))
                nc.vector.tensor_tensor(al[:, s, :], az[:, s, :], ah[:, s, :], ALU.subtract).then_inc(al_ready, 1)

            def body(i, more):
                features(i, 0)
                weights_of_list(i)
                for g in range(PG):
                    if g + 1 < PG:
                        features(i, g + 1)
                    if g == 1:
                        split(i, 1)
                    if g == GROUPS + 1 and more:
                        split(i + 1, 0)
                    hidden(i, g)

            split(0, 0)
            run(ve, body)

        @block.gpsimd
        def _(gp):
            identity(nc, gp, ident[:, :], made, 0)

            def gather(i, n):
                if n == 0:
                    gp.wait_ge(gid_in, count(i, 16, 16))
                if n >= RING or not at_start(i):
                    gp.wait_ge(t_done, count(i, PG, (n - RING) // 2 + 1))
                gp.sem_inc(passed, 1)
                nc.gpsimd.indirect_dma_start(xg[:, n % RING, :], None, io["xrow_dram"],
                                             bass.IndirectOffsetOnAxis(gid[:, n, 0:1], 0)).then_inc(gathered[n % RING], 16)

            def add(i, g):
                for b in range(2):
                    n = 2 * g + b
                    gp.wait_ge(y_ready, count(i, PT, n + 1))
                    if n % TILES == 0 and (n > 0 or not at_start(i)):
                        for s in range(4):
                            done = len([m for m in range(n) if m % 4 == s])
                            gp.wait_ge(added[s], count(i, 80, 16 * done))
                    gp.sem_inc(passed, 1)
                    nc.gpsimd.indirect_dma_start(io["out"], bass.IndirectOffsetOnAxis(sid[:, n, 0:1], 0),
                                                 yb[:, n % 4, :], None, compute_op=ALU.add,
                                                 ).then_inc(added[n % 4], 16)

            def body(i, more):
                for g in range(PG):
                    for b in range(2):
                        n = 2 * g + b + RING
                        if n < PT:
                            gather(i, n)
                        elif more:
                            gather(i + 1, n - PT)
                    if g > 0:
                        add(i, g - 1)
                add(i, PG - 1)

            for n in range(RING):
                gather(0, n)
            run(gp, body)
            for n in range(4):
                gp.wait_ge(added[n], 80 * PAIRS)


def build(nc, io):
    attention_phase(nc, io)
    mlp_phase(nc, io)
    routed_phase(nc, io)




def kernel(**inputs):
    import numpy as np
    import concourse.bacc as bacc
    from concourse.bass_utils import run_bass_kernel_spmd

    def plain(a):
        return np.ascontiguousarray(a)

    def columns(v):
        return plain(np.reshape(v, (-1, P)).T)

    def per_partition(w):
        e, k, n = w.shape
        return np.reshape(np.transpose(np.reshape(w, (e, k // P, P, n)), (0, 2, 1, 3)), (e, P, -1))

    a = {k: np.asarray(v) for k, v in inputs.items()}
    x = np.transpose(np.reshape(a["x"], (2 * SEQS, HALF, DT, P, 4)), (0, 4, 3, 2, 1))
    arrays = {
        "x": plain(x).reshape(2 * SEQS, XS, P, DT * HALF),
        "wsT": plain(a["L0_tok_weighted_sum"].T),
        "wT": plain(a["L0_tok_weight"].T),
        "wqT": plain(a["L0_attn_wq"].T),
        "wkT": plain(a["L0_attn_wk"].T),
        "wv": plain(a["L0_attn_wv"]),
        "wo": plain(a["L0_attn_wo"]),
        "proj": plain(a["L0_attn_proj"]),
        "g1": columns(a["L0_attn_g1"]),
        "beta1": columns(a["L0_attn_beta1"]),
        "w1": plain(a["L0_attn_w1"]),
        "b1": columns(a["L0_attn_b1"]),
        "w2": plain(a["L0_attn_w2"]),
        "b2": columns(a["L0_attn_b2"]),
        "g2": columns(a["L0_attn_g2"]),
        "beta2": columns(a["L0_attn_beta2"]),
        "gateT": plain(a["L0_ffn_gate_w"].T),
        "shgT": plain(a["L0_ffn_sh_gate_w"][0].T),
        "shuT": plain(a["L0_ffn_sh_up_w"][0].T),
        "shdT": plain(a["L0_ffn_sh_down_w"][0].T),
        "dyn_w": plain(np.concatenate([per_partition(np.transpose(a[n], (0, 2, 1))) for n in (
            "L0_ffn_dyn_gate_w", "L0_ffn_dyn_up_w", "L0_ffn_dyn_down_w")], axis=2)),
    }
    nc = bacc.Bacc("TRN2", target_bir_lowering=False, num_devices=1)
    io, launch = {}, {}
    for name, v in arrays.items():
        launch[f"in_{name}"] = v
        io[name] = nc.dram_tensor(f"in_{name}", list(v.shape), mybir.dt.from_np(v.dtype), kind="ExternalInput").ap()
    io["out"] = nc.dram_tensor("out_rows", [TOKENS + DUMMIES, D], F32, kind="ExternalOutput").ap()
    for name in ("h_dram", "x0_dram", "at_dram"):
        io[name] = nc.dram_tensor(name, [SEQS, DT, P, T], F32, kind="Internal").ap()
    io["xrow_dram"] = nc.dram_tensor("xrow_dram", [TOKENS + DUMMIES, 2 * D], F16, kind="Internal").ap()
    io["list_dram"] = nc.dram_tensor("list_dram", [EXPERTS * SLOTS, 2], U32, kind="Internal").ap()
    build(nc, io)
    r = run_bass_kernel_spmd(nc, [launch], core_ids=[0])
    return np.reshape(r.results[0]["out_rows"][:TOKENS], (SEQS, T, D))
```

```python
import math
from contextlib import ExitStack

import concourse.bass as bass
from concourse import mybir

F32 = mybir.dt.float32
F16 = mybir.dt.float16
U32 = mybir.dt.uint32
ALU = mybir.AluOpType
ACT = mybir.ActivationFunctionType
AX = mybir.AxisListType

P = 128
T = 512
SEQS = 16
D = 256
DT = D // P
XK = 8
HEADS = 16
DH = 64
QT = HEADS * DH // P
VW = DH + 1
CH = 4
EPS = 1e-5
DEN_EPS = 1e-6
HALF = T // 2
XS = XK // 2
FEATS = 8
VALS = 4
FEAT_ORDER = (0, 4, 1, 5, 2, 6, 3, 7)
DENSE = ((("f", 0),), (("f", 1), ("p", 0)), (("f", 2), ("v", 0)), (("f", 3), ("f", 4)), (("v", 1), ("f", 5)),
         (("v", 2), ("f", 6)), (("f", 7),), (("v", 3),))
OUT_BANK = 0
TURNS = 6 * CH - 2
EXP_LN_SET = 6
EXP_LN_SET = 6

TOK_SCALE = 256.0
V_SCALE = 64.0
WO_SCALE = 64.0
PHI_DOWN = 16.0
QK_SCALE = 1 / PHI_DOWN


def count(i, per, k):
    return i * per + k


def units(u, per, k):
    return count(u[0], 2 * per, u[1] * per + k)


def after(u, n):
    return u[0] + (u[1] + n) // 2, (u[1] + n) % 2


def some(value):
    return type(value) is not int or value > 0


def exp_ln_tables(nc, act):
    act.add_instruction(mybir.InstLoadActFuncSet(name=nc.get_next_instruction_name(), act_func_set_id=EXP_LN_SET))


def causal_mask(nc, gp, mask, made, n):
    gp.memset(mask, 1.0).then_inc(made, 1)
    gp.wait_ge(made, n + 1)
    gp.affine_select(out=mask, in_=mask, compare_op=ALU.is_ge, fill=0.0, base=0,
                     pattern=[[1, P]], channel_multiplier=-1).then_inc(made, 1)


def identity(nc, gp, ident, made, n):
    gp.memset(ident, 0.0).then_inc(made, 1)
    gp.wait_ge(made, n + 1)
    gp.affine_select(out=ident, in_=ident, compare_op=ALU.not_equal, fill=1.0, base=0,
                     pattern=[[-1, P]], channel_multiplier=1).then_inc(made, 1)


def attention_phase(nc, io):
    with ExitStack() as ctx:
        def sb(name, shape, dt=F32):
            return ctx.enter_context(nc.sbuf_tensor(name, [P, *shape], dt))

        def sem(name):
            return ctx.enter_context(nc.semaphore(name))

        tok_h, tok_l = sb("tok_h", [XK, D], F16), sb("tok_l", [XK, D], F16)
        qk_h, qk_l = sb("qk_h", [DT, 2 * QT * P], F16), sb("qk_l", [DT, 2 * QT * P], F16)
        wv_h, wv_l = sb("wv_h", [DT, HEADS * DH], F16), sb("wv_l", [DT, HEADS * DH], F16)
        wo_h, wo_l = sb("wo_h", [QT, D], F16), sb("wo_l", [QT, D], F16)
        ones = sb("ones", [P])
        ident = sb("ident", [P], F16)
        mask = sb("mask", [P])
        block_mask = sb("block_mask", [2, 2, VW])
        g1 = sb("g1", [DT])
        b1 = sb("b1", [DT])

        with ExitStack() as pre:
            def tmp(name, shape, dt=F32):
                return pre.enter_context(nc.sbuf_tensor(name, [P, *shape], dt))

            ws = tmp("ws", [DT, D])
            wd = tmp("wd", [4, D])
            tok_w = tmp("tok_w", [2, D])
            wqkT = tmp("wqkT", [2 * QT, D])
            proj2 = tmp("proj2", [P])
            qk_w = tmp("qk_w", [2, P])
            wv_w = tmp("wv_w", [DT, HEADS * DH])
            wo_w = tmp("wo_w", [QT, D])
            ps = [pre.enter_context(nc.psum_tensor(f"pre_ps{i}", [P, 512], F32)) for i in range(2)]
            loaded = pre.enter_context(nc.semaphore("w_loaded"))
            made = pre.enter_context(nc.semaphore("const_made"))
            zeroed = pre.enter_context(nc.semaphore("proj_zeroed"))
            tok_mul = pre.enter_context(nc.semaphore("tok_mul"))
            tok_hi = pre.enter_context(nc.semaphore("tok_hi"))
            tok_lo = pre.enter_context(nc.semaphore("tok_lo"))
            qk_mm = pre.enter_context(nc.semaphore("qk_mm"))
            qk_hi = pre.enter_context(nc.semaphore("qk_hi"))
            qk_lo = pre.enter_context(nc.semaphore("qk_lo"))
            vo_hi = pre.enter_context(nc.semaphore("vo_hi"))
            proj_loaded = pre.enter_context(nc.semaphore("proj_loaded"))
            with nc.Block() as block:
                @block.sync
                def _(sp):
                    sp.dma_start(ws[:, :, :], io["wsT"].rearrange("(t p) o -> p t o", p=P)).then_inc(loaded, 16)
                    sp.dma_start(wd[:, :, :].rearrange("p d o -> p (d o)"), io["wT"].rearrange("d o -> (d o)").partition_broadcast(P)).then_inc(loaded, 16)
                    sp.dma_start(wv_w[:, :, :], io["wv"].rearrange("(t p) n -> p t n", p=P)).then_inc(loaded, 16)
                    sp.dma_start(wo_w[:, :, :], io["wo"].rearrange("(t p) n -> p t n", p=P)).then_inc(loaded, 16)
                    sp.dma_start(g1[:, :], io["g1"]).then_inc(loaded, 16)
                    sp.dma_start(b1[:, :], io["beta1"]).then_inc(loaded, 16)
                    sp.wait_ge(zeroed, 1)
                    sp.dma_start(proj2[0:DH, 0:DH], io["proj"]).then_inc(proj_loaded, 16)
                    sp.dma_start(proj2[DH:P, DH:P], io["proj"]).then_inc(proj_loaded, 16)
                    sp.wait_ge(loaded, 96)
                    sp.wait_ge(proj_loaded, 64)

                @block.gpsimd
                def _(gp):
                    gp.memset(ones[:, :], 1.0 / D).then_inc(made, 1)
                    identity(nc, gp, ident[:, :], made, 1)
                    causal_mask(nc, gp, mask[:, :], made, 3)
                    gp.memset(block_mask[:, :, :, :], 0.0).then_inc(made, 1)
                    gp.wait_ge(made, 6)
                    gp.memset(block_mask[0:DH, :, 0, :], 1.0).then_inc(made, 1)
                    gp.memset(block_mask[DH:P, :, 1, :], 1.0).then_inc(made, 1)

                @block.tensor
                def _(pe):
                    pe.wait_ge(proj_loaded, 64)
                    for n in range(2 * QT * DT):
                        t, m = n // DT, n % DT
                        if n >= 2:
                            pe.wait_ge(qk_lo, n - 1)
                        pe.matmul(ps[n % 2][:, 0:P], wqkT[:, t, m * P:(m + 1) * P], proj2[:, :],
                                  start=True, stop=True).then_inc(qk_mm, 1)

                @block.scalar
                def _(act):
                    act.dma_start(wqkT[:, 0:QT, :], io["wqT"].rearrange("(t p) n -> p t n", p=P)).then_inc(proj_loaded, 16)
                    act.dma_start(wqkT[:, QT:2 * QT, :], io["wkT"].rearrange("(t p) n -> p t n", p=P)).then_inc(proj_loaded, 16)
                    for k in range(XK):
                        act.wait_ge(tok_mul, k + 1)
                        nc.scalar.activation(tok_h[:, k, :], tok_w[:, k % 2, :], ACT.Copy).then_inc(tok_hi, 1)
                    act.wait_ge(loaded, 96)
                    nc.scalar.activation(wv_h[:, :, :], wv_w[:, :, :], ACT.Copy, scale=V_SCALE).then_inc(vo_hi, 1)
                    nc.scalar.activation(wo_h[:, :, :], wo_w[:, :, :], ACT.Copy, scale=WO_SCALE).then_inc(vo_hi, 1)
                    for n in range(2 * QT * DT):
                        t, m = n // DT, n % DT
                        act.wait_ge(qk_mm, n + 1)
                        nc.scalar.activation(qk_h[:, m, t * P:(t + 1) * P], ps[n % 2][:, 0:P], ACT.Copy,
                                             scale=QK_SCALE).then_inc(qk_hi, 1)

                @block.vector
                def _(ve):
                    ve.memset(proj2[:, :], 0.0).then_inc(zeroed, 1)
                    ve.wait_ge(loaded, 96)
                    for k in range(XK):
                        d, t = k // DT, k % DT
                        if k >= 2:
                            ve.wait_ge(tok_hi, k - 1)
                            ve.wait_ge(tok_lo, k - 1)
                        nc.vector.scalar_tensor_tensor(tok_w[:, k % 2, :], ws[:, t, :], TOK_SCALE, wd[:, d, :],
                                                       ALU.mult, ALU.mult).then_inc(tok_mul, 1)
                        ve.wait_ge(tok_mul, k + 1)
                        ve.wait_ge(tok_hi, k + 1)
                        nc.vector.tensor_tensor(tok_l[:, k, :], tok_w[:, k % 2, :], tok_h[:, k, :],
                                                ALU.subtract).then_inc(tok_lo, 1)
                    ve.wait_ge(vo_hi, 1)
                    nc.vector.scalar_tensor_tensor(wv_l[:, :, :], wv_w[:, :, :], V_SCALE, wv_h[:, :, :],
                                                   ALU.mult, ALU.subtract)
                    ve.wait_ge(vo_hi, 2)
                    nc.vector.scalar_tensor_tensor(wo_l[:, :, :], wo_w[:, :, :], WO_SCALE, wo_h[:, :, :],
                                                   ALU.mult, ALU.subtract)
                    for n in range(2 * QT * DT):
                        t, m = n // DT, n % DT
                        ve.wait_ge(qk_hi, n + 1)
                        nc.vector.scalar_tensor_tensor(qk_l[:, m, t * P:(t + 1) * P], ps[n % 2][:, 0:P], QK_SCALE,
                                                       qk_h[:, m, t * P:(t + 1) * P], ALU.mult,
                                                       ALU.subtract).then_inc(qk_lo, 1)

        xs = sb("xs", [XS, 2, HALF])
        xh, xl = sb("xh", [XS, 2, HALF], F16), sb("xl", [XS, 2, HALF], F16)
        hT = sb("hT", [DT, HALF])
        xc = sb("xc", [DT, HALF])
        sq = sb("sq", [DT, HALF])
        lnt = sb("lnt", [HALF])
        r0 = sb("r0", [HALF])
        r1 = sb("r1", [HALF])
        x0 = sb("x0", [DT, HALF])
        tn = sb("tn", [DT, HALF])
        nh, nl = sb("nh", [DT, T], F16), sb("nl", [DT, T], F16)
        ez, rz, fz = sb("ez", [2, 2, HALF]), sb("rz", [2, 2, HALF]), sb("fz", [2, 2, HALF])
        qkh, qkl = sb("qkh", [2 * QT, T], F16), sb("qkl", [2 * QT, T], F16)
        vh, vl = sb("vh", [CH, HEADS, VW], F16), sb("vl", [CH, HEADS, VW], F16)
        kt = sb("kt", [2, QT, P], F16)
        kvt = sb("kvt", [2, 2, VW])
        kvacc = sb("kvacc", [QT, 2, VW])
        kvh, kvl = sb("kvh", [QT, 2, VW], F16), sb("kvl", [QT, 2, VW], F16)
        sm = sb("sm", [2, 4, P])
        sh, sl = sb("sh", [4, 4, P], F16), sb("sl", [4, 4, P], F16)
        dn, rd = sb("dn", [2, 4]), sb("rd", [2, 4])
        on = sb("on", [2, 4, DH])
        oh, ol = sb("oh", [2, 4 * DH], F16), sb("ol", [2, 4 * DH], F16)
        ot = sb("ot", [2, QT, T], F16)
        at = sb("at", [DT, HALF])

        def bank(name, dt=F32):
            return ctx.enter_context(nc.psum_tensor(name, [P, 2048 // (4 if dt == F32 else 2)], dt))

        pM = bank("pM")
        pF = [bank("pF0"), bank("pF1")]
        pS = bank("pS")
        pO = [bank("pO0"), bank("pO1")]
        pT = bank("pT", F16)
        pKV = bank("pKV")

        x_loaded = [sem(f"x_loaded{i}") for i in range(XS)]
        xh_ready, xl_ready, tok_done = sem("xh_ready"), sem("xl_ready"), sem("tok_done")
        h_ready, mean_done, xc_ready, sq_ready, var_done = (
            sem("h_ready"), sem("mean_done"), sem("xc_ready"), sem("sq_ready"), sem("var_done"))
        rs_step = sem("rs_step")
        x0_ready, tn_ready, nh_ready, nl_ready = sem("x0_ready"), sem("tn_ready"), sem("nh_ready"), sem("nl_ready")
        h_stored, x0_stored = sem("h_stored"), sem("x0_stored")
        qk_done, e_ready, z_read, f_ready, fh_ready, fl_ready = (
            sem("qk_done"), sem("e_ready"), sem("z_read"), sem("f_ready"), sem("fh_ready"), sem("fl_ready"))
        v_done, vh_ready, vl_ready, v_ones = sem("v_done"), sem("vh_ready"), sem("vl_ready"), sem("v_ones")
        s_done, sm_ready, sh_ready, sl_ready = sem("s_done"), sem("sm_ready"), sem("sh_ready"), sem("sl_ready")
        o_done, dn_ready, rd_ready, on_ready, oh_ready, ol_ready = (
            sem("o_done"), sem("dn_ready"), sem("rd_ready"), sem("on_ready"), sem("oh_ready"), sem("ol_ready"))
        turned, turn_read = sem("turned"), sem("turn_read")
        kv_done, kvt_ready, kva_ready, kvh_ready, kvl_ready = (
            sem("kv_done"), sem("kvt_ready"), sem("kva_ready"), sem("kvh_ready"), sem("kvl_ready"))
        at_done, at_ready, at_stored = sem("at_done"), sem("at_ready"), sem("at_stored")

        NKV = 4 * (CH - 1)
        UNITS = 2 * SEQS

        def quad_heads(q):
            return [8 * (q // 2) + q % 2 + 2 * k for k in range(4)]

        def score_place(h):
            return 2 * (h // 8) + h % 2, (h % 8) // 2

        def key_turn(i, c, part):
            return count(i, TURNS, 6 * c + 2 * part + 1)

        def output_turn(i, c, g):
            return count(i, TURNS, 6 * c + (2, 4, 5, 6)[g] if c < CH - 1 else 6 * c + g + 1)

        def run(engine, steps):
            def step(name, *args):
                if name in steps:
                    steps[name](*args)

            def use(u, what, bank, before):
                kind, n = what
                if kind == "p":
                    step("project", after(u, -1), before)
                elif kind == "f":
                    step("features", after(u, 1), n, bank, before)
                else:
                    step("values", after(u, 1), n, bank, before)

            def finish(u, what, bank):
                if what[0] == "f":
                    step("phi", after(u, 1), what[1], bank)
                elif what[0] == "p":
                    step("project_read", after(u, -1))

            def norm(u, s):
                if s < XS:
                    step("mix", u, s)
                    if s < XS - 1:
                        step("split", u, s + 1)
                    else:
                        step("h", u)
                elif s == 5:
                    step("x0", u)

            def norm_early(u, s):
                if s == 4:
                    step("mean", u)
                    step("centre", u)
                elif s == 5:
                    step("var", u)
                    step("rstd", u)
                elif s == 6:
                    step("normed", u)

            def dense(first, last):
                slots, before, n = [], {0: ("v", VALS - 1, 1), 1: ("f", FEATS - 1, 1)}, 0
                for s in range(8):
                    uses = [], []
                    for place, (kind, k) in enumerate(DENSE[s]):
                        if not ((kind == "p" and first) or (kind != "p" and last)):
                            uses[place].append(((kind, k), n % 2, before[n % 2]))
                            before[n % 2] = (kind, k, 0)
                        n += 1
                    slots.append(uses)
                return slots

            def unit(u, start=False, mix=True, last=False):
                i, h = u
                slots = dense(start, last)
                if mix:
                    step("split", after(u, 2), 0)
                for s in range(8):
                    c, g = 2 * h + s // 4, s % 4
                    early, late = slots[s]
                    summed = (c, g - 2) if g >= 2 and c < CH - 1 else (c - 1, g + 2) if g < 2 and c > 0 else None
                    if g < 2:
                        quad = (i, c, g + 2)
                    elif c < CH - 1:
                        quad = (i, c + 1, g - 2)
                    else:
                        quad = None if last else (i + 1, 0, g - 2)
                    for what in early:
                        use(u, *what)
                    if mix:
                        norm_early(after(u, 2), s)
                    if g >= 2:
                        step("turn", i, c, g - 2)
                    elif c > 0:
                        step("turn", i, c - 1, g + 2)
                    elif not start:
                        step("turn", i - 1, CH - 1, g + 2)
                    step("outputs", i, c, g)
                    for what in early:
                        finish(u, *what[:2])
                    if quad is not None:
                        step("scores", *quad)
                    step("outputs_split", i, c, g)
                    for what in late:
                        use(u, *what)
                    if summed is not None:
                        step("sums", i, *summed)
                    if g in (1, 2) and c < CH - 1:
                        step("keys", i, c, g - 1)
                    if quad is not None:
                        step("scores_split", *quad)
                    if summed is not None:
                        step("sums_split", i, *summed)
                    if mix:
                        norm(after(u, 2), s)
                    for what in late:
                        finish(u, *what[:2])

            step("split", (0, 0), 0)
            for s in range(8):
                norm_early((0, 0), s)
                norm((0, 0), s)
            step("split", (0, 1), 0)
            slots = dense(True, False)
            for s in range(8):
                for what, bank_no, before in slots[s][0] + slots[s][1]:
                    use((0, -1), what, bank_no, before)
                    finish((0, -1), what, bank_no)
                norm_early((0, 1), s)
                norm((0, 1), s)
            for q in range(2):
                step("scores", 0, 0, q)
                step("scores_split", 0, 0, q)
            unit((0, 0), start=True)
            unit((0, 1))
            with engine.Fori(1, SEQS - 1) as i:
                unit((i, 0))
                unit((i, 1))
            unit((SEQS - 1, 0), mix=False)
            unit((SEQS - 1, 1), mix=False, last=True)
            step("turn", SEQS - 1, CH - 1, 2)
            step("turn", SEQS - 1, CH - 1, 3)
            step("project", (SEQS - 1, 1), ("p", 0, 1))
            step("project_read", (SEQS - 1, 1))

        block = ctx.enter_context(nc.Block())

        @block.sync
        def _(sp):
            def load(u, k):
                if some(units(u, XS, k + 1 - XS)):
                    sp.wait_ge(xh_ready, units(u, XS, k + 1 - XS))
                    sp.wait_ge(xl_ready, units(u, XS, k + 1 - XS))
                sp.dma_start(xs[:, k, :, :].rearrange("p a n -> p (a n)"),
                             io["x"].rearrange("(s h) k p n -> s h k p n", h=2)[u[0], u[1], k]).then_inc(x_loaded[k], 16)

            def rows(name, u):
                return io[name][u[0], :, :, u[1] * HALF:(u[1] + 1) * HALF].rearrange("t p n -> p t n")

            def store_rows(u):
                sp.wait_ge(h_ready, units(u, 1, 1))
                sp.dma_start(rows("h_dram", u), hT[:, :, :]).then_inc(h_stored, 16)
                sp.wait_ge(x0_ready, units(u, 1, 1))
                sp.dma_start(rows("x0_dram", u), x0[:, :, :]).then_inc(x0_stored, 16)

            def store_attention(u):
                sp.wait_ge(at_ready, units(u, 1, 1))
                sp.dma_start(rows("at_dram", u), at[:, :, :]).then_inc(at_stored, 16)

            def unit(u, start=False, load_more=True, mix=True):
                if load_more:
                    load(after(u, 3), 0)
                    load(after(u, 3), 1)
                if not start:
                    store_attention(after(u, -1))
                if load_more:
                    load(after(u, 3), 2)
                    load(after(u, 3), 3)
                if mix:
                    store_rows(after(u, 2))

            for u in ((0, 0), (0, 1)):
                for k in range(XS):
                    load(u, k)
            store_rows((0, 0))
            for k in range(XS):
                load((1, 0), k)
            store_rows((0, 1))
            unit((0, 0), start=True)
            unit((0, 1))
            with sp.Fori(1, SEQS - 2) as i:
                unit((i, 0))
                unit((i, 1))
            unit((SEQS - 2, 0))
            unit((SEQS - 2, 1), load_more=False)
            unit((SEQS - 1, 0), load_more=False, mix=False)
            unit((SEQS - 1, 1), load_more=False, mix=False)
            store_attention((SEQS - 1, 1))
            sp.wait_ge(h_stored, 16 * UNITS)
            sp.wait_ge(x0_stored, 16 * UNITS)
            sp.wait_ge(at_stored, 16 * UNITS)

        @block.tensor
        def _(pe):
            def three(out, wh, wl, mh, ml, first, last):
                pe.matmul(out, wh, mh, start=first, stop=False, skip_group_check=True)
                pe.matmul(out, wl, mh, start=False, stop=False, skip_group_check=True)
                return pe.matmul(out, wh, ml, start=False, stop=last, skip_group_check=True)

            def half(u):
                return slice(u[1] * HALF, (u[1] + 1) * HALF)

            def mix(u, k):
                if k == 0 and some(units(u, 5, -4)):
                    pe.wait_ge(rs_step, units(u, 5, -4))
                pe.wait_ge(xh_ready, units(u, XS, k + 1))
                pe.wait_ge(xl_ready, units(u, XS, k + 1))
                for t in range(2):
                    for m in range(DT):
                        cols = slice(m * P, (m + 1) * P)
                        mm = three(pM[:, m * HALF:(m + 1) * HALF], tok_h[:, 2 * k + t, cols], tok_l[:, 2 * k + t, cols],
                                   xh[:, k, t, :], xl[:, k, t, :], k == t == m == 0, k == XS - 1 and t == 1)
                mm.then_inc(tok_done, 1)

            def mean(u):
                pe.wait_ge(h_ready, units(u, 1, 1))
                for t in range(DT):
                    mm = pe.matmul(pM[:, 0:HALF], ones[:, :], hT[:, t, :], start=(t == 0), stop=(t == DT - 1))
                mm.then_inc(mean_done, 1)

            def var(u):
                pe.wait_ge(sq_ready, units(u, 1, 1))
                for t in range(DT):
                    mm = pe.matmul(pM[:, 0:HALF], ones[:, :], sq[:, t, :], start=(t == 0), stop=(t == DT - 1))
                mm.then_inc(var_done, 1)

            def bank_free(w, before):
                kind, n, back = before
                if kind == "f" and some(units(w, FEATS, n + 1 - FEATS * back)):
                    pe.wait_ge(f_ready, units(w, FEATS, n + 1 - FEATS * back))
                elif kind == "v" and some(units(w, VALS, n + 1 - VALS * back)):
                    pe.wait_ge(vl_ready, units(w, VALS, n + 1 - VALS * back))
                elif kind == "p":
                    pe.wait_ge(at_ready, units(w, 1, -1))

            def features(w, n, bank_no, before):
                if n == 0:
                    pe.wait_ge(nh_ready, units(w, DT, DT))
                    pe.wait_ge(nl_ready, units(w, DT, DT))
                bank_free(w, before)
                for b in range(2):
                    j = 2 * FEAT_ORDER[n] + b
                    cols = slice(j * P, (j + 1) * P)
                    for t in range(DT):
                        mm = three(pF[bank_no][:, b * HALF:(b + 1) * HALF], qk_h[:, t, cols], qk_l[:, t, cols],
                                   nh[:, t, half(w)], nl[:, t, half(w)], b == t == 0, t == DT - 1)
                mm.then_inc(qk_done, 1)

            def values(w, n, bank_no, before):
                bank_free(w, before)
                c = 2 * w[1] + n // 2
                toks, cols = slice(c * P, (c + 1) * P), slice(n % 2 * T, (n % 2 + 1) * T)
                for t in range(DT):
                    mm = three(pF[bank_no][:, :], nh[:, t, toks], nl[:, t, toks], wv_h[:, t, cols], wv_l[:, t, cols],
                               t == 0, t == DT - 1)
                mm.then_inc(v_done, 1)

            def project(u, before):
                bank_free(after(u, 2 - before[2] * (before[0] == "p")), before)
                pe.wait_ge(turn_read, output_turn(u[0], 2 * u[1] + 1, 3))
                for m in range(DT):
                    cols = slice(m * P, (m + 1) * P)
                    for t in range(QT):
                        mm = three(pF[OUT_BANK][:, m * HALF:(m + 1) * HALF], wo_h[:, t, cols], wo_l[:, t, cols],
                                   ot[:, 0, t, half(u)], ot[:, 1, t, half(u)], m == t == 0, t == QT - 1)
                mm.then_inc(at_done, 1)

            def scores(i, c, q):
                toks = slice(c * P, (c + 1) * P)
                pe.wait_ge(fl_ready, units((i, c // 2), FEATS, 4 if q < 2 else FEATS))
                n = 4 * c + q
                if some(count(i, 16, n)):
                    pe.wait_ge(sm_ready, count(i, 16, n))
                for k, h in enumerate(quad_heads(q)):
                    rows = slice(DH * (h % 2), DH * (h % 2) + DH)
                    key, qry = QT + h // 2, h // 2
                    mm = three(pS[:, k * P:(k + 1) * P], qkh[rows, key, toks], qkl[rows, key, toks],
                               qkh[rows, qry, toks], qkl[rows, qry, toks], k == 0, True)
                mm.then_inc(s_done, 1)

            def keys(i, c, part):
                toks = slice(c * P, (c + 1) * P)
                if part == 1:
                    pe.wait_ge(fl_ready, units((i, c // 2), FEATS, FEATS))
                if some(key_turn(i, c, part) - 1):
                    pe.wait_ge(turn_read, key_turn(i, c, part) - 1)
                for half_no, src in enumerate((qkh, qkl)):
                    for p in range(4):
                        w = 4 * half_no + p
                        mm = pe.transpose(pT[:, w * P:(w + 1) * P], src[:, QT + 4 * part + p, toks], ident[:, :])
                mm.then_inc(turned, 1)

            def outputs(i, c, g):
                n = 4 * c + g
                toks = slice(c * P, (c + 1) * P)
                out = pO[g % 2]
                if some(count(i, 16, n - 1)):
                    pe.wait_ge(on_ready, count(i, 16, n - 1))
                first = True
                if c > 0:
                    pe.wait_ge(kvh_ready, count(i, NKV, 4 * (c - 1) + g + 1))
                    pe.wait_ge(kvl_ready, count(i, NKV, 4 * (c - 1) + g + 1))
                    for k in range(2):
                        p = 2 * g + k
                        mm = three(out[:, 2 * VW * k:2 * VW * (k + 1)], qkh[:, p, toks], qkl[:, p, toks],
                                   kvh[:, p, :, :], kvl[:, p, :, :], first, True)
                        first = False
                if g % 2 == 0:
                    pe.wait_ge(sh_ready, count(i, 16, 4 * c + g + 2))
                    pe.wait_ge(sl_ready, count(i, 16, 4 * c + g + 2))
                if g == 0:
                    if type(i) is int and i == 0 and c == 0:
                        pe.wait_ge(v_ones, 2)
                    pe.wait_ge(vh_ready, count(i, 2 * VALS, 2 * c + 2))
                    pe.wait_ge(vl_ready, count(i, 2 * VALS, 2 * c + 2))
                for k in range(4):
                    h = 4 * g + k
                    q, w = score_place(h)
                    mm = three(out[:, VW * k:VW * (k + 1)], sh[:, q, w, :], sl[:, q, w, :],
                               vh[:, c, h, :], vl[:, c, h, :], first, True)
                    first = False
                mm.then_inc(o_done, 1)

            def sums(i, c, g):
                u = 4 * c + g
                pe.wait_ge(turn_read, key_turn(i, c, g // 2))
                if some(count(i, NKV, u)):
                    pe.wait_ge(kvt_ready, count(i, NKV, u))
                for k in range(2):
                    p = 2 * g + k
                    mm = three(pKV[:, 2 * VW * k:2 * VW * (k + 1)], kt[:, 0, p, :], kt[:, 1, p, :],
                               vh[:, c, 2 * p:2 * p + 2, :], vl[:, c, 2 * p:2 * p + 2, :], k == 0, True)
                mm.then_inc(kv_done, 1)

            def turn(i, c, g):
                n = 4 * c + g
                if some(output_turn(i, c, g) - 1):
                    pe.wait_ge(turn_read, output_turn(i, c, g) - 1)
                pe.wait_ge(oh_ready, count(i, 16, n + 1))
                pe.wait_ge(ol_ready, count(i, 16, n + 1))
                for part, src in enumerate((oh, ol)):
                    for f in range(2):
                        w = 2 * part + f
                        mm = pe.transpose(pT[:, w * P:(w + 1) * P], src[:, n % 2, f * P:(f + 1) * P], ident[:, :])
                mm.then_inc(turned, 1)

            run(pe, dict(mix=mix, mean=mean, var=var, features=features, values=values, scores=scores, keys=keys,
                         outputs=outputs, sums=sums, turn=turn, project=project))

        @block.scalar
        def _(act):
            exp_ln_tables(nc, act)

            def split(u, k):
                act.wait_ge(x_loaded[k], units(u, 16, 16))
                if some(units(u, XS, k + 1 - XS)):
                    act.wait_ge(tok_done, units(u, XS, k + 1 - XS))
                nc.scalar.activation(xh[:, k, :, :], xs[:, k, :, :], ACT.Copy).then_inc(xh_ready, 1)

            def h(u):
                act.wait_ge(tok_done, units(u, XS, XS))
                if some(units(u, 1, 0)):
                    act.wait_ge(h_stored, units(u, 16, 0))
                    act.wait_ge(xc_ready, units(u, 1, 0))
                nc.scalar.activation(hT[:, :, :], pM[:, :].rearrange("p (m n) -> p m n", m=DT), ACT.Copy,
                                     scale=1 / TOK_SCALE).then_inc(h_ready, 1)

            def centre(u):
                act.wait_ge(xc_ready, units(u, 1, 1))
                nc.scalar.activation(sq[:, :, :], xc[:, :, :], ACT.Square).then_inc(sq_ready, 1)

            def rstd(u):
                act.wait_ge(var_done, units(u, 1, 1))
                if some(units(u, DT, 0)):
                    act.wait_ge(tn_ready, units(u, DT, 0))
                nc.scalar.activation(lnt[:, :], pM[:, 0:HALF], ACT.Ln, bias=EPS).then_inc(rs_step, 1)
                act.wait_ge(rs_step, units(u, 5, 1))
                nc.scalar.activation(r0[:, :], lnt[:, :], ACT.Exp, scale=-0.5).then_inc(rs_step, 1)
                act.wait_ge(rs_step, units(u, 5, 2))
                nc.scalar.activation(r1[:, :], r0[:, :], ACT.Square).then_inc(rs_step, 1)
                act.wait_ge(rs_step, units(u, 5, 3))
                nc.scalar.activation(lnt[:, :], r1[:, :], ACT.Ln, scale=-EPS, bias=1.0 + EPS).then_inc(rs_step, 1)
                act.wait_ge(rs_step, units(u, 5, 4))
                nc.scalar.activation(r1[:, :], lnt[:, :], ACT.Exp, scale=-0.5).then_inc(rs_step, 1)

            def normed(u):
                if some(units(u, VALS, -VALS)):
                    act.wait_ge(v_done, units(u, VALS, -VALS))
                for m in range(DT):
                    act.wait_ge(tn_ready, units(u, DT, m + 1))
                    nc.scalar.activation(nh[:, m, u[1] * HALF:(u[1] + 1) * HALF], tn[:, m, :], ACT.Identity,
                                         bias=b1[:, m:m + 1]).then_inc(nh_ready, 1)

            def features(w, n, bank_no, before):
                s = n % 2
                act.wait_ge(qk_done, units(w, FEATS, n + 1))
                if some(units(w, FEATS, n - 1)):
                    act.wait_ge(e_ready, units(w, FEATS, n - 1))
                nc.scalar.activation(rz[:, s, :, :], pF[bank_no][:, :].rearrange("p (b n) -> p b n", b=2), ACT.Relu,
                                     scale=-PHI_DOWN).then_inc(z_read, 1)
                act.wait_ge(z_read, units(w, FEATS, n + 1))
                if some(units(w, FEATS, n - 1)):
                    act.wait_ge(f_ready, units(w, FEATS, n - 1))
                nc.scalar.activation(ez[:, s, :, :], rz[:, s, :, :], ACT.Exp, scale=-1.0,
                                     bias=-math.log(PHI_DOWN)).then_inc(e_ready, 1)

            def values(w, n, bank_no, before):
                c, eight = 2 * w[1] + n // 2, n % 2
                act.wait_ge(v_done, units(w, VALS, n + 1))
                nc.scalar.activation(vh[:, c, 8 * eight:8 * eight + 8, 0:DH],
                                     pF[bank_no][:, :].rearrange("p (h e) -> p h e", e=DH), ACT.Copy,
                                     scale=1 / V_SCALE).then_inc(vh_ready, 1)

            def scores_split(i, c, q):
                n = 4 * c + q
                act.wait_ge(sm_ready, count(i, 16, n + 1))
                last = count(i, 16, 4 * (c - 1) + (2 if q < 2 else 4))
                if some(last):
                    act.wait_ge(o_done, last)
                nc.scalar.activation(sh[:, q, :, :], sm[:, n % 2, :, :], ACT.Copy).then_inc(sh_ready, 1)

            def turn(i, c, g):
                act.wait_ge(turned, output_turn(i, c, g))
                if some(units((i, c // 2), 1, -1)):
                    act.wait_ge(at_done, units((i, c // 2), 1, -1))
                nc.scalar.activation(ot[:, :, 2 * g:2 * g + 2, c * P:(c + 1) * P],
                                     pT[:, 0:4 * P].rearrange("p (a f n) -> p a f n", a=2, f=2),
                                     ACT.Copy).then_inc(turn_read, 1)

            def outputs_split(i, c, g):
                n = 4 * c + g
                act.wait_ge(on_ready, count(i, 16, n + 1))
                if g >= 2:
                    last = output_turn(i, c, g - 2)
                elif c > 0:
                    last = output_turn(i, c - 1, g + 2)
                else:
                    last = count(i, TURNS, g - 1)
                if some(last):
                    act.wait_ge(turned, last)
                nc.scalar.activation(oh[:, n % 2, :], on[:, n % 2, :, :].rearrange("p a b -> p (a b)"),
                                     ACT.Copy).then_inc(oh_ready, 1)

            def sums_split(i, c, g):
                u = 4 * c + g
                act.wait_ge(kva_ready, count(i, NKV, u + 1))
                act.wait_ge(o_done, count(i, 16, u + 1))
                nc.scalar.activation(kvh[:, 2 * g:2 * g + 2, :, :], kvacc[:, 2 * g:2 * g + 2, :, :],
                                     ACT.Copy).then_inc(kvh_ready, 1)

            run(act, dict(split=split, h=h, centre=centre, rstd=rstd, normed=normed, features=features, values=values,
                          scores_split=scores_split, turn=turn, outputs_split=outputs_split,
                          sums_split=sums_split))

        @block.vector
        def _(ve):
            def centre(u):
                ve.wait_ge(mean_done, units(u, 1, 1))
                if some(units(u, 1, 0)):
                    ve.wait_ge(sq_ready, units(u, 1, 0))
                    ve.wait_ge(x0_ready, units(u, 1, 0))
                nc.vector.tensor_tensor(xc[:, :, :], hT[:, :, :],
                                        pM[:, 0:HALF].unsqueeze(1).broadcast_to([P, DT, HALF]),
                                        ALU.subtract).then_inc(xc_ready, 1)

            def x0_rows(u):
                ve.wait_ge(rs_step, units(u, 5, 2))
                ve.wait_ge(xc_ready, units(u, 1, 1))
                if some(units(u, 1, 0)):
                    ve.wait_ge(x0_stored, units(u, 16, 0))
                    ve.wait_ge(tn_ready, units(u, DT, 0))
                nc.vector.tensor_tensor(x0[:, :, :], xc[:, :, :], r0[:, :].unsqueeze(1).broadcast_to([P, DT, HALF]),
                                        ALU.mult).then_inc(x0_ready, 1)

            def normed(u):
                ve.wait_ge(rs_step, units(u, 5, 5))
                ve.wait_ge(x0_ready, units(u, 1, 1))
                if some(units(u, DT, 0)):
                    ve.wait_ge(nh_ready, units(u, DT, 0))
                    ve.wait_ge(nl_ready, units(u, DT, 0))
                for m in range(DT):
                    nc.vector.scalar_tensor_tensor(tn[:, m, :], x0[:, m, :], g1[:, m:m + 1], r1[:, :],
                                                   ALU.mult, ALU.mult).then_inc(tn_ready, 1)
                for m in range(DT):
                    cols = slice(u[1] * HALF, (u[1] + 1) * HALF)
                    ve.wait_ge(tn_ready, units(u, DT, m + 1))
                    ve.wait_ge(nh_ready, units(u, DT, m + 1))
                    nc.vector.scalar_tensor_tensor(nl[:, m, cols], tn[:, m, :], b1[:, m:m + 1], nh[:, m, cols],
                                                   ALU.add, ALU.subtract).then_inc(nl_ready, 1)

            def phi(w, n, bank_no):
                s = n % 2
                pair = 2 * FEAT_ORDER[n]
                ve.wait_ge(e_ready, units(w, FEATS, n + 1))
                if some(units(w, FEATS, n - 1)):
                    ve.wait_ge(fl_ready, units(w, FEATS, n - 1))
                nc.vector.scalar_tensor_tensor(fz[:, s, :, :], pF[bank_no][:, :].rearrange("p (b n) -> p b n", b=2), 0.0,
                                               ez[:, s, :, :], ALU.max, ALU.add).then_inc(f_ready, 1)
                ve.wait_ge(f_ready, units(w, FEATS, n + 1))
                nc.vector.tensor_copy(qkh[:, pair:pair + 2, w[1] * HALF:(w[1] + 1) * HALF],
                                      fz[:, s, :, :]).then_inc(fh_ready, 1)

            def values(w, n, bank_no, before):
                c, heads = 2 * w[1] + n // 2, slice(n % 2 * 8, n % 2 * 8 + 8)
                ve.wait_ge(vh_ready, units(w, VALS, n + 1))
                nc.vector.scalar_tensor_tensor(vl[:, c, heads, 0:DH], pF[bank_no][:, :].rearrange("p (h e) -> p h e", e=DH),
                                               1 / V_SCALE, vh[:, c, heads, 0:DH],
                                               ALU.mult, ALU.subtract).then_inc(vl_ready, 1)

            def project_read(u):
                ve.wait_ge(at_done, units(u, 1, 1))
                if some(units(u, 1, 0)):
                    ve.wait_ge(at_stored, units(u, 16, 0))
                nc.vector.tensor_scalar(at[:, :, :], pF[OUT_BANK][:, :].rearrange("p (m n) -> p m n", m=DT), 1 / WO_SCALE, None,
                                        ALU.mult).then_inc(at_ready, 1)

            def scores(i, c, q):
                n = 4 * c + q
                ve.wait_ge(s_done, count(i, 16, n + 1))
                if some(count(i, 16, n - 1)):
                    ve.wait_ge(sh_ready, count(i, 16, n - 1))
                    ve.wait_ge(sl_ready, count(i, 16, n - 1))
                nc.vector.tensor_tensor(sm[:, n % 2, :, :], pS[:, :].rearrange("p (a b) -> p a b", b=P),
                                        mask[:, :].unsqueeze(1).broadcast_to([P, 4, P]),
                                        ALU.mult).then_inc(sm_ready, 1)

            def keys(i, c, part):
                ve.wait_ge(turned, key_turn(i, c, part))
                if some(count(i, NKV, 4 * c - 2 + 2 * part)):
                    ve.wait_ge(kv_done, count(i, NKV, 4 * c - 2 + 2 * part))
                nc.vector.tensor_copy(kt[:, :, 4 * part:4 * part + 4, :],
                                      pT[:, :].rearrange("p (a f n) -> p a f n", a=2, f=4)).then_inc(turn_read, 1)

            def outputs(i, c, g):
                n = 4 * c + g
                s = n % 2
                heads = pO[g % 2][:, 0:4 * VW].rearrange("p (h e) -> p h e", e=VW)
                ve.wait_ge(o_done, count(i, 16, n + 1))
                nc.vector.tensor_scalar(dn[:, s, :], heads[:, :, DH], DEN_EPS / PHI_DOWN ** 2, None,
                                        ALU.add).then_inc(dn_ready, 1)
                ve.wait_ge(dn_ready, count(i, 16, n + 1))
                nc.vector.reciprocal(rd[:, s, :], dn[:, s, :]).then_inc(rd_ready, 1)
                ve.wait_ge(rd_ready, count(i, 16, n + 1))
                if some(count(i, 16, n - 1)):
                    ve.wait_ge(oh_ready, count(i, 16, n - 1))
                    ve.wait_ge(ol_ready, count(i, 16, n - 1))
                nc.vector.tensor_tensor(on[:, s, :, :], heads[:, :, 0:DH],
                                        rd[:, s, :].unsqueeze(2).broadcast_to([P, 4, DH]),
                                        ALU.mult).then_inc(on_ready, 1)

            def sums(i, c, g):
                u = 4 * c + g
                ve.wait_ge(kv_done, count(i, NKV, u + 1))
                pairs = slice(2 * g, 2 * g + 2)
                found = pKV[:, 0:4 * VW].rearrange("p (a b e) -> p a b e", a=2, b=2)
                if c == 0:
                    if some(count(i, NKV, 0)):
                        ve.wait_ge(kvh_ready, count(i, NKV, 0))
                        ve.wait_ge(kvl_ready, count(i, NKV, 0))
                    nc.vector.tensor_tensor(kvt[:, :, :, :], found, block_mask[:, :, :, :],
                                            ALU.mult).then_inc(kvt_ready, 1)
                    ve.wait_ge(kvt_ready, count(i, NKV, u + 1))
                    nc.vector.tensor_copy(kvacc[:, pairs, :, :], kvt[:, :, :, :]).then_inc(kva_ready, 1)
                else:
                    ve.wait_ge(kva_ready, count(i, NKV, u))
                    nc.vector.tensor_tensor(kvt[:, :, :, :], found, block_mask[:, :, :, :],
                                            ALU.mult).then_inc(kvt_ready, 1)
                    ve.wait_ge(kvt_ready, count(i, NKV, u + 1))
                    ve.wait_ge(kvh_ready, count(i, NKV, u - 3))
                    ve.wait_ge(kvl_ready, count(i, NKV, u - 3))
                    nc.vector.tensor_tensor(kvacc[:, pairs, :, :], kvacc[:, pairs, :, :], kvt[:, :, :, :],
                                            ALU.add).then_inc(kva_ready, 1)

            run(ve, dict(centre=centre, x0=x0_rows, normed=normed, phi=phi, values=values, project_read=project_read,
                         scores=scores, keys=keys, outputs=outputs, sums=sums))

        @block.gpsimd
        def _(gp):
            gp.memset(vh[:, :, :, DH:VW], 1.0).then_inc(v_ones, 1)
            gp.memset(vl[:, :, :, DH:VW], 0.0).then_inc(v_ones, 1)

            def split(u, k):
                gp.wait_ge(xh_ready, units(u, XS, k + 1))
                if some(units(u, XS, k + 1 - XS)):
                    gp.wait_ge(tok_done, units(u, XS, k + 1 - XS))
                nc.gpsimd.tensor_tensor(xl[:, k, :, :], xs[:, k, :, :], xh[:, k, :, :], ALU.subtract).then_inc(xl_ready, 1)

            def phi(w, n, bank_no):
                pair = 2 * FEAT_ORDER[n]
                cols = slice(w[1] * HALF, (w[1] + 1) * HALF)
                gp.wait_ge(fh_ready, units(w, FEATS, n + 1))
                nc.gpsimd.tensor_tensor(qkl[:, pair:pair + 2, cols], fz[:, n % 2, :, :], qkh[:, pair:pair + 2, cols],
                                        ALU.subtract).then_inc(fl_ready, 1)

            def scores_split(i, c, q):
                n = 4 * c + q
                gp.wait_ge(sh_ready, count(i, 16, n + 1))
                nc.gpsimd.tensor_tensor(sl[:, q, :, :], sm[:, n % 2, :, :], sh[:, q, :, :],
                                        ALU.subtract).then_inc(sl_ready, 1)

            def outputs_split(i, c, g):
                n = 4 * c + g
                gp.wait_ge(oh_ready, count(i, 16, n + 1))
                nc.gpsimd.tensor_tensor(ol[:, n % 2, :], on[:, n % 2, :, :].rearrange("p a b -> p (a b)"),
                                        oh[:, n % 2, :], ALU.subtract).then_inc(ol_ready, 1)

            def sums_split(i, c, g):
                u = 4 * c + g
                gp.wait_ge(kvh_ready, count(i, NKV, u + 1))
                pairs = slice(2 * g, 2 * g + 2)
                nc.gpsimd.tensor_tensor(kvl[:, pairs, :, :], kvacc[:, pairs, :, :], kvh[:, pairs, :, :],
                                        ALU.subtract).then_inc(kvl_ready, 1)

            run(gp, dict(split=split, phi=phi, scores_split=scores_split, outputs_split=outputs_split,
                         sums_split=sums_split))


FT = 8
EXPERTS = 8
SLOTS = 1280
TILES = SLOTS // P
TOP = 4
ST = 4
TOKENS = SEQS * T
DUMMIES = P
W1_SCALE = 64.0
W2_SCALE = 64.0
GATE_SCALE = 8.0
SH_SCALE = 16.0
SHD_SCALE = 16.0
FAR = 1.0e6


def mlp_phase(nc, io):
    with ExitStack() as ctx:
        def sb(name, shape, dt=F32):
            return ctx.enter_context(nc.sbuf_tensor(name, [P, *shape], dt))

        def sem(name):
            return ctx.enter_context(nc.semaphore(name))

        w1_h, w1_l = sb("w1_h", [DT, FT * P], F16), sb("w1_l", [DT, FT * P], F16)
        w2_h, w2_l = sb("w2_h", [FT, D], F16), sb("w2_l", [FT, D], F16)
        sg_h, sg_l = sb("sg_h", [DT, 2 * ST * P], F16), sb("sg_l", [DT, 2 * ST * P], F16)
        sd_h, sd_l = sb("sd_h", [ST, D], F16), sb("sd_l", [ST, D], F16)
        gw_h, gw_l = sb("gw_h", [DT, EXPERTS + 1], F16), sb("gw_l", [DT, EXPERTS + 1], F16)
        ones = sb("ones2", [P])
        ones16 = sb("ones16", [P], F16)
        ident = sb("ident2", [P])
        ident16 = sb("ident16", [P], F16)
        upto = sb("upto", [P])
        upto16 = sb("upto16", [P], F16)
        earlier = sb("earlier", [EXPERTS, EXPERTS])
        first_slot = sb("first_slot", [EXPERTS])
        rank_no = sb("rank_no", [TOP, EXPERTS])
        tid = sb("tid", [CH])
        carry = sb("carry", [EXPERTS])
        vecs = sb("vecs", [4, DT])
        b1m = sb("b1m", [FT])
        mb2 = vecs[:, 2, :]
        empty = sb("empty", [EXPERTS * SLOTS // P, 2], U32)
        zrow = sb("zrow", [D])

        with ExitStack() as pre:
            def tmp(name, shape, dt=F32):
                return pre.enter_context(nc.sbuf_tensor(name, [P, *shape], dt))

            w1_w, w2_w = tmp("w1_w", [DT, FT * P]), tmp("w2_w", [FT, D])
            sg_w, sd_w = tmp("sg_w", [DT, 2 * ST * P]), tmp("sd_w", [ST, D])
            gw_w = tmp("gw_w", [DT, EXPERTS + 1])
            dummy_id = tmp("dummy_id", [1])
            loaded = pre.enter_context(nc.semaphore("w2_loaded"))
            hi_ready = pre.enter_context(nc.semaphore("w2_hi"))
            made = pre.enter_context(nc.semaphore("made2"))
            filled = pre.enter_context(nc.semaphore("filled"))
            cleared = pre.enter_context(nc.semaphore("cleared"))
            splits = [(w1_w, w1_h, w1_l, W1_SCALE), (w2_w, w2_h, w2_l, W2_SCALE), (sg_w, sg_h, sg_l, SH_SCALE),
                      (sd_w, sd_h, sd_l, SHD_SCALE), (gw_w, gw_h, gw_l, GATE_SCALE)]
            with nc.Block() as block:
                @block.sync
                def _(sp):
                    sp.dma_start(w1_w[:, :, :], io["w1"].rearrange("(t p) n -> p t n", p=P)).then_inc(loaded, 16)
                    sp.dma_start(w2_w[:, :, :], io["w2"].rearrange("(t p) n -> p t n", p=P)).then_inc(loaded, 16)
                    sp.dma_start(sg_w[:, :, 0:ST * P], io["shgT"].rearrange("(t p) n -> p t n", p=P)).then_inc(loaded, 16)
                    sp.dma_start(sg_w[:, :, ST * P:], io["shuT"].rearrange("(t p) n -> p t n", p=P)).then_inc(loaded, 16)
                    sp.dma_start(sd_w[:, :, :], io["shdT"].rearrange("(t p) n -> p t n", p=P)).then_inc(loaded, 16)
                    sp.dma_start(gw_w[:, :, :], io["gateT"].rearrange("(t p) n -> p t n", p=P)).then_inc(loaded, 16)
                    sp.dma_start(vecs[:, 0, :], io["g2"]).then_inc(loaded, 16)
                    sp.dma_start(vecs[:, 1, :], io["beta2"]).then_inc(loaded, 16)
                    sp.dma_start(vecs[:, 2, :], io["b2"]).then_inc(loaded, 16)
                    sp.dma_start(b1m[:, :], io["b1"]).then_inc(loaded, 16)
                    sp.wait_ge(filled, 1)
                    sp.dma_start(io["out"][TOKENS:TOKENS + DUMMIES, :], zrow[:, :]).then_inc(cleared, 16)
                    sp.dma_start(io["xrow_dram"][TOKENS:TOKENS + DUMMIES, :], zrow[:, :].bitcast(F16)).then_inc(cleared, 16)
                    sp.wait_ge(cleared, 32)
                    sp.wait_ge(loaded, 160)

                @block.gpsimd
                def _(gp):
                    gp.memset(ones[:, :], 1.0 / D).then_inc(made, 1)
                    identity(nc, gp, ident[:, :], made, 1)
                    causal_mask(nc, gp, upto[:, :], made, 3)
                    gp.memset(earlier[:, :, :], 1.0).then_inc(made, 1)
                    gp.wait_ge(made, 6)
                    gp.affine_select(out=earlier[:, :, :], in_=earlier[:, :, :], compare_op=ALU.is_gt, fill=0.0,
                                     base=0, pattern=[[1, EXPERTS], [-1, EXPERTS]],
                                     channel_multiplier=0).then_inc(made, 1)
                    gp.iota(first_slot[:, :], [[SLOTS, EXPERTS]], base=0, channel_multiplier=0,
                            allow_small_or_imprecise_dtypes=True).then_inc(made, 1)
                    gp.iota(rank_no[:, :, :], [[1, TOP], [0, EXPERTS]], base=0, channel_multiplier=0,
                            allow_small_or_imprecise_dtypes=True).then_inc(made, 1)
                    gp.iota(tid[:, :], [[P, CH]], base=0, channel_multiplier=1,
                            allow_small_or_imprecise_dtypes=True).then_inc(made, 1)
                    gp.iota(dummy_id[:, :], [[0, 1]], base=TOKENS, channel_multiplier=1,
                            allow_small_or_imprecise_dtypes=True).then_inc(made, 1)

                @block.vector
                def _(ve):
                    ve.memset(carry[:, :], 0.0)
                    ve.memset(ones16[:, :], 1.0)
                    ve.memset(zrow[:, :], 0.0).then_inc(filled, 1)
                    ve.memset(empty[:, :, :], 0).then_inc(filled, 1)
                    ve.wait_ge(made, 11)
                    ve.wait_ge(filled, 2)
                    nc.vector.tensor_copy(ident16[:, :], ident[:, :])
                    nc.vector.tensor_copy(upto16[:, :], upto[:, :]).then_inc(filled, 1)
                    nc.vector.tensor_copy(empty[:, :, 0],
                                          dummy_id[:, :].broadcast_to([P, EXPERTS * SLOTS // P])).then_inc(filled, 1)
                    ve.wait_ge(loaded, 160)
                    for n, (w, h, l, scale) in enumerate(splits):
                        ve.wait_ge(hi_ready, n + 1)
                        nc.vector.scalar_tensor_tensor(l[:, :, :], w[:, :, :], scale, h[:, :, :],
                                                       ALU.mult, ALU.subtract)

                @block.scalar
                def _(act):
                    act.wait_ge(loaded, 160)
                    for w, h, l, scale in splits:
                        nc.scalar.activation(h[:, :, :], w[:, :, :], ACT.Copy, scale=scale).then_inc(hi_ready, 1)

        x0b, hb_in, atb = sb("x0b", [DT, T]), sb("hb_in", [DT, T]), sb("atb", [DT, T])
        x1, hb, hx = sb("x1", [DT, T]), sb("hb", [DT, T]), sb("hx", [DT, T])
        xc2, sq2, ln2, rs2, tn2 = sb("xc2", [DT, T]), sb("sq2", [DT, T]), sb("ln2", [T]), sb("rs2", [T]), sb("tn2", [DT, T])
        n2h, n2l = sb("n2h", [DT, T], F16), sb("n2l", [DT, T], F16)
        gz = sb("gz", [4, T])
        gh, gl = sb("gh", [FT, T], F16), sb("gl", [FT, T], F16)
        hp = sb("hp", [DT, T])
        xc3, sq3, ln3, rs3, xn = sb("xc3", [DT, T]), sb("sq3", [DT, T]), sb("ln3", [T]), sb("rs3", [T]), sb("xn", [DT, T])
        xnh, xnl = sb("xnh", [DT, T], F16), sb("xnl", [DT, T], F16)
        xt = sb("xt", [CH, 2 * D], F16)
        ht = sb("ht", [CH, D])
        sz, az = sb("sz", [2, T]), sb("az", [2, T])
        ah, al = sb("ah", [ST, T], F16), sb("al", [ST, T], F16)
        ob = sb("ob", [CH, D])
        lg = sb("lg", [CH, EXPERTS + 1])
        pair = [sb(f"pair{i}", [CH * EXPERTS, EXPERTS]) for i in range(5)]
        few = [sb(f"few{i}", [CH, EXPERTS]) for i in range(9)]
        one = [sb(f"one{i}", [CH]) for i in range(6)]
        ml9, e9 = sb("ml9", [CH, EXPERTS + 1]), sb("e9", [CH, EXPERTS + 1])
        rw, m0, rank = sb("rw", [CH, EXPERTS]), sb("m0", [CH, EXPERTS]), sb("rank", [CH, EXPERTS])
        m16 = sb("m16", [CH, EXPERTS], F16)
        w8 = sb("w8", [CH])
        slot_f, w_f = sb("slot_f", [CH, TOP]), sb("w_f", [CH, TOP])
        slot_u = sb("slot_u", [CH, TOP], U32)
        entry = sb("entry", [CH, TOP, 2], U32)

        def bank(name):
            return ctx.enter_context(nc.psum_tensor(name, [P, 512], F32))

        pW = [bank("pW0"), bank("pW1")]
        pY = [bank("pY0"), bank("pY1")]
        pA = [bank("pA0"), bank("pA1")]
        pL = bank("pL")

        (x0_in, h_in, at_in, x1_ready, hb_ready, hx_ready, mean2_done, xc2_ready, sq2_ready, var2_done, rs2_step,
         tn2_ready, n2h_ready, n2l_ready) = [sem(n) for n in (
             "x0_in", "h_in", "at_in", "x1_ready", "hb_ready", "hx_ready", "mean2_done", "xc2_ready", "sq2_ready",
             "var2_done", "rs2_step", "tn2_ready", "n2h_ready", "n2l_ready")]
        (w1_done, gz_ready, gh_ready, gl_even, gl_odd, w2_done, hp_ready, mean3_done, xc3_ready, sq3_ready, var3_done,
         rs3_step, xn_ready, xnh_ready, xnl_ready) = [sem(n) for n in (
             "w1_done", "gz_ready", "gh_ready", "gl_even", "gl_odd", "w2_done", "hp_ready", "mean3_done", "xc3_ready",
             "sq3_ready", "var3_done", "rs3_step", "xn_ready", "xnh_ready", "xnl_ready")]
        (lg_done, lg_ready, xt_done, xt_ready, xt_stored, ht_done, ht_ready, gu_done, sz_ready, az_ready, ah_ready,
         al_ready, down_done, ob_ready, ob_stored) = [sem(n) for n in (
             "lg_done", "lg_ready", "xt_done", "xt_ready", "xt_stored", "ht_done", "ht_ready", "gu_done", "sz_ready",
             "az_ready", "ah_ready", "al_ready", "down_done", "ob_ready", "ob_stored")]
        (route, route_exp, mask_ready, cum_done, cum_read, routed, list_ready, list_sent, lists_cleared) = [sem(n) for n in (
            "route", "route_exp", "mask_ready", "cum_done", "cum_read", "routed", "list_ready", "list_sent", "lists_cleared")]

        passed = sem("passed2")

        def run(engine, s):
            def body(i, before, after):
                s["w1"](i, before, (0, 1))
                if after:
                    s["mean2"](i + 1)
                s["w1"](i, before, range(2, FT))
                if after:
                    s["centre2"](i + 1)
                if before:
                    s["mask"](i - 1)
                s["w2"](i, range(7))
                if before:
                    s["counts"](i - 1)
                s["w2"](i, range(7, FT))
                if after:
                    s["var2"](i + 1)
                if after:
                    s["scale2"](i + 1)
                if before:
                    s["gate_up"](i - 1, after, (0,))
                s["mean3"](i, before)
                if after:
                    s["shift2"](i + 1)
                if before:
                    s["gate_up"](i - 1, after, (1, 2))
                s["var3"](i)
                if before:
                    s["gate_up"](i - 1, after, (3,))
                s["rstd3"](i)
                if before:
                    s["down"](i - 1)
                s["turn_rows"](i, before)
                s["logits"](i)
                s["turn_sums"](i)

            s["mean2"](0)
            s["centre2"](0)
            s["var2"](0)
            s["scale2"](0)
            s["shift2"](0)
            body(0, False, True)
            body(1, True, True)
            with engine.Fori(2, SEQS - 2) as i:
                body(i, True, True)
            body(SEQS - 2, True, True)
            body(SEQS - 1, True, False)
            s["mask"](SEQS - 1)
            s["counts"](SEQS - 1)
            s["gate_up"](SEQS - 1, None, range(ST))
            s["down"](SEQS - 1)

        def at_start(i):
            return type(i) is int and i == 0

        block = ctx.enter_context(nc.Block())

        @block.sync
        def _(sp):
            def load(i):
                if not at_start(i):
                    sp.wait_ge(x1_ready, count(i, DT, 0))
                    sp.wait_ge(hb_ready, count(i, DT, 0))
                for dst, name, arrived in ((x0b, "x0_dram", x0_in), (atb, "at_dram", at_in), (hb_in, "h_dram", h_in)):
                    sp.dma_start(dst[:, :, :], io[name][i].rearrange("t p n -> p t n")).then_inc(arrived, 16)

            def store_rows(i):
                for half in range(2):
                    sp.wait_ge(xt_ready, count(i, 2, half + 1))
                    rows = io["xrow_dram"][0:TOKENS, :].rearrange("(s c p) n -> s p c n", c=CH, p=P)
                    sp.dma_start(rows[i, :, 2 * half:2 * half + 2, :],
                                 xt[:, 2 * half:2 * half + 2, :]).then_inc(xt_stored, 16)

            def store_out(i):
                rows = io["out"][0:TOKENS, :].rearrange("(s c p) n -> s p c n", c=CH, p=P)
                sp.wait_ge(ob_ready, count(i, CH, CH))
                sp.dma_start(rows[i], ob[:, :, :]).then_inc(ob_stored, 16)

            sp.dma_start(io["list_dram"].rearrange("(e p n) w -> p e n w", p=P, n=TILES),
                         empty[:, :, :].rearrange("p (e n) w -> p e n w", n=TILES)).then_inc(lists_cleared, 16)
            load(0)
            load(1)
            load(2)
            store_rows(0)
            load(3)
            store_out(0)
            store_rows(1)
            with sp.Fori(2, SEQS - 2) as i:
                load(i + 2)
                store_out(i - 1)
                store_rows(i)
            store_out(SEQS - 3)
            store_rows(SEQS - 2)
            store_out(SEQS - 2)
            store_rows(SEQS - 1)
            store_out(SEQS - 1)
            sp.wait_ge(xt_stored, 32 * SEQS)
            sp.wait_ge(ob_stored, 16 * SEQS)

        @block.tensor
        def _(pe):
            def three(out, wh, wl, mh, ml, first, last):
                pe.matmul(out, wh, mh, start=first, stop=False, skip_group_check=True)
                pe.matmul(out, wl, mh, start=False, stop=False, skip_group_check=True)
                return pe.matmul(out, wh, ml, start=False, stop=last, skip_group_check=True)

            def mean2(i):
                pe.wait_ge(x1_ready, count(i, DT, DT))
                if not (type(i) is int and i < 2):
                    pe.wait_ge(ht_ready, count(i, 2, -2))
                for t in range(DT):
                    mm = pe.matmul(pA[0][:, :], ones[:, :], x1[:, t, :], start=(t == 0), stop=(t == DT - 1))
                mm.then_inc(mean2_done, 1)

            def var2(i):
                if not (type(i) is int and i < 2):
                    pe.wait_ge(cum_read, count(i, 1, -1))
                pe.wait_ge(sq2_ready, count(i, DT, DT))
                for t in range(DT):
                    mm = pe.matmul(pA[1][:, :], ones[:, :], sq2[:, t, :], start=(t == 0), stop=(t == DT - 1))
                mm.then_inc(var2_done, 1)

            def w1(i, before, js):
                if js[0] == 0:
                    pe.wait_ge(n2h_ready, count(i, DT, DT))
                    pe.wait_ge(n2l_ready, count(i, DT, DT))
                for j in js:
                    if j >= 2:
                        pe.wait_ge(gz_ready, count(i, FT, j - 1))
                    elif not (type(i) is int and i < 2):
                        pe.wait_ge(az_ready, count(i, ST, -ST))
                    cols = slice(j * P, (j + 1) * P)
                    for t in range(DT):
                        mm = three(pW[j % 2][:, :], w1_h[:, t, cols], w1_l[:, t, cols], n2h[:, t, :], n2l[:, t, :],
                                   t == 0, t == DT - 1)
                    mm.then_inc(w1_done, 1)

            def w2(i, js):
                if js[0] == 0 and not (type(i) is int and i < 2):
                    pe.wait_ge(ob_ready, count(i, CH, -CH))
                for j in js:
                    pe.wait_ge(gh_ready, count(i, FT, j + 1))
                    pe.wait_ge(gl_odd if j % 2 else gl_even, count(i, FT // 2, j // 2 + 1))
                    for m in range(DT):
                        cols = slice(m * P, (m + 1) * P)
                        mm = three(pY[m][:, :], w2_h[:, j, cols], w2_l[:, j, cols], gh[:, j, :], gl[:, j, :],
                                   j == 0, j == FT - 1)
                if js[-1] == FT - 1:
                    mm.then_inc(w2_done, 1)

            def mean3(i, before):
                pe.wait_ge(hp_ready, count(i, DT, DT))
                if before:
                    pe.wait_ge(lg_ready, count(i, 1, 0))
                for t in range(DT):
                    mm = pe.matmul(pL[:, :], ones[:, :], hp[:, t, :], start=(t == 0), stop=(t == DT - 1))
                mm.then_inc(mean3_done, 1)

            def gate_up(i, after, js):
                for j in js:
                    g, u = (pW[0], pW[1]) if j % 2 == 0 else (pA[0], pA[1])
                    if j >= 2:
                        pe.wait_ge(az_ready, count(i, ST, j - 1))
                    elif j == 0 and after is not None:
                        pe.wait_ge(gz_ready, count(i + 1, FT, FT))
                    elif j == 0:
                        pe.wait_ge(gz_ready, FT * SEQS)
                    elif after:
                        pe.wait_ge(xc2_ready, count(i + 2, DT, DT))
                        pe.wait_ge(rs2_step, count(i + 2, 2, 1))
                    else:
                        pe.wait_ge(ht_ready, count(i, 2, 2))
                        pe.wait_ge(cum_read, count(i, 1, 1))
                    for out, base in ((g, 0), (u, ST * P)):
                        cols = slice(base + j * P, base + (j + 1) * P)
                        for t in range(DT):
                            mm = three(out[:, :], sg_h[:, t, cols], sg_l[:, t, cols], xnh[:, t, :], xnl[:, t, :],
                                       t == 0, t == DT - 1)
                        mm.then_inc(gu_done, 1)

            def var3(i):
                pe.wait_ge(sq3_ready, count(i, DT, DT))
                pe.wait_ge(xc3_ready, count(i, DT, DT))
                for t in range(DT):
                    mm = pe.matmul(pL[:, :], ones[:, :], sq3[:, t, :], start=(t == 0), stop=(t == DT - 1))
                mm.then_inc(var3_done, 1)

            def down(i):
                pe.wait_ge(hp_ready, DT * SEQS if type(i) is int and i == SEQS - 1 else count(i + 1, DT, DT))
                for k in range(ST):
                    pe.wait_ge(ah_ready, count(i, ST, k + 1))
                    pe.wait_ge(al_ready, count(i, ST, k + 1))
                    for c in range(CH):
                        toks = slice(c * P, (c + 1) * P)
                        mm = three(pY[c % 2][:, c // 2 * D:(c // 2 + 1) * D], ah[:, k, toks], al[:, k, toks],
                                   sd_h[:, k, :], sd_l[:, k, :], k == 0 and c < 2, k == ST - 1)
                mm.then_inc(down_done, 1)

            def logits(i):
                pe.wait_ge(rs3_step, count(i, 2, 1))
                pe.wait_ge(xnh_ready, count(i, DT, DT))
                pe.wait_ge(xnl_ready, count(i, DT, DT))
                n = EXPERTS + 1
                for c in range(CH):
                    toks = slice(c * P, (c + 1) * P)
                    for t in range(DT):
                        mm = three(pL[:, c * n:(c + 1) * n], xnh[:, t, toks], xnl[:, t, toks], gw_h[:, t, :],
                                   gw_l[:, t, :], c == 0 and t == 0, t == DT - 1)
                mm.then_inc(lg_done, 1)

            def turn_rows(i, before):
                pe.wait_ge(xnh_ready, count(i, DT, DT))
                pe.wait_ge(xnl_ready, count(i, DT, DT))
                for half in range(2):
                    if half == 0:
                        if before:
                            pe.wait_ge(az_ready, count(i, ST, 0))
                        else:
                            pe.wait_ge(xc2_ready, count(i + 1, DT, DT))
                            pe.wait_ge(rs2_step, count(i + 1, 2, 1))
                    bank16 = pA[half][:, :].bitcast(F16)
                    for c in range(2):
                        toks = slice((2 * half + c) * P, (2 * half + c + 1) * P)
                        for part, src in enumerate((xnh, xnl)):
                            for t in range(DT):
                                w = (c * 2 + part) * DT + t
                                mm = pe.transpose(bank16[:, w * P:(w + 1) * P], src[:, t, toks], ident16[:, :])
                    mm.then_inc(xt_done, 1)

            def turn_sums(i):
                for half in range(2):
                    pe.wait_ge(xt_ready, count(i, 2, half + 1))
                    for c in range(2):
                        toks = slice((2 * half + c) * P, (2 * half + c + 1) * P)
                        for t in range(DT):
                            w = c * DT + t
                            mm = pe.transpose(pA[half][:, w * P:(w + 1) * P], hp[:, t, toks], ident[:, :])
                    mm.then_inc(ht_done, 1)

            def counts(i):
                pe.wait_ge(mask_ready, count(i, 1, 1))
                pe.wait_ge(ht_ready, count(i, 2, 2))
                first = True
                for c in range(CH + 1):
                    out = pA[1][:, c * EXPERTS:(c + 1) * EXPERTS]
                    for before in range(c):
                        mm = pe.matmul(out, ones16[:, :], m16[:, before, :], start=first, stop=before == CH - 1,
                                       skip_group_check=True)
                        first = False
                    if c < CH:
                        mm = pe.matmul(out, upto16[:, :], m16[:, c, :], start=first, stop=True, skip_group_check=True)
                        first = False
                mm.then_inc(cum_done, 1)

            def nothing(i):
                pass

            run(pe, dict(mean2=mean2, var2=var2, w1=w1, w2=w2, mean3=mean3, gate_up=gate_up, var3=var3, down=down,
                         centre2=nothing, scale2=nothing, shift2=nothing, mask=nothing,
                         rstd3=nothing, logits=logits, turn_rows=turn_rows, turn_sums=turn_sums,
                         counts=counts))

        @block.scalar
        def _(act):
            def mean2(i):
                act.wait_ge(h_in, count(i, 16, 16))
                if not at_start(i):
                    act.wait_ge(hx_ready, count(i, DT, 0))
                for m in range(DT):
                    nc.scalar.activation(hb[:, m, :], hb_in[:, m, :], ACT.Identity,
                                         bias=vecs[:, 2, m:m + 1]).then_inc(hb_ready, 1)

            def centre2(i):
                for m in range(DT):
                    act.wait_ge(xc2_ready, count(i, DT, m + 1))
                    nc.scalar.activation(sq2[:, m, :], xc2[:, m, :], ACT.Square).then_inc(sq2_ready, 1)

            def var2(i):
                act.wait_ge(var2_done, count(i, 1, 1))
                if type(i) is int and i < 2:
                    exp_ln_tables(nc, act)
                nc.scalar.activation(ln2[:, :], pA[1][:, :], ACT.Ln, bias=EPS).then_inc(rs2_step, 1)
                act.wait_ge(rs2_step, count(i, 2, 1))
                if not at_start(i):
                    act.wait_ge(tn2_ready, count(i, DT, 0))
                nc.scalar.activation(rs2[:, :], ln2[:, :], ACT.Exp, scale=-0.5).then_inc(rs2_step, 1)

            def shift2(i):
                for m in range(DT):
                    act.wait_ge(tn2_ready, count(i, DT, m + 1))
                    if not at_start(i):
                        act.wait_ge(w1_done, count(i, FT, 0))
                    nc.scalar.activation(n2h[:, m, :], tn2[:, m, :], ACT.Identity,
                                         bias=vecs[:, 1, m:m + 1]).then_inc(n2h_ready, 1)

            def w1(i, before, js):
                for j in js:
                    act.wait_ge(w1_done, count(i, FT, j + 1))
                    if j >= 4 or not at_start(i):
                        act.wait_ge(gl_odd if j % 2 else gl_even, count(i, FT // 2, j // 2 - 1))
                    nc.scalar.activation(gz[:, j % 4, :], pW[j % 2][:, :], ACT.Gelu, scale=1 / W1_SCALE,
                                         bias=b1m[:, j:j + 1]).then_inc(gz_ready, 1)

            def mean3(i, before):
                for m in range(DT):
                    act.wait_ge(xc3_ready, count(i, DT, m + 1))
                    nc.scalar.activation(sq3[:, m, :], xc3[:, m, :], ACT.Square).then_inc(sq3_ready, 1)

            def gate_up(i, after, js):
                for j in js:
                    g = pW[0] if j % 2 == 0 else pA[0]
                    act.wait_ge(gu_done, count(i, 2 * ST, 2 * j + 1))
                    if j >= 2 or not at_start(i):
                        act.wait_ge(az_ready, count(i, ST, j - 1))
                    nc.scalar.activation(sz[:, j % 2, :], g[:, :], ACT.Silu, scale=1 / SH_SCALE).then_inc(sz_ready, 1)

            def rstd3(i):
                exp_ln_tables(nc, act)
                act.wait_ge(var3_done, count(i, 1, 1))
                nc.scalar.activation(ln3[:, :], pL[:, :], ACT.Ln, bias=EPS).then_inc(rs3_step, 1)
                act.wait_ge(rs3_step, count(i, 2, 1))
                if not at_start(i):
                    act.wait_ge(xn_ready, count(i, DT, 0))
                nc.scalar.activation(rs3[:, :], ln3[:, :], ACT.Exp, scale=-0.5).then_inc(rs3_step, 1)

            def logits(i):
                act.wait_ge(lg_done, count(i, 1, 1))
                if not at_start(i):
                    act.wait_ge(routed, count(i, 1, 0))
                nc.scalar.activation(lg[:, :, :], pL[:, 0:CH * (EXPERTS + 1)].rearrange("p (c e) -> p c e", c=CH),
                                     ACT.Copy, scale=1 / GATE_SCALE).then_inc(lg_ready, 1)
                act.wait_ge(route, count(i, ROUTE_STEPS, EXP1_AFTER))
                nc.scalar.activation(few[1][:, :, :], few[0][:, :, :], ACT.Exp).then_inc(route_exp, 1)

            def turn_rows(i, before):
                for half in range(2):
                    act.wait_ge(xt_done, count(i, 2, half + 1))
                    if not at_start(i):
                        act.wait_ge(xt_stored, count(i, 32, 0))
                    nc.scalar.activation(xt[:, 2 * half:2 * half + 2, :],
                                         pA[half][:, :].bitcast(F16).rearrange("p (c n) -> p c n", c=2),
                                         ACT.Copy).then_inc(xt_ready, 1)

            def turn_sums(i):
                for half in range(2):
                    act.wait_ge(ht_done, count(i, 2, half + 1))
                    if not at_start(i):
                        act.wait_ge(ob_ready, count(i, CH, 0))
                    nc.scalar.activation(ht[:, 2 * half:2 * half + 2, :],
                                         pA[half][:, :].rearrange("p (c n) -> p c n", c=2), ACT.Copy).then_inc(ht_ready, 1)

            def counts(i):
                exp_ln_tables(nc, act)
                act.wait_ge(route, count(i, ROUTE_STEPS, EXP2_AFTER))
                nc.scalar.activation(e9[:, :, :], ml9[:, :, :], ACT.Exp).then_inc(route_exp, 1)

            def nothing(i, *rest):
                pass

            run(act, dict(mean2=mean2, centre2=centre2, var2=var2, scale2=nothing, shift2=shift2, mask=nothing, w1=w1, w2=nothing, mean3=mean3, gate_up=gate_up, var3=nothing,
                          rstd3=rstd3, down=nothing, logits=logits, turn_rows=turn_rows, turn_sums=turn_sums,
                          counts=counts))

        @block.vector
        def _(ve):
            def centre2(i):
                ve.wait_ge(mean2_done, count(i, 1, 1))
                if not at_start(i):
                    ve.wait_ge(tn2_ready, count(i, DT, 0))
                for m in range(DT):
                    nc.vector.tensor_tensor(xc2[:, m, :], x1[:, m, :], pA[0][:, :], ALU.subtract).then_inc(xc2_ready, 1)

            def scale2(i):
                ve.wait_ge(rs2_step, count(i, 2, 2))
                ve.wait_ge(xc2_ready, count(i, DT, DT))
                if not at_start(i):
                    ve.wait_ge(n2h_ready, count(i, DT, 0))
                    ve.wait_ge(n2l_ready, count(i, DT, 0))
                for m in range(DT):
                    nc.vector.scalar_tensor_tensor(tn2[:, m, :], xc2[:, m, :], vecs[:, 0, m:m + 1], rs2[:, :],
                                                   ALU.mult, ALU.mult).then_inc(tn2_ready, 1)

            def shift2(i):
                for m in range(DT):
                    ve.wait_ge(tn2_ready, count(i, DT, m + 1))
                    ve.wait_ge(n2h_ready, count(i, DT, m + 1))
                    nc.vector.scalar_tensor_tensor(n2l[:, m, :], tn2[:, m, :], vecs[:, 1, m:m + 1], n2h[:, m, :],
                                                   ALU.add, ALU.subtract).then_inc(n2l_ready, 1)

            def w1(i, before, js):
                if js[0] == 0 and not at_start(i):
                    ve.wait_ge(w2_done, count(i, 1, 0))
                for j in js:
                    ve.wait_ge(gz_ready, count(i, FT, j + 1))
                    nc.vector.tensor_copy(gh[:, j, :], gz[:, j % 4, :]).then_inc(gh_ready, 1)
                    if j % 2 == 1:
                        ve.wait_ge(gh_ready, count(i, FT, j + 1))
                        nc.vector.tensor_tensor(gl[:, j, :], gz[:, j % 4, :], gh[:, j, :], ALU.subtract).then_inc(gl_odd, 1)
                    if before:
                        routing(i - 1, EXP1_AFTER + 2 * j, EXP1_AFTER + 2 * j + 2)

            def w2(i, js):
                if js[-1] < FT - 1:
                    return
                ve.wait_ge(w2_done, count(i, 1, 1))
                ve.wait_ge(hx_ready, count(i, DT, DT))
                if not at_start(i):
                    ve.wait_ge(ht_done, count(i, 2, 0))
                for m in range(DT):
                    nc.vector.scalar_tensor_tensor(hp[:, m, :], pY[m][:, :], 1 / W2_SCALE, hx[:, m, :],
                                                   ALU.mult, ALU.add).then_inc(hp_ready, 1)

            def mean3(i, before):
                ve.wait_ge(mean3_done, count(i, 1, 1))
                ve.wait_ge(hp_ready, count(i, DT, DT))
                for m in range(DT):
                    nc.vector.tensor_tensor(xc3[:, m, :], hp[:, m, :], pL[:, :], ALU.subtract).then_inc(xc3_ready, 1)

            def gate_up(i, after, js):
                for j in js:
                    u = pW[1] if j % 2 == 0 else pA[1]
                    ve.wait_ge(gu_done, count(i, 2 * ST, 2 * j + 2))
                    ve.wait_ge(sz_ready, count(i, ST, j + 1))
                    if j >= 2 or not at_start(i):
                        ve.wait_ge(al_ready, count(i, ST, j - 1))
                    nc.vector.scalar_tensor_tensor(az[:, j % 2, :], u[:, :], 1 / SH_SCALE, sz[:, j % 2, :],
                                                   ALU.mult, ALU.mult).then_inc(az_ready, 1)
                    ve.wait_ge(az_ready, count(i, ST, j + 1))
                    if not at_start(i):
                        ve.wait_ge(down_done, count(i, 1, 0))
                    nc.vector.tensor_copy(ah[:, j, :], az[:, j % 2, :]).then_inc(ah_ready, 1)
                    if j < ST - 1:
                        routing(i, ROUTE_CUTS[j], ROUTE_CUTS[j + 1])

            def rstd3(i):
                ve.wait_ge(rs3_step, count(i, 2, 2))
                ve.wait_ge(xc3_ready, count(i, DT, DT))
                if not at_start(i):
                    ve.wait_ge(xnl_ready, count(i, DT, 0))
                    ve.wait_ge(xt_done, count(i, 2, 0))
                    ve.wait_ge(gu_done, count(i, 2 * ST, 0))
                for m in range(DT):
                    nc.vector.tensor_tensor(xn[:, m, :], xc3[:, m, :], rs3[:, :], ALU.mult).then_inc(xn_ready, 1)
                for m in range(DT):
                    ve.wait_ge(xn_ready, count(i, DT, m + 1))
                    nc.vector.tensor_copy(xnh[:, m, :], xn[:, m, :]).then_inc(xnh_ready, 1)

            def down(i):
                ve.wait_ge(routed, count(i, 1, 1))
                ve.wait_ge(ht_ready, count(i, 2, 2))
                if not at_start(i):
                    ve.wait_ge(ob_stored, count(i, 16, 0))
                ve.wait_ge(down_done, count(i, 1, 1))
                for c in range(CH):
                    nc.vector.scalar_tensor_tensor(ob[:, c, :], pY[c % 2][:, c // 2 * D:(c // 2 + 1) * D], w8[:, c:c + 1], ht[:, c, :],
                                                   ALU.mult, ALU.add).then_inc(ob_ready, 1)

            def flat(t):
                return t[:, :, :].rearrange("p c e -> p (c e)")

            def routing(i, lo, hi):
                E = EXPERTS
                state = [0]

                def link(make):
                    state[0] += 1
                    if lo < state[0] <= hi:
                        make().then_inc(route, 1)
                        ve.wait_ge(route, count(i, ROUTE_STEPS, state[0]))

                def wait(sem_, per, k):
                    if lo <= state[0] < hi:
                        ve.wait_ge(sem_, count(i, per, k))

                V = nc.vector
                mine = lg[:, :, 0:E].unsqueeze(3).broadcast_to([P, CH, E, E])
                other = lg[:, :, 0:E].unsqueeze(2).broadcast_to([P, CH, E, E])

                def cube(t):
                    return t[:, :, :].rearrange("p (c e) f -> p c e f", c=CH)

                def over_mine(t):
                    return t[:, :, :].unsqueeze(2).broadcast_to([P, CH, E, E])

                def per_chunk(t):
                    return t[:, :].unsqueeze(2).broadcast_to([P, CH, E])

                before, scr, near, a, b = pair
                lead, ex, cprev, su, mu, mf, t1, t2, gd = few
                mx, z, zq, s1, r1_, zd = one
                link(lambda: V.tensor_reduce(mx[:, :], lg[:, :, 0:E], AX.X, ALU.max))
                link(lambda: V.tensor_tensor(lead[:, :, :], lg[:, :, 0:E], per_chunk(mx), ALU.subtract))
                link(lambda: V.tensor_tensor(cube(scr), other, mine, ALU.is_equal))
                link(lambda: V.tensor_tensor(cube(scr), cube(scr),
                                             earlier[:, :, :].unsqueeze(1).broadcast_to([P, CH, E, E]), ALU.mult))
                link(lambda: V.tensor_tensor(cube(before), other, mine, ALU.is_gt))
                link(lambda: V.tensor_tensor(before[:, :, :], before[:, :, :], scr[:, :, :], ALU.add))
                link(lambda: V.tensor_reduce(flat(rank), before[:, :, :], AX.X, ALU.add))
                link(lambda: V.scalar_tensor_tensor(mu[:, :, :], lg[:, :, 0:E], -1.0, lg[:, :, 0:E], ALU.mult, ALU.max))
                link(lambda: V.tensor_tensor(cube(a), over_mine(mu),
                                             mu[:, :, :].unsqueeze(3).broadcast_to([P, CH, E, E]), ALU.max))
                link(lambda: V.tensor_tensor(cube(b), mine, other, ALU.subtract))
                link(lambda: V.scalar_tensor_tensor(near[:, :, :], a[:, :, :], 0.2, b[:, :, :], ALU.mult, ALU.is_ge))
                link(lambda: V.scalar_tensor_tensor(near[:, :, :], before[:, :, :], 0.5, near[:, :, :],
                                                    ALU.is_lt, ALU.mult))
                wait(route_exp, 2, 1)
                link(lambda: V.tensor_tensor(cube(a), cube(near), over_mine(ex), ALU.mult))
                link(lambda: V.tensor_reduce(flat(su), a[:, :, :], AX.X, ALU.add))
                link(lambda: V.tensor_scalar(su[:, :, :], su[:, :, :], 1e-37, None, ALU.max))
                link(lambda: V.reciprocal(t1[:, :, :], su[:, :, :]))
                link(lambda: V.tensor_tensor(mu[:, :, :], ex[:, :, :], t1[:, :, :], ALU.mult))
                link(lambda: V.tensor_tensor(cube(b), cube(before), over_mine(ex), ALU.mult))
                link(lambda: V.tensor_reduce(flat(cprev), b[:, :, :], AX.X, ALU.add))
                link(lambda: V.tensor_reduce(z[:, :], ex[:, :, :], AX.X, ALU.add))
                link(lambda: V.tensor_scalar(zq[:, :], z[:, :], 0.75, None, ALU.mult))
                link(lambda: V.tensor_tensor(t2[:, :, :], cprev[:, :, :], per_chunk(zq), ALU.is_lt))
                link(lambda: V.scalar_tensor_tensor(t2[:, :, :], rank[:, :, :], TOP - 0.5, t2[:, :, :],
                                                    ALU.is_lt, ALU.mult))
                link(lambda: V.tensor_tensor(rw[:, :, :], mu[:, :, :], t2[:, :, :], ALU.mult))
                link(lambda: V.tensor_reduce(s1[:, :], rw[:, :, :], AX.X, ALU.add))
                link(lambda: V.reciprocal(r1_[:, :], s1[:, :]))
                link(lambda: V.tensor_tensor(rw[:, :, :], rw[:, :, :], per_chunk(r1_), ALU.mult))
                link(lambda: V.tensor_scalar(m0[:, :, :], rw[:, :, :], 0.0, None, ALU.is_gt))
                assert state[0] == MASK_AFTER
                if lo < MASK_AFTER <= hi:
                    V.tensor_copy(m16[:, :, :], m0[:, :, :]).then_inc(mask_ready, 1)
                wait(cum_done, 1, 1)
                link(lambda: V.tensor_tensor(t1[:, :, :], pA[1][:, 0:CH * E].rearrange("p (c e) -> p c e", c=CH),
                                             carry[:, :].unsqueeze(1).broadcast_to([P, CH, E]), ALU.add))
                link(lambda: V.tensor_tensor(carry[:, :], carry[:, :], pA[1][:, CH * E:(CH + 1) * E], ALU.add))
                if lo < state[0] <= hi:
                    V.scalar_tensor_tensor(mf[:, :, :], t1[:, :, :], SLOTS + 0.5, m0[:, :, :],
                                           ALU.is_lt, ALU.mult).then_inc(cum_read, 1)
                    ve.wait_ge(cum_read, count(i, 1, 1))
                link(lambda: V.tensor_scalar(t2[:, :, :], mf[:, :, :], 1.0, 1e30, ALU.subtract, ALU.mult))
                link(lambda: V.tensor_tensor(ml9[:, :, 0:E], lg[:, :, 0:E], mf[:, :, :], ALU.mult))
                link(lambda: V.tensor_tensor(ml9[:, :, 0:E], ml9[:, :, 0:E], t2[:, :, :], ALU.add))
                link(lambda: V.tensor_copy(ml9[:, :, E], lg[:, :, E]))
                link(lambda: V.tensor_reduce(mx[:, :], ml9[:, :, :], AX.X, ALU.max))
                link(lambda: V.tensor_tensor(ml9[:, :, :], ml9[:, :, :], mx[:, :].unsqueeze(2).broadcast_to([P, CH, E + 1]),
                                             ALU.subtract))
                assert state[0] == EXP2_AFTER
                link(lambda: V.tensor_tensor(t1[:, :, :], t1[:, :, :],
                                             first_slot[:, :].unsqueeze(1).broadcast_to([P, CH, E]), ALU.add))
                link(lambda: V.tensor_tensor(t1[:, :, :], t1[:, :, :], mf[:, :, :], ALU.mult))
                wait(route_exp, 2, 2)
                link(lambda: V.tensor_reduce(zd[:, :], e9[:, :, 0:E], AX.X, ALU.add))
                link(lambda: V.tensor_tensor(z[:, :], zd[:, :], e9[:, :, E], ALU.add))
                link(lambda: V.reciprocal(zq[:, :], z[:, :]))
                link(lambda: V.scalar_tensor_tensor(w8[:, :], e9[:, :, E], 1 / SHD_SCALE, zq[:, :], ALU.mult, ALU.mult))
                link(lambda: V.tensor_tensor(s1[:, :], zd[:, :], zq[:, :], ALU.mult))
                link(lambda: V.tensor_tensor(gd[:, :, :], rw[:, :, :], per_chunk(s1), ALU.mult))
                link(lambda: V.tensor_tensor(gd[:, :, :], gd[:, :, :], mf[:, :, :], ALU.mult))
                by_rank = a[:, 0:CH * TOP, :].rearrange("p (c k) e -> p c k e", c=CH)
                picked = b[:, 0:CH * TOP, :].rearrange("p (c k) e -> p c k e", c=CH)

                def over_ranks(t):
                    return t[:, :, :].unsqueeze(2).broadcast_to([P, CH, TOP, E])

                link(lambda: V.tensor_tensor(by_rank, over_ranks(rank),
                                             rank_no[:, :, :].unsqueeze(1).broadcast_to([P, CH, TOP, E]), ALU.is_equal))
                link(lambda: V.tensor_tensor(picked, by_rank, over_ranks(t1), ALU.mult))
                link(lambda: V.tensor_reduce(flat(slot_f), b[:, 0:CH * TOP, :], AX.X, ALU.add))
                link(lambda: V.tensor_tensor(picked, by_rank, over_ranks(gd), ALU.mult))
                if lo <= state[0] < hi and not at_start(i):
                    ve.wait_ge(list_sent, count(i, 16 * CH * TOP, 0))
                link(lambda: V.tensor_reduce(w_f[:, :, :].rearrange("p c k -> p (c k)"), b[:, 0:CH * TOP, :], AX.X, ALU.add))
                link(lambda: V.tensor_copy(entry[:, :, :, 1].bitcast(F32), w_f[:, :, :]))
                link(lambda: V.tensor_copy(entry[:, :, :, 0], tid[:, :].unsqueeze(2).broadcast_to([P, CH, TOP])))
                link(lambda: V.tensor_scalar(tid[:, :], tid[:, :], float(T), None, ALU.add))
                link(lambda: V.tensor_scalar(w_f[:, :, :], slot_f[:, :, :], 0.0, FAR, ALU.is_equal, ALU.mult))
                if hi == ROUTE_STEPS:
                    V.scalar_tensor_tensor(slot_u[:, :, :], slot_f[:, :, :], -1.0, w_f[:, :, :],
                                           ALU.add, ALU.add).then_inc(routed, 1)
                assert state[0] == ROUTE_STEPS, state

            def logits(i):
                ve.wait_ge(lg_ready, count(i, 1, 1))
                routing(i, 0, EXP1_AFTER)

            def mask(i):
                routing(i, EXP1_AFTER + (0 if type(i) is int and i == SEQS - 1 else 2 * FT), MASK_AFTER)

            def counts(i):
                routing(i, MASK_AFTER, ROUTE_CUTS[0])

            def nothing(i, *rest):
                pass

            run(ve, dict(mean2=nothing, centre2=centre2, var2=nothing, scale2=scale2, shift2=shift2, mask=mask, w1=w1, w2=w2, mean3=mean3, gate_up=gate_up, var3=nothing,
                         rstd3=rstd3, down=down, logits=logits, turn_rows=nothing, turn_sums=nothing, counts=counts))

        @block.gpsimd
        def _(gp):
            def rows(i):
                gp.wait_ge(x0_in, count(i, 16, 16))
                gp.wait_ge(at_in, count(i, 16, 16))
                if not at_start(i):
                    gp.wait_ge(xc2_ready, count(i, DT, 0))
                    gp.wait_ge(mean2_done, count(i, 1, 0))
                    gp.wait_ge(hx_ready, count(i, DT, 0))
                for m in range(DT):
                    nc.gpsimd.tensor_tensor(x1[:, m, :], x0b[:, m, :], atb[:, m, :], ALU.add).then_inc(x1_ready, 1)

            def w1(i, before, js):
                for j in (j for j in js if j % 2 == 0):
                    gp.wait_ge(gh_ready, count(i, FT, j + 1))
                    nc.gpsimd.tensor_tensor(gl[:, j, :], gz[:, j % 4, :], gh[:, j, :], ALU.subtract).then_inc(gl_even, 1)
                    if before and not (type(i) is int and i < 2):
                        send(i - 2, *((1, (2,)), (1, (3,)), (2, (0,)), (2, (1,)))[j // 2])

            def sums(i):
                gp.wait_ge(hb_ready, count(i, DT, DT))
                gp.wait_ge(x1_ready, count(i, DT, DT))
                if not at_start(i):
                    gp.wait_ge(hp_ready, count(i, DT, 0))
                for m in range(DT):
                    nc.gpsimd.tensor_tensor(hx[:, m, :], hb[:, m, :], x1[:, m, :], ALU.add).then_inc(hx_ready, 1)

            def gate_up(i, after, js):
                for j in js:
                    gp.wait_ge(ah_ready, count(i, ST, j + 1))
                    nc.gpsimd.tensor_tensor(al[:, j, :], az[:, j % 2, :], ah[:, j, :], ALU.subtract).then_inc(al_ready, 1)

            def rstd3(i):
                for m in range(DT):
                    gp.wait_ge(xnh_ready, count(i, DT, m + 1))
                    nc.gpsimd.tensor_tensor(xnl[:, m, :], xn[:, m, :], xnh[:, m, :], ALU.subtract).then_inc(xnl_ready, 1)
                if not (type(i) is int and i >= SEQS - 2):
                    rows(i + 2)

            def send(i, c, ranks):
                if c == ranks[0] == 0:
                    gp.wait_ge(lists_cleared, 16)
                    gp.wait_ge(routed, count(i, 1, 1))
                    gp.sem_inc(passed, 1)
                for k in ranks:
                    nc.gpsimd.indirect_dma_start(
                        io["list_dram"], bass.IndirectOffsetOnAxis(slot_u[:, c, k:k + 1], 0), entry[:, c, k, :],
                        None, bounds_check=EXPERTS * SLOTS - 1, oob_is_err=False).then_inc(list_sent, 16)

            def nothing(i, *rest):
                pass

            def mean3(i, before):
                if type(i) is int and i == SEQS - 1:
                    return
                sums(i + 1)

            def var2(i):
                if at_start(i):
                    sums(0)

            def counts(i):
                pass

            def down(i):
                send(i, 0, range(TOP))
                send(i, 1, (0, 1))
                if type(i) is int and i >= SEQS - 2:
                    send(i, 1, (2, 3))
                    send(i, 2, range(TOP))
                    send(i, 3, range(TOP))

            def w2(i, js):
                if js[0] > 0 and not (type(i) is int and i < 2):
                    send(i - 2, 2, (2, 3))
                    send(i - 2, 3, range(TOP))

            def mean2(i):
                if type(i) is int and i < 2:
                    rows(i)

            run(gp, dict(mean2=mean2, centre2=nothing, var2=var2, scale2=nothing, shift2=nothing, mask=nothing, w1=w1, w2=w2, mean3=mean3, gate_up=gate_up, var3=nothing,
                         rstd3=rstd3, down=down, logits=nothing, turn_rows=nothing, turn_sums=nothing, counts=counts))
            gp.wait_ge(list_sent, 16 * CH * TOP * SEQS)


ROUTE_STEPS = 54
EXP1_AFTER = 2
MASK_AFTER = 28
EXP2_AFTER = 36
ROUTE_CUTS = (43, 47, 51, ROUTE_STEPS)
DYN_SCALE = 8.0
WCOLS = 2 * DT * P + D
GROUPS = TILES // 2
PG = 2 * GROUPS
PT = 2 * TILES
RING = 10


def routed_phase(nc, io):
    with ExitStack() as ctx:
        def sb(name, shape, dt=F32):
            return ctx.enter_context(nc.sbuf_tensor(name, [P, *shape], dt))

        def sem(name):
            return ctx.enter_context(nc.semaphore(name))

        def bank(name):
            return ctx.enter_context(nc.psum_tensor(name, [P, 512], F32))

        ident = sb("ident3", [P], F16)
        wf = sb("wf", [2, WCOLS])
        wh, wl = sb("wh", [2, WCOLS], F16), sb("wl", [2, WCOLS], F16)
        gid = sb("gid", [TILES * 2, 2], U32)
        sid = sb("sid", [TILES * 2, 2], U32)
        lw = sb("lw", [TILES * 2])
        xg = sb("xg", [RING, 2 * D], F16)
        xf = sb("xf", [2, 2 * DT, 2 * P], F16)
        sz, az = sb("sz3", [2, 2 * P]), sb("az3", [2, 2 * P])
        ah, al = sb("ah3", [2, 2 * P], F16), sb("al3", [2, 2 * P], F16)
        yb = sb("yb", [4, D])
        pT = [bank("pT3a"), bank("pT3b")]
        pG = [bank("pG3a"), bank("pG3b")]
        pD = [bank("pD3a"), bank("pD3b")]

        made, gid_in, sid_in, lw_ready = sem("made3"), sem("gid_in"), sem("sid_in"), sem("lw_ready")
        w_in = [sem("w_in0"), sem("w_in1")]
        wh_ready, wl_ready = sem("wh_ready"), sem("wl_ready")
        gathered = [sem(f"gathered{n}") for n in range(RING)]
        t_done, xf_ready, gu_done = sem("t_done"), sem("xf_ready"), sem("gu_done3")
        sz_ready, az_ready, ah_ready, al_ready = sem("sz_ready3"), sem("az_ready3"), sem("ah_ready3"), sem("al_ready3")
        d_done, y_ready = sem("d_done"), sem("y_ready")
        added = [sem(f"added{n}") for n in range(4)]
        passed = sem("passed")
        PAIRS = EXPERTS // 2
        lists = io["list_dram"].rearrange("(e two p n) w -> e p two n w", two=2, p=P, n=TILES)

        def at_start(i):
            return type(i) is int and i == 0

        def run(engine, body):
            body(0, True)
            with engine.Fori(1, PAIRS - 1) as i:
                body(i, True)
            body(PAIRS - 1, False)

        block = ctx.enter_context(nc.Block())

        @block.sync
        def _(sp):
            def gather_list(i):
                if not at_start(i):
                    for n in range(RING):
                        sp.wait_ge(gathered[n], count(i, 32, 0))
                sp.dma_start(gid[:, :, :].rearrange("p (two n) w -> p two n w", two=2), lists[i]).then_inc(gid_in, 16)

            def scatter_list(i):
                if not at_start(i):
                    for n in range(4):
                        sp.wait_ge(added[n], count(i, 80, 0))
                    sp.wait_ge(lw_ready, count(i, 1, 0))
                sp.dma_start(sid[:, :, :].rearrange("p (two n) w -> p two n w", two=2), lists[i]).then_inc(sid_in, 16)

            def weights(i, s):
                if not at_start(i):
                    sp.wait_ge(wl_ready, count(i, 2, s - 1))
                pairs = io["dyn_w"].rearrange("(e two) p n -> e two p n", two=2)
                sp.dma_start(wf[:, s, :], pairs[i, s]).then_inc(w_in[s], 16)

            def body(i, more):
                if more:
                    weights(i + 1, 0)
                    gather_list(i + 1)
                    weights(i + 1, 1)
                    scatter_list(i + 1)

            gather_list(0)
            weights(0, 0)
            weights(0, 1)
            scatter_list(0)
            run(sp, body)

        @block.tensor
        def _(pe):
            def three(out, wh_, wl_, mh, ml, first, last):
                pe.matmul(out, wh_, mh, start=first, stop=False, skip_group_check=True)
                pe.matmul(out, wl_, mh, start=False, stop=False, skip_group_check=True)
                return pe.matmul(out, wh_, ml, start=False, stop=last, skip_group_check=True)

            def turn(i, g):
                if g >= 2 or not at_start(i):
                    pe.wait_ge(xf_ready, count(i, PG, g - 1))
                out = pT[g % 2][:, :].bitcast(F16)
                for b in range(2):
                    slot = (2 * g + b) % RING
                    pe.wait_ge(gathered[slot], count(i, 32, 16 * ((2 * g + b) // RING + 1)))
                    for w in range(2 * DT):
                        at = w * 2 * P + b * P
                        mm = pe.transpose(out[:, at:at + P], xg[:, slot, w * P:(w + 1) * P], ident[:, :])
                mm.then_inc(t_done, 1)

            def gate_up(i, g):
                e = g // GROUPS
                if g % GROUPS == 0:
                    pe.wait_ge(wh_ready, count(i, 2, e + 1))
                    pe.wait_ge(wl_ready, count(i, 2, e + 1))
                pe.wait_ge(xf_ready, count(i, PG, g + 1))
                if g >= 2 or not at_start(i):
                    pe.wait_ge(az_ready, count(i, PG, g - 1))
                for half in range(2):
                    for t in range(DT):
                        at = (half * DT + t) * P
                        mm = three(pG[g % 2][:, half * 2 * P:(half + 1) * 2 * P], wh[:, e, at:at + P], wl[:, e, at:at + P],
                                   xf[:, g % 2, t, :], xf[:, g % 2, DT + t, :], half == 0 and t == 0, t == DT - 1)
                mm.then_inc(gu_done, 1)

            def down(i, g):
                e = g // GROUPS
                pe.wait_ge(ah_ready, count(i, PG, g + 1))
                pe.wait_ge(al_ready, count(i, PG, g + 1))
                if g >= 2 or not at_start(i):
                    pe.wait_ge(y_ready, count(i, PT, 2 * (g - 1)))
                cols = slice(2 * DT * P, WCOLS)
                for b in range(2):
                    toks = slice(b * P, (b + 1) * P)
                    mm = three(pD[g % 2][:, b * D:(b + 1) * D], ah[:, g % 2, toks], al[:, g % 2, toks],
                               wh[:, e, cols], wl[:, e, cols], b == 0, True)
                mm.then_inc(d_done, 1)

            def body(i, more):
                turn(i, 0)
                for g in range(PG):
                    if g + 1 < PG:
                        turn(i, g + 1)
                    gate_up(i, g)
                    if g > 0:
                        down(i, g - 1)
                down(i, PG - 1)

            pe.wait_ge(made, 2)
            run(pe, body)

        @block.scalar
        def _(act):
            def split(i, e):
                act.wait_ge(w_in[e], count(i, 16, 16))
                if not at_start(i):
                    act.wait_ge(d_done, count(i, PG, (e - 1) * GROUPS))
                nc.scalar.activation(wh[:, e, :], wf[:, e, :], ACT.Copy, scale=DYN_SCALE).then_inc(wh_ready, 1)

            def silu(i, g):
                act.wait_ge(gu_done, count(i, PG, g + 1))
                if g >= 2 or not at_start(i):
                    act.wait_ge(az_ready, count(i, PG, g - 1))
                nc.scalar.activation(sz[:, g % 2, :], pG[g % 2][:, 0:2 * P], ACT.Silu,
                                     scale=1 / DYN_SCALE).then_inc(sz_ready, 1)

            def weigh(i, g):
                act.wait_ge(d_done, count(i, PG, g + 1))
                if g == 0:
                    act.wait_ge(lw_ready, count(i, 1, 1))
                for b in range(2):
                    n = 2 * g + b
                    if n >= 4 or not at_start(i):
                        act.wait_ge(added[n % 4], count(i, 80, 16 * (n // 4)))
                    nc.scalar.activation(yb[:, n % 4, :], pD[g % 2][:, b * D:(b + 1) * D], ACT.Copy,
                                         scale=lw[:, n:n + 1]).then_inc(y_ready, 1)

            def body(i, more):
                for g in range(PG):
                    if g == 1:
                        split(i, 1)
                    if g == GROUPS + 1 and more:
                        split(i + 1, 0)
                    silu(i, g)
                    if g > 0:
                        weigh(i, g - 1)
                weigh(i, PG - 1)

            split(0, 0)
            run(act, body)

        @block.vector
        def _(ve):
            def split(i, e):
                ve.wait_ge(wh_ready, count(i, 2, e + 1))
                nc.vector.scalar_tensor_tensor(wl[:, e, :], wf[:, e, :], DYN_SCALE, wh[:, e, :],
                                               ALU.mult, ALU.subtract).then_inc(wl_ready, 1)

            def weights_of_list(i):
                ve.wait_ge(sid_in, count(i, 16, 16))
                if not at_start(i):
                    ve.wait_ge(y_ready, count(i, PT, 0))
                nc.vector.tensor_scalar(lw[:, :], sid[:, :, 1].bitcast(F32), 1 / DYN_SCALE, None,
                                        ALU.mult).then_inc(lw_ready, 1)

            def features(i, g):
                ve.wait_ge(t_done, count(i, PG, g + 1))
                if g >= 2 or not at_start(i):
                    ve.wait_ge(gu_done, count(i, PG, g - 1))
                nc.vector.tensor_copy(xf[:, g % 2, :, :], pT[g % 2][:, :].bitcast(F16).rearrange(
                    "p (w n) -> p w n", n=2 * P)).then_inc(xf_ready, 1)

            def hidden(i, g):
                s = g % 2
                ve.wait_ge(sz_ready, count(i, PG, g + 1))
                nc.vector.scalar_tensor_tensor(az[:, s, :], pG[s][:, 2 * P:], 1 / DYN_SCALE, sz[:, s, :],
                                               ALU.mult, ALU.mult).then_inc(az_ready, 1)
                ve.wait_ge(az_ready, count(i, PG, g + 1))
                if g >= 2 or not at_start(i):
                    ve.wait_ge(d_done, count(i, PG, g - 1))
                nc.vector.tensor_copy(ah[:, s, :], az[:, s, :]).then_inc(ah_ready, 1)
                ve.wait_ge(ah_ready, count(i, PG, g + 1))
                nc.vector.tensor_tensor(al[:, s, :], az[:, s, :], ah[:, s, :], ALU.subtract).then_inc(al_ready, 1)

            def body(i, more):
                features(i, 0)
                weights_of_list(i)
                for g in range(PG):
                    if g + 1 < PG:
                        features(i, g + 1)
                    if g == 1:
                        split(i, 1)
                    if g == GROUPS + 1 and more:
                        split(i + 1, 0)
                    hidden(i, g)

            split(0, 0)
            run(ve, body)

        @block.gpsimd
        def _(gp):
            identity(nc, gp, ident[:, :], made, 0)

            def gather(i, n):
                if n == 0:
                    gp.wait_ge(gid_in, count(i, 16, 16))
                if n >= RING or not at_start(i):
                    gp.wait_ge(t_done, count(i, PG, (n - RING) // 2 + 1))
                gp.sem_inc(passed, 1)
                nc.gpsimd.indirect_dma_start(xg[:, n % RING, :], None, io["xrow_dram"],
                                             bass.IndirectOffsetOnAxis(gid[:, n, 0:1], 0)).then_inc(gathered[n % RING], 16)

            def add(i, g):
                for b in range(2):
                    n = 2 * g + b
                    gp.wait_ge(y_ready, count(i, PT, n + 1))
                    if n % TILES == 0 and (n > 0 or not at_start(i)):
                        for s in range(4):
                            done = len([m for m in range(n) if m % 4 == s])
                            gp.wait_ge(added[s], count(i, 80, 16 * done))
                    gp.sem_inc(passed, 1)
                    nc.gpsimd.indirect_dma_start(io["out"], bass.IndirectOffsetOnAxis(sid[:, n, 0:1], 0),
                                                 yb[:, n % 4, :], None, compute_op=ALU.add,
                                                 ).then_inc(added[n % 4], 16)

            def body(i, more):
                for g in range(PG):
                    for b in range(2):
                        n = 2 * g + b + RING
                        if n < PT:
                            gather(i, n)
                        elif more:
                            gather(i + 1, n - PT)
                    if g > 0:
                        add(i, g - 1)
                add(i, PG - 1)

            for n in range(RING):
                gather(0, n)
            run(gp, body)
            for n in range(4):
                gp.wait_ge(added[n], 80 * PAIRS)


def build(nc, io):
    attention_phase(nc, io)
    mlp_phase(nc, io)
    routed_phase(nc, io)




def kernel(**inputs):
    import numpy as np
    import concourse.bacc as bacc
    from concourse.bass_utils import run_bass_kernel_spmd

    def plain(a):
        return np.ascontiguousarray(a)

    def columns(v):
        return plain(np.reshape(v, (-1, P)).T)

    def per_partition(w):
        e, k, n = w.shape
        return np.reshape(np.transpose(np.reshape(w, (e, k // P, P, n)), (0, 2, 1, 3)), (e, P, -1))

    a = {k: np.asarray(v) for k, v in inputs.items()}
    x = np.transpose(np.reshape(a["x"], (2 * SEQS, HALF, DT, P, 4)), (0, 4, 3, 2, 1))
    arrays = {
        "x": plain(x).reshape(2 * SEQS, XS, P, DT * HALF),
        "wsT": plain(a["L0_tok_weighted_sum"].T),
        "wT": plain(a["L0_tok_weight"].T),
        "wqT": plain(a["L0_attn_wq"].T),
        "wkT": plain(a["L0_attn_wk"].T),
        "wv": plain(a["L0_attn_wv"]),
        "wo": plain(a["L0_attn_wo"]),
        "proj": plain(a["L0_attn_proj"]),
        "g1": columns(a["L0_attn_g1"]),
        "beta1": columns(a["L0_attn_beta1"]),
        "w1": plain(a["L0_attn_w1"]),
        "b1": columns(a["L0_attn_b1"]),
        "w2": plain(a["L0_attn_w2"]),
        "b2": columns(a["L0_attn_b2"]),
        "g2": columns(a["L0_attn_g2"]),
        "beta2": columns(a["L0_attn_beta2"]),
        "gateT": plain(a["L0_ffn_gate_w"].T),
        "shgT": plain(a["L0_ffn_sh_gate_w"][0].T),
        "shuT": plain(a["L0_ffn_sh_up_w"][0].T),
        "shdT": plain(a["L0_ffn_sh_down_w"][0].T),
        "dyn_w": plain(np.concatenate([per_partition(np.transpose(a[n], (0, 2, 1))) for n in (
            "L0_ffn_dyn_gate_w", "L0_ffn_dyn_up_w", "L0_ffn_dyn_down_w")], axis=2)),
    }
    nc = bacc.Bacc("TRN2", target_bir_lowering=False, num_devices=1)
    io, launch = {}, {}
    for name, v in arrays.items():
        launch[f"in_{name}"] = v
        io[name] = nc.dram_tensor(f"in_{name}", list(v.shape), mybir.dt.from_np(v.dtype), kind="ExternalInput").ap()
    io["out"] = nc.dram_tensor("out_rows", [TOKENS + DUMMIES, D], F32, kind="ExternalOutput").ap()
    for name in ("h_dram", "x0_dram", "at_dram"):
        io[name] = nc.dram_tensor(name, [SEQS, DT, P, T], F32, kind="Internal").ap()
    io["xrow_dram"] = nc.dram_tensor("xrow_dram", [TOKENS + DUMMIES, 2 * D], F16, kind="Internal").ap()
    io["list_dram"] = nc.dram_tensor("list_dram", [EXPERTS * SLOTS, 2], U32, kind="Internal").ap()
    build(nc, io)
    r = run_bass_kernel_spmd(nc, [launch], core_ids=[0])
    return np.reshape(r.results[0]["out_rows"][:TOKENS], (SEQS, T, D))
```
